# Optimizing a Trainium2 kernel written in Bass

```python
import numpy as np
import jax
import jax.numpy as jnp

def _softmax(x, axis=-1):
    return jax.nn.softmax(x, axis=axis)

def _gelu(x):
    return jax.nn.gelu(x, approximate=True)

def _silu(x):
    return jax.nn.silu(x)

def _sigmoid(x):
    return jax.nn.sigmoid(x)

def _layernorm(x, axis=-1, eps=1e-05):
    m = jnp.mean(x, axis=axis, keepdims=True)
    v = jnp.var(x, axis=axis, keepdims=True)
    return (x - m) / jnp.sqrt(v + eps)

def _scatter_add(tgt, idx, src, axis=0):
    return tgt.at[idx].add(src)

def _segment_sum(src, seg, n):
    return jax.ops.segment_sum(src, seg, n)
kernel_name = 'mk_seq_postln_d2_jaxref_r8_8b5253'

def setup_inputs(seed: int=0):
    np.random.seed(seed)
    _w = jnp.asarray

    def _L0_attn_setup():
        import jax, jax.numpy as jnp
        import numpy as np
        H = 256
        key = jax.random.key(seed)
        ks = jax.random.split(key, 7)
        s = 1.0 / np.sqrt(H)
        return {'input': jax.random.normal(ks[0], (2, 512, H), dtype=jnp.float32), 'Wq': jax.random.uniform(ks[1], (H, H), jnp.float32, -s, s), 'bq': jax.random.uniform(ks[2], (H,), jnp.float32, -s, s), 'Wk': jax.random.uniform(ks[3], (H, H), jnp.float32, -s, s), 'bk': jax.random.uniform(ks[4], (H,), jnp.float32, -s, s), 'Wv': jax.random.uniform(ks[5], (H, H), jnp.float32, -s, s), 'bv': jax.random.uniform(ks[6], (H,), jnp.float32, -s, s)}
    _L0_attn_in = _L0_attn_setup()

    def _L0_ffn_setup():
        import jax, jax.numpy as jnp
        import numpy as np
        HIDDEN = 256
        INTER = 1024
        B, S = (4, 128)

        def _qmatmul(x, w_int8, scale):
            y = jnp.einsum('bsh,ho->bso', x, w_int8.astype(x.dtype))
            return y * scale
        key = jax.random.key(seed)
        ks = jax.random.split(key, 7)
        x = jax.random.normal(ks[0], (B, S, HIDDEN), dtype=jnp.float32)
        w_gate = jax.random.randint(ks[1], (HIDDEN, INTER), -128, 128, dtype=jnp.int32).astype(jnp.int8)
        w_up = jax.random.randint(ks[2], (HIDDEN, INTER), -128, 128, dtype=jnp.int32).astype(jnp.int8)
        w_down = jax.random.randint(ks[3], (INTER, HIDDEN), -128, 128, dtype=jnp.int32).astype(jnp.int8)
        s_gate = jax.random.uniform(ks[4], (INTER,), dtype=jnp.float32) * 0.02 + 0.001
        s_up = jax.random.uniform(ks[5], (INTER,), dtype=jnp.float32) * 0.02 + 0.001
        s_down = jax.random.uniform(ks[6], (HIDDEN,), dtype=jnp.float32) * 0.02 + 0.001
        return {'x': x, 'w_gate': w_gate, 'w_up': w_up, 'w_down': w_down, 's_gate': s_gate, 's_up': s_up, 's_down': s_down}
    _L0_ffn_in = _L0_ffn_setup()

    def _L1_attn_setup():
        import jax, jax.numpy as jnp
        import numpy as np
        B, S, HIDDEN, H = (4, 512, 256, 16)
        HD = HIDDEN // H

        def apply_rope(x, inv_freq):
            seq_len = x.shape[1]
            t = jnp.arange(seq_len, dtype=jnp.float32)[:, None]
            angle = t * inv_freq[None, :]
            sin = jnp.sin(angle)[None, :, None, :]
            cos = jnp.cos(angle)[None, :, None, :]
            x1, x2 = (x[..., ::2], x[..., 1::2])
            return jnp.concatenate([x1 * cos - x2 * sin, x1 * sin + x2 * cos], axis=-1)
        key = jax.random.key(seed)
        ks = jax.random.split(key, 5)
        x = jax.random.normal(ks[0], (B, S, HIDDEN), dtype=jnp.float32)
        scale = 1.0 / np.sqrt(HIDDEN)
        wq = jax.random.normal(ks[1], (HIDDEN, HIDDEN), dtype=jnp.float32) * scale
        wk = jax.random.normal(ks[2], (HIDDEN, HIDDEN), dtype=jnp.float32) * scale
        wv = jax.random.normal(ks[3], (HIDDEN, HIDDEN), dtype=jnp.float32) * scale
        wo = jax.random.normal(ks[4], (HIDDEN, HIDDEN), dtype=jnp.float32) * scale
        inv_freq = (1.0 / 10000.0 ** (np.arange(0, HD, 2, dtype=np.float32) / HD)).astype(np.float32)
        inv_freq = jnp.asarray(inv_freq)
        return {'x': x, 'wq': wq, 'wk': wk, 'wv': wv, 'wo': wo, 'inv_freq': inv_freq}
    _L1_attn_in = _L1_attn_setup()

    def _L1_ffn_setup():
        import jax, jax.numpy as jnp
        import numpy as np
        H = 256
        E = 64
        I = 64
        SI = 64
        TOP_K = 8
        B, T = (2, 64)
        key = jax.random.key(seed)
        ks = jax.random.split(key, 8)
        s = 0.02
        return {'h': jax.random.normal(ks[0], (B, T, H), jnp.float32), 'gate_w': jax.random.normal(ks[1], (E, H), jnp.float32) * s, 'gu_w': jax.random.normal(ks[2], (E, 2 * I, H), jnp.float32) * s, 'dp_w': jax.random.normal(ks[3], (E, H, I), jnp.float32) * s, 'sh_gate_w': jax.random.normal(ks[4], (SI, H), jnp.float32) * s, 'sh_up_w': jax.random.normal(ks[5], (SI, H), jnp.float32) * s, 'sh_down_w': jax.random.normal(ks[6], (H, SI), jnp.float32) * s, 'sh_gate1_w': jax.random.normal(ks[7], (1, H), jnp.float32) * s}
    _L1_ffn_in = _L1_ffn_setup()
    _d = {'L0_attn_input': _L0_attn_in['input'], 'L0_attn_Wq': _L0_attn_in['Wq'], 'L0_attn_bq': _L0_attn_in['bq'], 'L0_attn_Wk': _L0_attn_in['Wk'], 'L0_attn_bk': _L0_attn_in['bk'], 'L0_attn_Wv': _L0_attn_in['Wv'], 'L0_attn_bv': _L0_attn_in['bv'], 'L0_ffn_w_gate': _L0_ffn_in['w_gate'], 'L0_ffn_w_up': _L0_ffn_in['w_up'], 'L0_ffn_w_down': _L0_ffn_in['w_down'], 'L0_ffn_s_gate': _L0_ffn_in['s_gate'], 'L0_ffn_s_up': _L0_ffn_in['s_up'], 'L0_ffn_s_down': _L0_ffn_in['s_down'], 'L1_attn_wq': _L1_attn_in['wq'], 'L1_attn_wk': _L1_attn_in['wk'], 'L1_attn_wv': _L1_attn_in['wv'], 'L1_attn_wo': _L1_attn_in['wo'], 'L1_attn_inv_freq': _L1_attn_in['inv_freq'], 'L1_ffn_gate_w': _L1_ffn_in['gate_w'], 'L1_ffn_gu_w': _L1_ffn_in['gu_w'], 'L1_ffn_dp_w': _L1_ffn_in['dp_w'], 'L1_ffn_sh_gate_w': _L1_ffn_in['sh_gate_w'], 'L1_ffn_sh_up_w': _L1_ffn_in['sh_up_w'], 'L1_ffn_sh_down_w': _L1_ffn_in['sh_down_w'], 'L1_ffn_sh_gate1_w': _L1_ffn_in['sh_gate1_w']}
    _x0 = _d['L0_attn_input']
    _d['L0_attn_input'] = jax.random.normal(jax.random.fold_in(jax.random.key(seed), 1), (2, 1024, 256), dtype=_x0.dtype)
    del _x0
    return _d

def reference(L0_attn_input, L0_attn_Wq, L0_attn_bq, L0_attn_Wk, L0_attn_bk, L0_attn_Wv, L0_attn_bv, L0_ffn_w_gate, L0_ffn_w_up, L0_ffn_w_down, L0_ffn_s_gate, L0_ffn_s_up, L0_ffn_s_down, L1_attn_wq, L1_attn_wk, L1_attn_wv, L1_attn_wo, L1_attn_inv_freq, L1_ffn_gate_w, L1_ffn_gu_w, L1_ffn_dp_w, L1_ffn_sh_gate_w, L1_ffn_sh_up_w, L1_ffn_sh_down_w, L1_ffn_sh_gate1_w):

    def _L0_attn_ref(input, Wq, bq, Wk, bk, Wv, bv):
        import jax, jax.numpy as jnp
        import numpy as np
        H = 256
        q = jnp.einsum('bsh,oh->bso', input, Wq) + bq
        k = jnp.einsum('bsh,oh->bso', input, Wk) + bk
        v = jnp.einsum('bsh,oh->bso', input, Wv) + bv
        scores = jnp.einsum('bqh,bkh->bqk', q, k)
        attn = jax.nn.softmax(scores, axis=-1)
        out = jnp.einsum('bqk,bkh->bqh', attn, v)
        return out

    def _L0_ffn_ref(x, w_gate, w_up, w_down, s_gate, s_up, s_down):
        import jax, jax.numpy as jnp
        import numpy as np
        HIDDEN = 256
        INTER = 1024
        B, S = (4, 128)

        def _qmatmul(x, w_int8, scale):
            y = jnp.einsum('bsh,ho->bso', x, w_int8.astype(x.dtype))
            return y * scale
        gate = jax.nn.silu(_qmatmul(x, w_gate, s_gate))
        up = _qmatmul(x, w_up, s_up)
        fuse = gate * up
        return _qmatmul(fuse, w_down, s_down)

    def _L1_attn_ref(x, wq, wk, wv, wo, inv_freq):
        import jax, jax.numpy as jnp
        import numpy as np
        B, S, HIDDEN, H = (4, 512, 256, 16)
        HD = HIDDEN // H

        def apply_rope(x, inv_freq):
            seq_len = x.shape[1]
            t = jnp.arange(seq_len, dtype=jnp.float32)[:, None]
            angle = t * inv_freq[None, :]
            sin = jnp.sin(angle)[None, :, None, :]
            cos = jnp.cos(angle)[None, :, None, :]
            x1, x2 = (x[..., ::2], x[..., 1::2])
            return jnp.concatenate([x1 * cos - x2 * sin, x1 * sin + x2 * cos], axis=-1)
        b, s, _ = x.shape
        q = (x @ wq.T).reshape(b, s, H, HD)
        k = (x @ wk.T).reshape(b, s, H, HD)
        v = (x @ wv.T).reshape(b, s, H, HD)
        q = apply_rope(q, inv_freq)
        k = apply_rope(k, inv_freq)
        scores = jnp.einsum('bshd,bstd->bsht', q, k) / jnp.sqrt(jnp.float32(HD))
        weights = jax.nn.softmax(scores, axis=-1)
        attn = jnp.einsum('bsht,bstd->bshd', weights, v)
        attn = attn.reshape(b, s, HIDDEN)
        return attn @ wo.T

    def _L1_ffn_ref(h, gate_w, gu_w, dp_w, sh_gate_w, sh_up_w, sh_down_w, sh_gate1_w):
        import jax, jax.numpy as jnp
        import numpy as np
        H = 256
        E = 64
        I = 64
        SI = 64
        TOP_K = 8
        B, T = (2, 64)
        Bb, Tt, Hh = h.shape
        x = h.reshape(Bb * Tt, Hh)
        N = x.shape[0]
        logits = x @ gate_w.T
        topv, topi = jax.lax.top_k(logits, TOP_K)
        rw = jax.nn.softmax(topv.astype(jnp.float32), axis=-1).astype(x.dtype)
        W = jnp.zeros((N, E), x.dtype).at[jnp.arange(N)[:, None], topi].set(rw)
        gu = jnp.einsum('nh,eih->nei', x, gu_w)
        gate, up = (gu[..., :I], gu[..., I:])
        inter = jax.nn.silu(gate) * up
        inter_w = inter * W[:, :, None]
        out = jnp.einsum('nei,ehi->nh', inter_w, dp_w)
        sh_inter = jax.nn.silu(x @ sh_gate_w.T) * (x @ sh_up_w.T)
        sh_out = sh_inter @ sh_down_w.T
        sh_g = jax.nn.sigmoid(x @ sh_gate1_w.T)
        out = out + sh_g * sh_out
        return out.reshape(Bb, Tt, Hh)
    x = L0_attn_input
    x = _layernorm(x + _L0_attn_ref(x, L0_attn_Wq, L0_attn_bq, L0_attn_Wk, L0_attn_bk, L0_attn_Wv, L0_attn_bv), axis=-1)
    x = _layernorm(x + _L0_ffn_ref(x, L0_ffn_w_gate, L0_ffn_w_up, L0_ffn_w_down, L0_ffn_s_gate, L0_ffn_s_up, L0_ffn_s_down), axis=-1)
    x = _layernorm(x + _L1_attn_ref(x, L1_attn_wq, L1_attn_wk, L1_attn_wv, L1_attn_wo, L1_attn_inv_freq), axis=-1)
    x = _layernorm(x + _L1_ffn_ref(x, L1_ffn_gate_w, L1_ffn_gu_w, L1_ffn_dp_w, L1_ffn_sh_gate_w, L1_ffn_sh_up_w, L1_ffn_sh_down_w, L1_ffn_sh_gate1_w), axis=-1)
    return x

_drawn_inputs = setup_inputs


def setup_inputs(seed=0):
    import zlib

    import numpy as np

    out = dict(_drawn_inputs(seed))
    spreads = {}
    factors = {'L0_attn_bk': 8.0,
     'L1_attn_inv_freq': 8.0,
     'L1_ffn_gate_w': 8.0,
     'L1_ffn_gu_w': 8.0,
     'L1_ffn_dp_w': 8.0,
     'L1_ffn_sh_gate_w': 8.0,
     'L1_ffn_sh_up_w': 8.0,
     'L1_ffn_sh_down_w': 8.0,
     'L1_ffn_sh_gate1_w': 8.0}
    for name, (base, spread) in spreads.items():
        noise = np.random.default_rng([zlib.crc32(name.encode()), seed]).standard_normal(out[name].shape)
        drawn = base * np.exp(spread * noise) if base else spread * noise
        out[name] = jnp.asarray(drawn.astype(out[name].dtype))
    for name, factor in factors.items():
        out[name] = (out[name] * factor).astype(out[name].dtype)
    return out
```

```python
from contextlib import ExitStack

import concourse.bass as bass
from concourse import mybir

F32 = mybir.dt.float32
FR = mybir.dt.float32r
BF16 = mybir.dt.bfloat16
I8 = mybir.dt.int8
I32 = mybir.dt.int32
ALU = mybir.AluOpType
ACT = mybir.ActivationFunctionType
AX = mybir.AxisListType

P = 128
EPS = 1e-5


class Core:

    def __init__(self, nc, ctx):
        self.nc, self.ctx = nc, ctx

    def sb(self, name, shape, dt, ctx=None):
        return (ctx or self.ctx).enter_context(self.nc.sbuf_tensor("sb_" + name, shape, dt))

    def sem(self, name, ctx=None):
        return self.ctx.enter_context(self.nc.semaphore(name))


def chained(eng, sem):
    count = [0]

    def link(ins):
        count[0] += 1
        ins.then_inc(sem, 1)
        eng.wait_ge(sem, count[0])

    return link


def stage_l0_project(k, d, XH, XL, X, ident, qh, ql, kh, kl, V):
    nc = k.nc
    H, N = 256, X.shape[1] * P
    KC, NCH, TPC = H // P, N // 512, 4
    with ExitStack() as c:
        xf = k.sb("xf", [P, KC, N], F32, c)
        wf = k.sb("wf", [P, KC, 3 * H], F32, c)
        wh = k.sb("wh", [P, KC, 3 * H], FR, c)
        wl = k.sb("wl", [P, KC, 3 * H], FR, c)
        bqk = k.sb("bqk", [P, 4], F32, c)
        bvb = k.sb("bvb", [P, H], F32, c)
        ps = [c.enter_context(nc.psum_tensor(f"p1_{i}", [P, 512], F32)) for i in range(8)]
        x_in = [k.sem(f"x_in{i}", c) for i in range(NCH)]
        w_in = k.sem("w_in", c)
        misc_in = k.sem("misc_in", c)
        w_hi = k.sem("w_hi", c)
        w_split = k.sem("w_split", c)
        x_hi = k.sem("x_hi", c)
        x_split = k.sem("x_split", c)
        qk_done = k.sem("qk_done", c)
        v_done = k.sem("v_done", c)
        qk_hi = k.sem("qk_hi", c)
        qk_lo = k.sem("qk_lo", c)
        v_out = k.sem("v_out", c)

        with nc.Block() as block:
            @block.sync
            def _(sp):
                sp.dma_start(wf[:], d["wqkv"].rearrange("(c p) n -> p c n", p=P)).then_inc(w_in, 16)
                xt = d["xT"].rearrange("(c p) n -> p c n", p=P)
                for ch in range(NCH):
                    s = slice(512 * ch, 512 * ch + 512)
                    sp.dma_start(xf[:, :, s], xt[:, :, s]).then_inc(x_in[ch], 16)
                sp.dma_start(bqk[:], d["bqk"]).then_inc(misc_in, 16)
                sp.dma_start(bvb[:], d["bv"].partition_broadcast(P)).then_inc(misc_in, 16)
                sp.dma_start(ident[:], d["ident"]).then_inc(misc_in, 16)
                sp.dma_start(X[:], d["x"].rearrange("(t p) n -> p t n", p=P)).then_inc(misc_in, 16)
                sp.wait_ge(misc_in, 64)

            @block.scalar
            def _(act):
                act.wait_ge(w_in, 16)
                nc.scalar.copy(wh[:], wf[:]).then_inc(w_hi, 1)
                for ch in range(NCH):
                    s = slice(512 * ch, 512 * ch + 512)
                    act.wait_ge(x_in[ch], 16)
                    nc.scalar.copy(XH[:, :, s], xf[:, :, s]).then_inc(x_hi, 1)
                act.wait_ge(misc_in, 64)
                for n in range(4 * NCH):
                    ch, which, o = n // 4, (n // 2) % 2, n % 2
                    act.wait_ge(qk_done, n + 1)
                    dst = (qh, kh)[which]
                    nc.scalar.activation(dst[:, o, 512 * ch:512 * ch + 512], ps[n % 4][:], ACT.Identity,
                                         bias=bqk[:, 2 * which + o:2 * which + o + 1]).then_inc(qk_hi, 1)

            @block.vector
            def _(dve):
                dve.wait_ge(w_hi, 1)
                nc.vector.tensor_tensor(wl[:], wf[:], wh[:].bitcast(F32), ALU.subtract).then_inc(w_split, 1)
                for ch in range(NCH):
                    s = slice(512 * ch, 512 * ch + 512)
                    dve.wait_ge(x_hi, ch + 1)
                    nc.vector.tensor_tensor(XL[:, :, s], xf[:, :, s], XH[:, :, s].bitcast(F32),
                                            ALU.subtract).then_inc(x_split, 1)
                dve.wait_ge(misc_in, 64)
                for ch in range(NCH):
                    for j in range(4):
                        n, which, o = 4 * ch + j, j // 2, j % 2
                        hi, lo = ((qh, ql), (kh, kl))[which]
                        s = slice(512 * ch, 512 * ch + 512)
                        dve.wait_ge(qk_hi, n + 1)
                        nc.vector.scalar_tensor_tensor(
                            out=lo[:, o, s], in0=ps[n % 4][:], scalar=bqk[:, 2 * which + o:2 * which + o + 1],
                            in1=hi[:, o, s].bitcast(F32), op0=ALU.add, op1=ALU.subtract).then_inc(qk_lo, 1)
                    for j in range(TPC):
                        t = TPC * ch + j
                        dve.wait_ge(v_done, t + 1)
                        nc.vector.tensor_tensor(V[:, t, :], ps[4 + t % 4][:, 0:H], bvb[:], ALU.add).then_inc(v_out, 1)

            @block.tensor
            def _(pe):
                pe.wait_ge(w_split, 1)
                for ch in range(NCH):
                    pe.wait_ge(x_split, ch + 1)
                    s = slice(512 * ch, 512 * ch + 512)
                    for j in range(4):
                        n, which, o = 4 * ch + j, j // 2, j % 2
                        col = slice(H * which + P * o, H * which + P * o + P)
                        if n >= 4:
                            pe.wait_ge(qk_lo, n - 3)
                        mms = [(w[:, kc, col], x[:, kc, s]) for kc in range(KC)
                               for w, x in ((wh, XH), (wh, XL), (wl, XH))]
                        for i, (l, r) in enumerate(mms):
                            mm = pe.matmul(ps[n % 4][:], l, r, start=i == 0, stop=i == len(mms) - 1)
                        mm.then_inc(qk_done, 1)
                    for j in range(TPC):
                        t = TPC * ch + j
                        if t >= 4:
                            pe.wait_ge(v_out, t - 3)
                        ts = slice(P * t, P * t + P)
                        mms = [(x[:, kc, ts], w[:, kc, 2 * H:3 * H]) for kc in range(KC)
                               for x, w in ((XH, wh), (XL, wh), (XH, wl))]
                        for i, (l, r) in enumerate(mms):
                            mm = pe.matmul(ps[4 + t % 4][:, 0:H], l, r, start=i == 0, stop=i == len(mms) - 1)
                        mm.then_inc(v_done, 1)


class Norm:

    def __init__(self, k, ctx, half, tag):
        self.nc, self.half = k.nc, half
        self.stats = k.sb(tag + "_ln_stats", [P, 6], F32, ctx)
        self.mv = k.sb(tag + "_ln_mv", [P, 2, 2], F32, ctx)
        self.ve = k.sb(tag + "_ln_ve", [P, 1], F32, ctx)
        self.rstd = k.sb(tag + "_ln_rstd", [P, 2, 1], F32, ctx)
        self.var_ready = k.sem(tag + "_ln_var_ready", ctx)
        self.eps_added = k.sem(tag + "_ln_eps_added", ctx)
        self.rstd_ready = k.sem(tag + "_ln_rstd_ready", ctx)

    def statistics(self, n, y, link):
        link(self.nc.vector.bn_stats(self.stats[:], y))
        self.nc.vector.bn_aggr(self.mv[:, n % 2, :], self.stats[:]).then_inc(self.var_ready, 1)

    def power(self, pool, n):
        pool.wait_ge(self.var_ready, n + 1)
        if n >= 1:
            pool.wait_ge(self.rstd_ready, n)
        self.nc.gpsimd.tensor_scalar(self.ve[:], self.mv[:, n % 2, 1:2], EPS, None, ALU.add).then_inc(self.eps_added, 1)
        pool.wait_ge(self.eps_added, n + 1)
        self.nc.gpsimd.tensor_tensor(self.rstd[:, n % 2, :], self.ve[:], self.half[:], ALU.pow).then_inc(self.rstd_ready, 1)

    def scale(self, dve, n, out, y):
        dve.wait_ge(self.rstd_ready, n + 1)
        return self.nc.vector.tensor_scalar(out, y, self.mv[:, n % 2, 0:1], self.rstd[:, n % 2, :],
                                            ALU.subtract, ALU.mult)


def stage_l0_attention(k, XH, XL, X, ident, half, qh, ql, kh, kl, V):
    nc = k.nc
    H, T = 256, X.shape[1]
    S = 1024
    KT = S // P
    with ExitStack() as c:
        prob = k.sb("prob", [P, 2, S], F32, c)
        probT = k.sb("probT", [P, 2, KT, P], F32, c)
        neg_max = k.sb("neg_max", [P, 2, 1], F32, c)
        row_sum = k.sb("row_sum", [P, 2, 1], F32, c)
        inv_sum = k.sb("inv_sum", [P, 1], F32, c)
        y = k.sb("y2", [P, H], F32, c)
        p_s = [c.enter_context(nc.psum_tensor(f"p2_s{i}", [P, S], F32)) for i in range(2)]
        p_t = [c.enter_context(nc.psum_tensor(f"p2_t{i}", [P, 4, P], F32)) for i in range(2)]
        p_o = [c.enter_context(nc.psum_tensor(f"p2_o{i}", [P, 512], F32)) for i in range(2)]
        norm = Norm(k, c, half, "s2")
        scores_ready = k.sem("scores_ready", c)
        max_ready = k.sem("max_ready", c)
        prob_ready = k.sem("prob_ready", c)
        turned = k.sem("turned", c)
        turned_out = [k.sem(f"turned_out{i}", c) for i in range(2)]
        out_ready = k.sem("out_ready", c)
        x_new = k.sem("x_new", c)
        xT_ready = k.sem("xT_ready", c)
        xh_out = k.sem("xh_out", c)
        xl_out = k.sem("xl_out", c)
        v_chain = k.sem("v_chain", c)

        with nc.Block() as block:
            @block.tensor
            def _(pe):
                for t in range(T + 2):
                    if t < T:
                        if t >= 2:
                            pe.wait_ge(prob_ready, t - 1)
                        b, ts = t * P // S, slice(P * t, P * t + P)
                        for half_ in range(2):
                            ks = slice(b * S + 512 * half_, b * S + 512 * half_ + 512)
                            mms = [(q[:, kc, ts], kk[:, kc, ks]) for kc in range(2)
                                   for q, kk in ((qh, kh), (qh, kl), (ql, kh))]
                            for i, (l, r) in enumerate(mms):
                                mm = pe.matmul(p_s[t % 2][:, 512 * half_:512 * half_ + 512], l, r,
                                               start=i == 0, stop=i == len(mms) - 1)
                        mm.then_inc(scores_ready, 1)
                    u = t - 1
                    if 0 <= u < T:
                        pe.wait_ge(prob_ready, u + 1)
                        for h in range(2):
                            if u >= 1:
                                pe.wait_ge(turned_out[h], u)
                            for j in range(4):
                                kt = 4 * h + j
                                mm = pe.transpose(p_t[h][:, j, :], prob[:, u % 2, P * kt:P * kt + P], ident[:])
                            mm.then_inc(turned, 1)
                    w = t - 2
                    if 0 <= w < T:
                        pe.wait_ge(x_new, w + 1)
                        for kc in range(2):
                            mm = pe.transpose(p_o[w % 2][:, H + P * kc:H + P * kc + P], X[:, w, P * kc:P * kc + P], ident[:])
                        mm.then_inc(xT_ready, 1)
                    if 0 <= u < T:
                        pe.wait_ge(turned_out[0], u + 1)
                        pe.wait_ge(turned_out[1], u + 1)
                        if u >= 2:
                            pe.wait_ge(xl_out, u - 1)
                        b = u * P // S
                        for kt in range(KT):
                            mm = pe.matmul(p_o[u % 2][:, 0:H], probT[:, u % 2, kt, :], V[:, b * KT + kt, :],
                                           start=kt == 0, stop=kt == KT - 1)
                        mm.then_inc(out_ready, 1)

            @block.scalar
            def _(act):
                for t in range(T + 2):
                    if t < T:
                        act.wait_ge(max_ready, t + 1)
                        if t >= 2:
                            act.wait_ge(turned, 2 * (t - 1))
                        nc.scalar.activation(prob[:, t % 2, :], p_s[t % 2][:], ACT.Exp, bias=neg_max[:, t % 2, :],
                                             accum_out=row_sum[:, t % 2, :]).then_inc(prob_ready, 1)
                    u = t - 1
                    if 0 <= u < T:
                        act.wait_ge(turned, 2 * u + 1)
                        if u >= 2:
                            act.wait_ge(out_ready, u - 1)
                        nc.scalar.copy(probT[:, u % 2, 0:4, :], p_t[0][:]).then_inc(turned_out[0], 1)
                    w = t - 2
                    if 0 <= w < T:
                        act.wait_ge(xT_ready, w + 1)
                        nc.scalar.copy(XH[:, :, P * w:P * w + P],
                                       p_o[w % 2][:, H:2 * H].rearrange("p (c n) -> p c n", c=2)).then_inc(xh_out, 1)

            @block.vector
            def _(dve):
                link = chained(dve, v_chain)
                for t in range(T + 2):
                    if t < T:
                        dve.wait_ge(scores_ready, t + 1)
                        nc.vector.tensor_reduce(neg_max[:, t % 2, :], p_s[t % 2][:], AX.X, ALU.max,
                                                negate=True).then_inc(max_ready, 1)
                    u = t - 1
                    if 0 <= u < T:
                        dve.wait_ge(turned, 2 * u + 2)
                        if u >= 2:
                            dve.wait_ge(out_ready, u - 1)
                        nc.vector.tensor_copy(probT[:, u % 2, 4:8, :], p_t[1][:]).then_inc(turned_out[1], 1)
                    w = t - 2
                    if 0 <= w < T:
                        dve.wait_ge(xh_out, w + 1)
                        nc.vector.tensor_tensor(XL[:, :, P * w:P * w + P],
                                                p_o[w % 2][:, H:2 * H].rearrange("p (c n) -> p c n", c=2),
                                                XH[:, :, P * w:P * w + P].bitcast(F32), ALU.subtract).then_inc(xl_out, 1)
                    if 0 <= u < T:
                        dve.wait_ge(prob_ready, u + 1)
                        link(nc.vector.reciprocal(inv_sum[:], row_sum[:, u % 2, :]))
                        dve.wait_ge(out_ready, u + 1)
                        link(nc.vector.scalar_tensor_tensor(out=y[:], in0=p_o[u % 2][:, 0:H], scalar=inv_sum[:],
                                                            in1=X[:, u, :], op0=ALU.mult, op1=ALU.add))
                        norm.statistics(u, y[:], link)
                        norm.scale(dve, u, X[:, u, :], y[:]).then_inc(x_new, 1)
                        dve.wait_ge(x_new, u + 1)

            @block.gpsimd
            def _(pool):
                for u in range(T):
                    norm.power(pool, u)


def stage_ffn(k, d, XH, XL, X, ident, half):
    nc = k.nc
    H, IT, T = 256, 8, X.shape[1]
    I = IT * P
    NCH = T // 4
    with ExitStack() as c:
        wg8 = k.sb("wg8", [P, 2, I // 4], I32, c)
        wu8 = k.sb("wu8", [P, 2, I // 4], I32, c)
        wd8 = k.sb("wd8", [P, IT, H // 4], I32, c)
        wg = k.sb("wg", [P, 2, I], FR, c)
        wu = k.sb("wu", [P, 2, I], FR, c)
        wd = k.sb("wd", [P, IT, H], FR, c)
        s_gu = k.sb("s_gu", [P, 2, IT], F32, c)
        s_down = k.sb("s_down", [P, H], F32, c)
        gated = k.sb("gated", [P, 2, 512], F32, c)
        fuse = k.sb("fuse", [P, 2, 512], F32, c)
        fh = k.sb("fh", [P, 2, IT, 512], FR, c)
        fl = k.sb("fl", [P, 2, IT, 512], FR, c)
        y = k.sb("y3", [P, 2, H], F32, c)
        p_g = [c.enter_context(nc.psum_tensor(f"p3_g{i}", [P, 512], F32)) for i in range(2)]
        p_u = [c.enter_context(nc.psum_tensor(f"p3_u{i}", [P, 512], F32)) for i in range(2)]
        p_d = [c.enter_context(nc.psum_tensor(f"p3_d{i}", [P, 512], F32)) for i in range(2)]
        p_x = [c.enter_context(nc.psum_tensor(f"p3_x{i}", [P, 4, P], F32)) for i in range(2)]
        norm = Norm(k, c, half, "s3")
        wg_in, wu_in, wd_in, s_in = (k.sem(n, c) for n in ("wg_in", "wu_in", "wd_in", "s_in"))
        wg_cast, wu_cast, wd_cast = (k.sem(n, c) for n in ("wg_cast", "wu_cast", "wd_cast"))
        gate_ready, up_ready = k.sem("gate_ready", c), k.sem("up_ready", c)
        gated_ready, fuse_ready = k.sem("gated_ready", c), k.sem("fuse_ready", c)
        fh_ready, fl_ready = k.sem("fh_ready", c), k.sem("fl_ready", c)
        down_ready, scaled = k.sem("down_ready", c), k.sem("scaled", c)
        x_new, xT_ready, xh_out, xl_out = (k.sem(n, c) for n in ("x_new3", "xT_ready3", "xh_out3", "xl_out3"))
        v_chain = k.sem("v_chain3", c)

        def turned_after(m):
            return down_after(m - 2)

        def down_after(m):
            ch, i = divmod(m, IT)
            return [4 * (ch - 1) + (i - 1) // 2] if m >= 0 and ch >= 1 and i % 2 == 1 and ch < NCH else []

        with nc.Block() as block:
            @block.sync
            def _(sp):
                sp.dma_start(wg8[:], d["w_gate"].rearrange("(c p) n -> p c n", p=P)).then_inc(wg_in, 16)
                sp.dma_start(wu8[:], d["w_up"].rearrange("(c p) n -> p c n", p=P)).then_inc(wu_in, 16)
                sp.dma_start(s_gu[:], d["s_gu"]).then_inc(s_in, 16)
                sp.dma_start(s_down[:], d["s_down"].partition_broadcast(P)).then_inc(s_in, 16)
                sp.dma_start(wd8[:], d["w_down"].rearrange("(c p) n -> p c n", p=P)).then_inc(wd_in, 16)
                sp.wait_ge(wd_in, 16)

            @block.scalar
            def _(act):
                act.wait_ge(wg_in, 16)
                nc.scalar.copy(wg[:], wg8[:].bitcast(I8)).then_inc(wg_cast, 1)
                act.wait_ge(s_in, 32)
                for n in range(NCH * IT + 1):
                    if n == 1:
                        act.wait_ge(wd_in, 16)
                        nc.scalar.copy(wd[:], wd8[:].bitcast(I8)).then_inc(wd_cast, 1)
                    if n < NCH * IT:
                        i = n % IT
                        act.wait_ge(gate_ready, n + 1)
                        if n >= 2:
                            act.wait_ge(fuse_ready, n - 1)
                        nc.scalar.activation(gated[:, n % 2, :], p_g[n % 2][:], ACT.Silu,
                                             scale=s_gu[:, 0, i:i + 1]).then_inc(gated_ready, 1)
                    m = n - 1
                    if m >= 0:
                        ch, i = m // IT, m % IT
                        act.wait_ge(fuse_ready, m + 1)
                        if ch >= 2:
                            act.wait_ge(down_ready, 4 * (ch - 1))
                        nc.scalar.copy(fh[:, ch % 2, i, :], fuse[:, m % 2, :]).then_inc(fh_ready, 1)
                        for w in turned_after(m - 1):
                            act.wait_ge(xT_ready, w + 1)
                            nc.scalar.copy(XH[:, :, P * w:P * w + P], p_x[w % 2][:, 0:2, :]).then_inc(xh_out, 1)
                for w in range(T - 6, T):
                    act.wait_ge(xT_ready, w + 1)
                    nc.scalar.copy(XH[:, :, P * w:P * w + P], p_x[w % 2][:, 0:2, :]).then_inc(xh_out, 1)

            @block.vector
            def _(dve):
                link = chained(dve, v_chain)
                dve.wait_ge(wu_in, 16)
                nc.vector.tensor_copy(wu[:], wu8[:].bitcast(I8)).then_inc(wu_cast, 1)
                dve.wait_ge(s_in, 32)

                def low_x(w):
                    dve.wait_ge(xh_out, w + 1)
                    nc.vector.tensor_tensor(XL[:, :, P * w:P * w + P], p_x[w % 2][:, 0:2, :],
                                            XH[:, :, P * w:P * w + P].bitcast(F32), ALU.subtract).then_inc(xl_out, 1)

                def finish(t):
                    dve.wait_ge(down_ready, t + 1)
                    nc.vector.tensor_tensor(y[:, t % 2, :], p_d[t % 2][:, 0:H], s_down[:], ALU.mult).then_inc(scaled, 1)
                    dve.wait_ge(scaled, t + 1)
                    link(nc.vector.tensor_tensor(y[:, t % 2, :], y[:, t % 2, :], X[:, t, :], ALU.add))
                    norm.statistics(t, y[:, t % 2, :], link)
                    norm.scale(dve, t, X[:, t, :], y[:, t % 2, :]).then_inc(x_new, 1)

                for m in range(NCH * IT):
                    ch, i = divmod(m, IT)
                    dve.wait_ge(gated_ready, m + 1)
                    dve.wait_ge(up_ready, m + 1)
                    if m >= 2:
                        dve.wait_ge(fh_ready, m - 1)
                        dve.wait_ge(fl_ready, m - 1)
                    nc.vector.scalar_tensor_tensor(out=fuse[:, m % 2, :], in0=p_u[m % 2][:], scalar=s_gu[:, 1, i:i + 1],
                                                   in1=gated[:, m % 2, :], op0=ALU.mult, op1=ALU.mult).then_inc(fuse_ready, 1)
                    for w in turned_after(m - 1):
                        low_x(w)
                    for t in down_after(m - 1):
                        finish(t)
                low_x(T - 6)
                finish(T - 5)
                finish(T - 4)
                low_x(T - 5)
                for t in range(T - 3, T):
                    finish(t)
                    low_x(t - 1)
                low_x(T - 1)

            @block.gpsimd
            def _(pool):
                for m in range(NCH * IT):
                    ch, i = divmod(m, IT)
                    for t in down_after(m - 1):
                        norm.power(pool, t)
                    pool.wait_ge(fh_ready, m + 1)
                    if ch >= 2:
                        pool.wait_ge(down_ready, 4 * (ch - 1))
                    nc.gpsimd.tensor_tensor(fl[:, ch % 2, i, :], fuse[:, m % 2, :], fh[:, ch % 2, i, :].bitcast(F32),
                                            ALU.subtract).then_inc(fl_ready, 1)
                for t in range(T - 5, T):
                    norm.power(pool, t)

            @block.tensor
            def _(pe):
                def down(t):
                    ch, tt = divmod(t, 4)
                    pe.wait_ge(fl_ready, IT * (ch + 1))
                    if t == 0:
                        pe.wait_ge(wd_cast, 1)
                    if t >= 2:
                        pe.wait_ge(scaled, t - 1)
                    n = 0
                    for i in range(IT):
                        for part in (fh, fl):
                            mm = pe.matmul(p_d[t % 2][:, 0:H], part[:, ch % 2, i, P * tt:P * tt + P], wd[:, i, :],
                                           start=n == 0, stop=n == 2 * IT - 1)
                            n += 1
                    mm.then_inc(down_ready, 1)

                def turn(w):
                    pe.wait_ge(x_new, w + 1)
                    if w >= 2:
                        pe.wait_ge(xl_out, w - 1)
                    for kc in range(2):
                        mm = pe.transpose(p_x[w % 2][:, kc, :], X[:, w, P * kc:P * kc + P], ident[:])
                    mm.then_inc(xT_ready, 1)

                pe.wait_ge(wg_cast, 1)
                for m in range(NCH * IT):
                    ch, i = divmod(m, IT)
                    s = slice(512 * ch, 512 * ch + 512)
                    for dst, w, done, freed, cast in ((p_g, wg, gate_ready, gated_ready, wg_cast),
                                                      (p_u, wu, up_ready, fuse_ready, wu_cast)):
                        if m == 0:
                            pe.wait_ge(cast, 1)
                        if m >= 2:
                            pe.wait_ge(freed, m - 1)
                        mms = [(w[:, kc, P * i:P * i + P], x[:, kc, s]) for kc in range(2) for x in (XH, XL)]
                        for j, (l, r) in enumerate(mms):
                            mm = pe.matmul(dst[m % 2][:], l, r, start=j == 0, stop=j == len(mms) - 1)
                        mm.then_inc(done, 1)
                    for w_ in turned_after(m):
                        turn(w_)
                    for t in down_after(m):
                        down(t)
                down(T - 4)
                turn(T - 5)
                for t in range(T - 3, T):
                    down(t)
                    turn(t - 1)
                turn(T - 1)


HEADS, HD = 16, 16
TWO_PI = 6.283185307179586
TURN_PARTS = (6.28125, 0.001934051513671875, 1.255422830581665e-06, 2.430840251310684e-10)
ROUND = 12582912.0
HI0, MID1, Q_HI2, Q_MID4, Q_LO5 = 0, 1, 2, 4, 5
MAX_ROW, STACK_ROWS = 96, 99


def stage_l1_prepare(k, d, cos, sin, wh, wl, woh, wol):
    nc = k.nc
    ST = cos.shape[1]
    parts = TURN_PARTS
    with ExitStack() as c:
        wf = k.sb("l1_wf", [P, 2, 768], F32, c)
        wof = k.sb("l1_wof", [P, 2, 256], F32, c)
        pos = k.sb("pos", [P, ST], F32, c)
        freq = k.sb("freq", [P, 8], F32, c)
        ang = k.sb("ang", [P, ST, 8], F32, c)
        turns = k.sb("turns", [P, ST, 8], F32, c)
        over = k.sb("over", [P, ST, 8], F32, c)
        shifted = k.sb("shifted", [P, ST, 8], F32, c)
        w_in, hi_ready, small_in = k.sem("l1w_in"), k.sem("l1w_hi"), k.sem("l1_small_in")
        lo_ready, v_chain, reduced = k.sem("l1w_lo"), k.sem("v_chain4"), k.sem("angles_reduced")
        with nc.Block() as block:
            @block.sync
            def _(sp):
                sp.dma_start(pos[:], d["pos"]).then_inc(small_in, 16)
                sp.dma_start(freq[:], d["inv_freq"].partition_broadcast(P)).then_inc(small_in, 16)
                sp.dma_start(wf[:], d["l1_wqkv"].rearrange("(c p) n -> p c n", p=P)).then_inc(w_in, 16)
                sp.dma_start(wof[:], d["l1_wo"].rearrange("(c p) n -> p c n", p=P)).then_inc(w_in, 16)
                sp.wait_ge(w_in, 32)

            @block.scalar
            def _(act):
                act.wait_ge(w_in, 32)
                nc.scalar.copy(wh[:], wf[:]).then_inc(hi_ready, 1)
                nc.scalar.copy(woh[:], wof[:]).then_inc(hi_ready, 1)
                act.wait_ge(reduced, 2)
                nc.scalar.activation(sin[:], ang[:], ACT.Sin)
                nc.scalar.activation(cos[:], shifted[:], ACT.Sin)

            @block.vector
            def _(dve):
                link = chained(dve, v_chain)
                dve.wait_ge(small_in, 32)
                link(nc.vector.tensor_tensor(ang[:], pos[:].unsqueeze(2).broadcast_to([P, ST, 8]),
                                             freq[:].unsqueeze(1).broadcast_to([P, ST, 8]), ALU.mult))
                link(nc.vector.tensor_scalar(turns[:], ang[:], 1.0 / TWO_PI, None, ALU.mult))
                link(nc.vector.tensor_scalar(turns[:], turns[:], ROUND, None, ALU.add))
                link(nc.vector.tensor_scalar(turns[:], turns[:], -ROUND, None, ALU.add))
                for part in parts:
                    if part:
                        link(nc.vector.scalar_tensor_tensor(out=ang[:], in0=turns[:], scalar=-part, in1=ang[:],
                                                            op0=ALU.mult, op1=ALU.add))
                link(nc.vector.tensor_scalar(shifted[:], ang[:], TWO_PI / 4, None, ALU.add))
                link(nc.vector.tensor_scalar(over[:], shifted[:], TWO_PI / 2, -TWO_PI, ALU.is_gt, ALU.mult))
                link(nc.vector.tensor_tensor(shifted[:], shifted[:], over[:], ALU.add))
                for x in (ang, shifted):
                    nc.vector.tensor_scalar(x[:], x[:], 3.1415925, -3.1415925, ALU.min, ALU.max).then_inc(reduced, 1)
                dve.wait_ge(hi_ready, 2)
                nc.vector.tensor_tensor(wl[:], wf[:], wh[:].bitcast(F32), ALU.subtract).then_inc(lo_ready, 1)
                nc.vector.tensor_tensor(wol[:], wof[:], woh[:].bitcast(F32), ALU.subtract).then_inc(lo_ready, 1)


def stage_l1_attention(k, XH, XL, X, ident, half, cos, sin, wh, wl, woh, wol):
    nc = k.nc
    H, T = 256, X.shape[1]
    ST = cos.shape[1]
    SCALE = HD ** -0.5
    POOL_HEADS = 12
    with ExitStack() as c:
        rt = k.sb("rope_t", [P, 4, 2 * HEADS, 8], F32, c)
        rope = k.sb("rope", [P, 2, 2 * HEADS, HD], F32, c)
        v = k.sb("v5", [P, 2, HEADS, HD], F32, c)
        prod = k.sb("prod", [P, HEADS, HEADS, HD], F32, c)
        score = k.sb("score", [P, HEADS, HEADS], F32, c)
        nmax = k.sb("nmax", [P, HEADS], F32, c)
        shifted = k.sb("shifted5", [P, HEADS, HEADS], F32, c)
        prob = k.sb("prob5", [P, 2, HEADS, HEADS], F32, c)
        total = k.sb("total", [P, HEADS], F32, c)
        inv = k.sb("inv5", [P, HEADS], F32, c)
        pv = k.sb("pv", [P, HEADS, HEADS, HD], F32, c)
        a = k.sb("a5", [P, 2, HEADS, HD], F32, c)
        ah = k.sb("ah", [P, 2, 2, P], FR, c)
        al = k.sb("al", [P, 2, 2, P], FR, c)
        y = k.sb("y5", [P, 2, H], F32, c)
        p_qk = [c.enter_context(nc.psum_tensor(f"p5_qk{i}", [P, 512], F32)) for i in range(2)]
        p_v = c.enter_context(nc.psum_tensor("p5_v", [P, 512], F32))
        p_s = c.enter_context(nc.psum_tensor("p5_s", [P, 512], F32))
        p_a = c.enter_context(nc.psum_tensor("p5_a", [P, 4, P], F32))
        p_o = c.enter_context(nc.psum_tensor("p5_o", [P, 512], F32))
        p_x = [c.enter_context(nc.psum_tensor(f"p5_x{i}", [P, 4, P], F32)) for i in range(2)]
        norm = Norm(k, c, half, "s5")
        sem = lambda n: k.sem(n + "5")
        qk_ready, v_ready, v_out, rotated, roped = (sem(n) for n in ("qk_ready", "v_ready", "v_out", "rotated", "roped"))
        prod_pool, prod_dve, score_ready = sem("prod_pool"), sem("prod_dve"), sem("score_ready")
        shifted_ready, prob_ready = sem("shifted_ready"), sem("prob_ready")
        pv_pool, pv_dve, mixed, a_ready = sem("pv_pool"), sem("pv_dve"), sem("mixed"), sem("a_ready")
        aT_ready, ah_ready, al_ready = sem("aT_ready"), sem("ah_ready"), sem("al_ready")
        o_ready, summed, x_new = sem("o_ready"), sem("summed"), sem("x_new")
        xT_ready, xh_out, xl_out, v_chain = sem("xT_ready"), sem("xh_out"), sem("xl_out"), sem("v_chain")

        def score_product(eng, i, lo, hi):
            n = hi - lo
            return eng.tensor_tensor(prod[:, lo:hi], rope[:, i, lo:hi, :].unsqueeze(2).broadcast_to([P, n, HEADS, HD]),
                                     rope[:, i, HEADS:2 * HEADS, :].unsqueeze(1).broadcast_to([P, n, HEADS, HD]), ALU.mult)

        def value_product(eng, i, lo, hi):
            n = hi - lo
            return eng.tensor_tensor(pv[:, lo:hi], v[:, i, lo:hi, :].unsqueeze(2).broadcast_to([P, n, HEADS, HD]),
                                     prob[:, i, :, lo:hi].rearrange("p h t -> p t h").unsqueeze(3).broadcast_to([P, n, HEADS, HD]),
                                     ALU.mult)

        with nc.Block() as block:
            @block.gpsimd
            def _(pool):
                for t in range(T + 1):
                    if t < T:
                        pool.wait_ge(roped, 2 * (t + 1))
                        if t >= 1:
                            pool.wait_ge(score_ready, t)
                        score_product(nc.gpsimd, t % 2, 0, POOL_HEADS).then_inc(prod_pool, 1)
                    u = t - 1
                    if u >= 0:
                        pool.wait_ge(prob_ready, u + 1)
                        pool.wait_ge(v_out, u + 1)
                        if u >= 1:
                            pool.wait_ge(mixed, u)
                        value_product(nc.gpsimd, u % 2, 0, POOL_HEADS).then_inc(pv_pool, 1)
                    if u >= 1:
                        norm.power(pool, u - 1)
                norm.power(pool, T - 1)

            @block.vector
            def _(dve):
                link = chained(dve, v_chain)

                def rotate(t):
                    i = t % 2
                    dve.wait_ge(qk_ready, t + 1)
                    if t >= 1:
                        dve.wait_ge(roped, 2 * t)
                    qk = p_qk[i][:].rearrange("p (h n two) -> p h n two", n=8, two=2)
                    cb = cos[:, t % ST, :].unsqueeze(1).broadcast_to([P, 2 * HEADS, 8])
                    sb = sin[:, t % ST, :].unsqueeze(1).broadcast_to([P, 2 * HEADS, 8])
                    for m, (x, f) in enumerate(((0, cb), (1, sb), (0, sb), (1, cb))):
                        nc.vector.tensor_tensor(rt[:, m], qk[:, :, :, x], f, ALU.mult).then_inc(rotated, 1)
                    dve.wait_ge(rotated, 4 * (t + 1))
                    if t >= 2:
                        dve.wait_ge(prod_pool, t - 1)
                    nc.vector.tensor_tensor(rope[:, i, :, 0:8], rt[:, 0], rt[:, 1], ALU.subtract).then_inc(roped, 1)
                    nc.vector.tensor_tensor(rope[:, i, :, 8:16], rt[:, 2], rt[:, 3], ALU.add).then_inc(roped, 1)

                def attend(t):
                    i = t % 2
                    dve.wait_ge(roped, 2 * (t + 1))
                    score_product(nc.vector, i, POOL_HEADS, HEADS).then_inc(prod_dve, 1)
                    if t + 1 < T:
                        rotate(t + 1)
                    dve.wait_ge(prod_dve, t + 1)
                    dve.wait_ge(prod_pool, t + 1)
                    nc.vector.tensor_reduce(score[:], prod[:], AX.X, ALU.add).then_inc(score_ready, 1)
                    dve.wait_ge(score_ready, t + 1)
                    link(nc.vector.tensor_reduce(nmax[:], score[:], AX.X, ALU.max, negate=True))
                    if t >= 1:
                        dve.wait_ge(prob_ready, t)
                    nc.vector.tensor_tensor(shifted[:], score[:], nmax[:].unsqueeze(2).broadcast_to([P, HEADS, HEADS]),
                                            ALU.add).then_inc(shifted_ready, 1)
                    dve.wait_ge(shifted_ready, t + 1)

                def mix(u):
                    i = u % 2
                    dve.wait_ge(prob_ready, u + 1)
                    dve.wait_ge(v_out, u + 1)
                    if u >= 1:
                        dve.wait_ge(mixed, u)
                    value_product(nc.vector, i, POOL_HEADS, HEADS).then_inc(pv_dve, 1)
                    link(nc.vector.tensor_reduce(total[:], prob[:, i], AX.X, ALU.add))
                    link(nc.vector.reciprocal(inv[:], total[:]))

                def normalise(u):
                    dve.wait_ge(mixed, u + 1)
                    if u >= 2:
                        dve.wait_ge(aT_ready, u - 1)
                    nc.vector.tensor_tensor(a[:, u % 2], p_s[:, 0:H].rearrange("p (h n) -> p h n", h=HEADS),
                                            inv[:].unsqueeze(2).broadcast_to([P, HEADS, HD]), ALU.mult).then_inc(a_ready, 1)
                    dve.wait_ge(a_ready, u + 1)

                def low_a(u):
                    dve.wait_ge(ah_ready, u + 1)
                    if u >= 2:
                        dve.wait_ge(o_ready, u - 1)
                    nc.vector.tensor_tensor(al[:, u % 2], p_a[:, 0:2, :], ah[:, u % 2].bitcast(F32),
                                            ALU.subtract).then_inc(al_ready, 1)

                def residual(u):
                    dve.wait_ge(o_ready, u + 1)
                    nc.vector.tensor_tensor(y[:, u % 2, :], p_o[:, 0:H], X[:, u, :], ALU.add).then_inc(summed, 1)
                    dve.wait_ge(summed, u + 1)
                    norm.statistics(u, y[:, u % 2, :], link)

                def scale(u):
                    norm.scale(dve, u, X[:, u, :], y[:, u % 2, :]).then_inc(x_new, 1)
                    dve.wait_ge(x_new, u + 1)

                def low_x(w):
                    dve.wait_ge(xh_out, w + 1)
                    nc.vector.tensor_tensor(XL[:, :, P * w:P * w + P], p_x[w % 2][:, 0:2, :],
                                            XH[:, :, P * w:P * w + P].bitcast(F32), ALU.subtract).then_inc(xl_out, 1)

                rotate(0)
                for t in range(T + 4):
                    if t < T:
                        attend(t)
                    if 0 <= t - 2 < T:
                        low_a(t - 2)
                    if 0 <= t - 1 < T:
                        mix(t - 1)
                    if 0 <= t - 2 < T:
                        residual(t - 2)
                    if 0 <= t - 1 < T:
                        normalise(t - 1)
                    if 0 <= t - 3 < T:
                        scale(t - 3)
                    if 0 <= t - 4 < T:
                        low_x(t - 4)

            @block.scalar
            def _(act):
                for t in range(T + 5):
                    if t < T:
                        act.wait_ge(v_ready, t + 1)
                        if t >= 2:
                            act.wait_ge(pv_pool, t - 1)
                            act.wait_ge(pv_dve, t - 1)
                        nc.scalar.copy(v[:, t % 2], p_v[:, 0:H].rearrange("p (h n) -> p h n", h=HEADS)).then_inc(v_out, 1)
                        act.wait_ge(shifted_ready, t + 1)
                        if t >= 2:
                            act.wait_ge(pv_dve, t - 1)
                            act.wait_ge(mixed, t - 1)
                        nc.scalar.activation(prob[:, t % 2], shifted[:], ACT.Exp, scale=SCALE).then_inc(prob_ready, 1)
                    u = t - 1
                    if 0 <= u < T:
                        act.wait_ge(aT_ready, u + 1)
                        if u >= 2:
                            act.wait_ge(o_ready, u - 1)
                        nc.scalar.copy(ah[:, u % 2], p_a[:, 0:2, :]).then_inc(ah_ready, 1)
                    w = t - 4
                    if 0 <= w < T:
                        act.wait_ge(xT_ready, w + 1)
                        nc.scalar.copy(XH[:, :, P * w:P * w + P], p_x[w % 2][:, 0:2, :]).then_inc(xh_out, 1)

            @block.tensor
            def _(pe):
                def project(t):
                    ts = slice(P * t, P * t + P)
                    mms = [(x, w, kc) for kc in range(2) for x, w in ((XH, wh), (XL, wh), (XH, wl))]
                    if t >= 2:
                        pe.wait_ge(rotated, 4 * (t - 1))
                    for n, (x, w, kc) in enumerate(mms):
                        mm = pe.matmul(p_qk[t % 2][:], x[:, kc, ts], w[:, kc, 0:512], start=n == 0, stop=n == 5)
                    mm.then_inc(qk_ready, 1)
                    if t >= 1:
                        pe.wait_ge(v_out, t)
                    for n, (x, w, kc) in enumerate(mms):
                        mm = pe.matmul(p_v[:, 0:H], x[:, kc, ts], w[:, kc, 512:768], start=n == 0, stop=n == 5)
                    mm.then_inc(v_ready, 1)

                project(0)
                for t in range(T + 5):
                    if t + 1 < T:
                        project(t + 1)
                    u = t - 2
                    if 0 <= u < T:
                        pe.wait_ge(al_ready, u + 1)
                        if u >= 1:
                            pe.wait_ge(summed, u)
                        mms = [(x, w, kc) for kc in range(2) for x, w in ((ah, woh), (al, woh), (ah, wol))]
                        for n, (x, w, kc) in enumerate(mms):
                            mm = pe.matmul(p_o[:, 0:H], x[:, u % 2, kc, :], w[:, kc, :], start=n == 0, stop=n == 5)
                        mm.then_inc(o_ready, 1)
                    u = t - 1
                    if 0 <= u < T:
                        if u >= 1:
                            pe.wait_ge(a_ready, u)
                        pe.wait_ge(pv_dve, u + 1)
                        for n, tt in enumerate([*range(POOL_HEADS, HEADS), *range(POOL_HEADS)]):
                            if n == HEADS - POOL_HEADS:
                                pe.wait_ge(pv_pool, u + 1)
                            mm = pe.matmul(p_s[:, 0:H], ident[:], pv[:, tt], start=n == 0, stop=n == HEADS - 1)
                        mm.then_inc(mixed, 1)
                        pe.wait_ge(a_ready, u + 1)
                        if u >= 1:
                            pe.wait_ge(al_ready, u)
                        for kc in range(2):
                            mm = pe.transpose(p_a[:, kc, :], a[:, u % 2, 8 * kc:8 * kc + 8, :].rearrange("p h n -> p (h n)"),
                                              ident[:])
                        mm.then_inc(aT_ready, 1)
                    w = t - 4
                    if 0 <= w < T:
                        pe.wait_ge(x_new, w + 1)
                        if w >= 2:
                            pe.wait_ge(xl_out, w - 1)
                        for kc in range(2):
                            mm = pe.transpose(p_x[w % 2][:, kc, :], X[:, w, P * kc:P * kc + P], ident[:])
                        mm.then_inc(xT_ready, 1)


EXPERTS, TOP = 64, 8
LOWEST = -3.0e38


def stage_route(k, d, XH, XL, ident, WT, WS):
    nc = k.nc
    T = XH.shape[2] // P
    E1 = EXPERTS + 1
    with ExitStack() as c:
        rf = k.sb("router_f", [P, 2, E1], F32, c)
        rh = k.sb("router_h", [P, 2, E1 + 1], FR, c)
        rl = k.sb("router_l", [P, 2, E1 + 1], FR, c)
        logit = k.sb("logit", [P, T, E1], F32, c)
        left = k.sb("left", [P, T, EXPERTS], F32, c)
        best = k.sb("best", [P, T, TOP], F32, c)
        chosen = k.sb("chosen", [P, T, EXPERTS], F32, c)
        weight = k.sb("weight", [P, T, EXPERTS], F32, c)
        total = k.sb("total6", [P, T], F32, c)
        inv = k.sb("inv6", [P, T], F32, c)
        sig = k.sb("sig", [P, T], F32, c)
        wn = k.sb("wn", [P, T, 2 * EXPERTS], FR, c)
        sn = k.sb("sn", [P, T, 2], FR, c)
        p_l = [c.enter_context(nc.psum_tensor(f"p6_l{i}", [P, 512], F32)) for i in range(2)]
        p_w = [c.enter_context(nc.psum_tensor(f"p6_w{i}", [P, 4, P], F32)) for i in range(2)]
        p_g = [c.enter_context(nc.psum_tensor(f"p6_g{i}", [P, 4, P], F32)) for i in range(2)]
        sem = lambda n: k.sem(n + "6")
        r_in, r_zero, r_hi, r_lo = sem("r_in"), sem("r_zero"), sem("r_hi"), sem("r_lo")
        l_ready, l_out, replaced = sem("l_ready"), sem("l_out"), sem("replaced")
        lowered, exp_ready, v_chain = sem("lowered"), sem("exp_ready"), sem("v_chain")
        split, t_ready, t_out = sem("split"), sem("t_ready"), sem("t_out")
        with nc.Block() as block:
            @block.sync
            def _(sp):
                sp.dma_start(rf[:], d["router"].rearrange("(c p) n -> p c n", p=P)).then_inc(r_in, 16)
                sp.wait_ge(r_in, 16)

            @block.tensor
            def _(pe):
                pe.wait_ge(r_lo, 1)
                for t in range(T):
                    if t >= 2:
                        pe.wait_ge(l_out, t - 1)
                    mms = [(x, w, kc) for kc in range(2) for x, w in ((XH, rh), (XL, rh), (XH, rl))]
                    for n, (x, w, kc) in enumerate(mms):
                        mm = pe.matmul(p_l[t % 2][:, 0:E1 + 1], x[:, kc, P * t:P * t + P], w[:, kc, :], start=n == 0, stop=n == 5)
                    mm.then_inc(l_ready, 1)
                pe.wait_ge(split, 4)
                for r in range(T // 4):
                    if r >= 2:
                        pe.wait_ge(t_out, 2 * (r - 1))
                    for j in range(4):
                        mm = pe.transpose(p_w[r % 2][:, j, :], wn[:, 4 * r + j, :].bitcast(F32), ident[:])
                        mm = pe.transpose(p_g[r % 2][0:2, j, :], sn[:, 4 * r + j, :].bitcast(F32), ident[:])
                    mm.then_inc(t_ready, 1)

            @block.scalar
            def _(act):
                act.wait_ge(r_in, 16)
                act.wait_ge(r_zero, 1)
                nc.scalar.copy(rh[:, :, 0:E1], rf[:]).then_inc(r_hi, 1)
                for t in range(T):
                    act.wait_ge(l_ready, t + 1)
                    nc.scalar.copy(logit[:, t, :], p_l[t % 2][:, 0:E1]).then_inc(l_out, 1)
                act.wait_ge(l_out, T)
                nc.scalar.activation(sig[:], logit[:, :, EXPERTS], ACT.Exp, scale=-1.0).then_inc(exp_ready, 1)
                act.wait_ge(lowered, 1)
                nc.scalar.activation(weight[:], weight[:], ACT.Exp).then_inc(exp_ready, 1)
                for r in range(T // 4):
                    act.wait_ge(t_ready, r + 1)
                    nc.scalar.copy(WT[:, 512 * r:512 * r + 512], p_w[r % 2][:].rearrange("p a n -> p (a n)")).then_inc(t_out, 1)
                    nc.scalar.copy(WS[:, 512 * r:512 * r + 512], p_g[r % 2][0:2].rearrange("p a n -> p (a n)")).then_inc(t_out, 1)

            @block.vector
            def _(dve):
                link = chained(dve, v_chain)
                link(nc.vector.memset(rh[:, :, E1:E1 + 1].bitcast(F32), 0.0))
                nc.vector.memset(rl[:, :, E1:E1 + 1].bitcast(F32), 0.0).then_inc(r_zero, 1)
                dve.wait_ge(r_hi, 1)
                nc.vector.tensor_tensor(rl[:, :, 0:E1], rf[:], rh[:, :, 0:E1].bitcast(F32), ALU.subtract).then_inc(r_lo, 1)
                for t in range(T):
                    dve.wait_ge(l_out, t + 1)
                    link(nc.vector.max(best[:, t, :], logit[:, t, 0:EXPERTS]))
                    nc.vector.match_replace(left[:, t, :], best[:, t, :], logit[:, t, 0:EXPERTS], LOWEST).then_inc(replaced, 1)
                wide = lambda x: x.unsqueeze(2).broadcast_to([P, T, EXPERTS])
                nc.vector.tensor_tensor(weight[:], logit[:, :, 0:EXPERTS], wide(best[:, :, 0]), ALU.subtract).then_inc(lowered, 1)
                dve.wait_ge(replaced, T)
                link(nc.vector.tensor_tensor(chosen[:], left[:], logit[:, :, 0:EXPERTS], ALU.not_equal))
                dve.wait_ge(exp_ready, 2)
                link(nc.vector.tensor_tensor(weight[:], weight[:], chosen[:], ALU.mult))
                link(nc.vector.tensor_reduce(total[:], weight[:], AX.X, ALU.add))
                link(nc.vector.reciprocal(inv[:], total[:]))
                link(nc.vector.tensor_tensor(weight[:], weight[:], wide(inv[:]), ALU.mult))
                nc.vector.tensor_copy(wn[:, :, 0:EXPERTS], weight[:]).then_inc(split, 1)
                dve.wait_ge(split, 1)
                nc.vector.tensor_tensor(wn[:, :, EXPERTS:2 * EXPERTS], weight[:], wn[:, :, 0:EXPERTS].bitcast(F32),
                                        ALU.subtract).then_inc(split, 1)
                link(nc.vector.tensor_scalar(sig[:], sig[:], 1.0, None, ALU.add))
                link(nc.vector.reciprocal(sig[:], sig[:]))
                nc.vector.tensor_copy(sn[:, :, 0], sig[:]).then_inc(split, 1)
                dve.wait_ge(split, 3)
                nc.vector.tensor_tensor(sn[:, :, 1], sig[:], sn[:, :, 0].bitcast(F32), ALU.subtract).then_inc(split, 1)


PAIRS = EXPERTS // 2


def stage_experts(k, d, XH, XL, X, ident, half, WT, WS, out):
    nc = k.nc
    H, T = 256, X.shape[1]
    NCH = T // 4
    STEPS = PAIRS + 1
    with ExitStack() as c:
        gu = k.sb("gu", [P, 2, STEPS, 256], F32, c)
        dn = k.sb("dn", [P, STEPS, 256], F32, c)
        sel_f = k.sb("sel_f", [P, 2, P], F32, c)
        sel = k.sb("sel", [P, 2, P], FR, c)
        ones = k.sb("ones7", [2, P], FR, c)
        guh = k.sb("guh", [P, 2, 2, 256], FR, c)
        gul = k.sb("gul", [P, 2, 2, 256], FR, c)
        dh = k.sb("dh", [P, 2, 256], FR, c)
        dl = k.sb("dl", [P, 2, 256], FR, c)
        gated = k.sb("gated7", [P, 2, 512], F32, c)
        weighted = k.sb("weighted", [P, 2, 512], F32, c)
        inter = k.sb("inter", [P, 2, 512], F32, c)
        ih = k.sb("ih", [P, 2, 512], FR, c)
        il = k.sb("il", [P, 2, 512], FR, c)
        acc = k.sb("acc", [P, 2, 512], F32, c)
        y = k.sb("y7", [P, 2, H], F32, c)
        p_g = [c.enter_context(nc.psum_tensor(f"p7_g{i}", [P, 512], F32)) for i in range(2)]
        p_u = [c.enter_context(nc.psum_tensor(f"p7_u{i}", [P, 512], F32)) for i in range(2)]
        p_w = [c.enter_context(nc.psum_tensor(f"p7_w{i}", [P, 512], F32)) for i in range(2)]
        p_y = [c.enter_context(nc.psum_tensor(f"p7_y{i}", [P, 512], F32)) for i in range(2)]
        norm = Norm(k, c, half, "s7")
        sem = lambda n: k.sem(n + "7")
        LOADS = 8
        w_in = [sem(f"w_in{i}") for i in range(LOADS)]
        sel_in = [sem(f"sel_in{i}") for i in range(2)]
        sel_cast, ones_set = sem("sel_cast"), sem("ones_set")
        guh_ready, dh_ready, gul_ready, dl_ready = sem("guh_ready"), sem("dh_ready"), sem("gul_ready"), sem("dl_ready")
        w_ready, g_ready, u_ready, down_done = sem("w_ready"), sem("g_ready"), sem("u_ready"), sem("down_done")
        gated_ready, weighted_ready, inter_ready = sem("gated_ready"), sem("weighted_ready"), sem("inter_ready")
        ih_ready, il_ready, acc_out, summed = sem("ih_ready"), sem("il_ready"), sem("acc_out"), sem("summed")
        turned, x_new, v_chain, stored = sem("turned"), sem("x_new"), sem("v_chain"), sem("stored")
        bounds = [STEPS * i // LOADS for i in range(LOADS + 1)]
        load_of = [next(i for i in range(LOADS) if bounds[i] <= p < bounds[i + 1]) for p in range(STEPS)]

        def w_uses(n):
            ch, p = divmod(n, STEPS)
            return n + 4 * max(0, ch - 1 + (1 if ch and p >= 1 else 0))

        with nc.Block() as block:
            @block.sync
            def _(sp):
                gus = d["gu"].rearrange("(c p) (e n) -> p c e n", p=P, n=256)
                dns = d["dn"].rearrange("(e p) n -> p e n", p=P)
                sels = d["sel"].rearrange("p (e n) -> p e n", n=P)
                N = NCH * STEPS
                for i in range(LOADS):
                    s = slice(bounds[i], bounds[i + 1])
                    for kc in range(2):
                        sp.dma_start(gu[:, kc, s, :], gus[:, kc, s, :]).then_inc(w_in[i], 16)
                    sp.dma_start(dn[:, s, :], dns[:, s, :]).then_inc(w_in[i], 16)
                    if i == 0:
                        for n in range(2):
                            sp.dma_start(sel_f[:, n, :], sels[:, n, :]).then_inc(sel_in[n], 16)
                m = 2
                for n in range(2, N):
                    if n % STEPS == PAIRS:
                        continue
                    sp.wait_ge(sel_cast, m - 1)
                    sp.dma_start(sel_f[:, m % 2, :], sels[:, n % STEPS, :]).then_inc(sel_in[m % 2], 16)
                    m += 1
                sp.wait_ge(stored, 16 * T)

            @block.scalar
            def _(act):
                N = NCH * STEPS
                sels = [0]

                def split_weights(n):
                    p = n % STEPS
                    if n < STEPS:
                        act.wait_ge(w_in[load_of[p]], 48)
                    if p < PAIRS:
                        m = sels[0]
                        sels[0] += 1
                        act.wait_ge(sel_in[m % 2], 16 * (m // 2 + 1))
                        if n >= 2:
                            act.wait_ge(w_ready, n - 1)
                        nc.scalar.copy(sel[:, n % 2, :], sel_f[:, m % 2, :]).then_inc(sel_cast, 1)
                    if n >= 2:
                        act.wait_ge(u_ready, n - 1)
                        act.wait_ge(gul_ready, n - 1)
                    nc.scalar.copy(guh[:, n % 2], gu[:, :, p, :]).then_inc(guh_ready, 1)
                    if n >= 2:
                        act.wait_ge(down_done, n - 1)
                        act.wait_ge(dl_ready, n - 1)
                    nc.scalar.copy(dh[:, n % 2], dn[:, p, :]).then_inc(dh_ready, 1)

                split_weights(0)
                split_weights(1)
                for n in range(N):
                    act.wait_ge(g_ready, n + 1)
                    if n >= 2:
                        act.wait_ge(weighted_ready, n - 1)
                    nc.scalar.activation(gated[:, n % 2, :], p_g[n % 2][:], ACT.Silu).then_inc(gated_ready, 1)
                    act.wait_ge(inter_ready, n + 1)
                    if n >= 2:
                        act.wait_ge(down_done, n - 1)
                    nc.scalar.copy(ih[:, n % 2, :], inter[:, n % 2, :]).then_inc(ih_ready, 1)
                    if n % STEPS == 0 and n:
                        ch = n // STEPS - 1
                        act.wait_ge(down_done, n)
                        if ch:
                            act.wait_ge(turned, 4 * ch)
                        for i in range(2):
                            nc.scalar.copy(acc[:, i, :], p_y[i][:]).then_inc(acc_out, 1)
                    if n + 2 < N:
                        split_weights(n + 2)
                act.wait_ge(down_done, N)
                act.wait_ge(turned, 4 * (NCH - 1))
                for i in range(2):
                    nc.scalar.copy(acc[:, i, :], p_y[i][:]).then_inc(acc_out, 1)
                for t in range(T):
                    act.wait_ge(x_new, t + 1)
                    act.dma_start(out[P * t:P * t + P, :], X[:, t, :]).then_inc(stored, 16)

            @block.gpsimd
            def _(pool):
                N = NCH * STEPS

                def split_weights(n):
                    p = n % STEPS
                    pool.wait_ge(guh_ready, n + 1)
                    if n >= 2:
                        pool.wait_ge(u_ready, n - 1)
                    nc.gpsimd.tensor_tensor(gul[:, n % 2], gu[:, :, p, :], guh[:, n % 2].bitcast(F32), ALU.subtract).then_inc(gul_ready, 1)
                    pool.wait_ge(dh_ready, n + 1)
                    if n >= 2:
                        pool.wait_ge(down_done, n - 1)
                    nc.gpsimd.tensor_tensor(dl[:, n % 2], dn[:, p, :], dh[:, n % 2].bitcast(F32), ALU.subtract).then_inc(dl_ready, 1)

                for n in range(N):
                    split_weights(n)
                    if n >= 4 and n % STEPS == 1:
                        for t in range(4 * (n // STEPS) - 4, 4 * (n // STEPS)):
                            norm.power(pool, t)
                for t in range(T - 4, T):
                    norm.power(pool, t)

            @block.vector
            def _(dve):
                link = chained(dve, v_chain)
                N = NCH * STEPS
                link(nc.vector.memset(ones[:].bitcast(F32), 1.0))
                nc.vector.tensor_copy(ones[:], ones[:].bitcast(F32)).then_inc(ones_set, 1)

                def step(n):
                    i = n % 2
                    dve.wait_ge(gated_ready, n + 1)
                    dve.wait_ge(w_ready, n + 1)
                    if n >= 2:
                        dve.wait_ge(inter_ready, n - 1)
                    nc.vector.tensor_tensor(weighted[:, i, :], gated[:, i, :], p_w[w_uses(n) % 2][:], ALU.mult).then_inc(weighted_ready, 1)
                    dve.wait_ge(weighted_ready, n + 1)
                    dve.wait_ge(u_ready, n + 1)
                    if n >= 2:
                        dve.wait_ge(ih_ready, n - 1)
                        dve.wait_ge(il_ready, n - 1)
                    nc.vector.tensor_tensor(inter[:, i, :], weighted[:, i, :], p_u[i][:], ALU.mult).then_inc(inter_ready, 1)

                def low(n):
                    i = n % 2
                    dve.wait_ge(ih_ready, n + 1)
                    if n >= 2:
                        dve.wait_ge(down_done, n - 1)
                    nc.vector.tensor_tensor(il[:, i, :], inter[:, i, :], ih[:, i, :].bitcast(F32), ALU.subtract).then_inc(il_ready, 1)

                def finish(ch):
                    n = (ch + 1) * STEPS
                    first = w_uses(n) + 1 if ch + 1 < NCH else w_uses(N - 1) + 1
                    for j in range(4):
                        t = 4 * ch + j
                        dve.wait_ge(turned, t + 1)
                        nc.vector.tensor_tensor(y[:, t % 2, :], p_w[(first + j) % 2][:, 0:H], X[:, t, :], ALU.add).then_inc(summed, 1)
                        dve.wait_ge(summed, t + 1)
                        norm.statistics(t, y[:, t % 2, :], link)
                        norm.scale(dve, t, X[:, t, :], y[:, t % 2, :]).then_inc(x_new, 1)
                        dve.wait_ge(x_new, t + 1)

                for n in range(N):
                    step(n)
                    low(n)
                    if n % STEPS == 0 and n:
                        finish(n // STEPS - 1)
                finish(NCH - 1)

            @block.tensor
            def _(pe):
                N = NCH * STEPS

                def gates(n):
                    ch, p = divmod(n, STEPS)
                    i, s = n % 2, slice(512 * ch, 512 * ch + 512)
                    pw = p_w[w_uses(n) % 2]
                    if n >= 2:
                        pe.wait_ge(weighted_ready, n - 1)
                    if ch and p == 1:
                        pe.wait_ge(weighted_ready, n)
                    if ch and p in (1, 2):
                        pe.wait_ge(summed, 4 * ch)
                    if p < PAIRS:
                        pe.wait_ge(sel_cast, n - n // STEPS + 1)
                        pe.matmul(pw[:], sel[:, i, :], WT[:, s], start=True, stop=True).then_inc(w_ready, 1)
                    else:
                        pe.wait_ge(ones_set, 1)
                        pe.matmul(pw[:], ones[:], WS[:, s], start=True, stop=True).then_inc(w_ready, 1)
                    pe.wait_ge(gul_ready, n + 1)
                    for dst, done, freed, o in ((p_g, g_ready, gated_ready, 0), (p_u, u_ready, inter_ready, P)):
                        if n >= 2:
                            pe.wait_ge(freed, n - 1)
                        mms = [(w, x, kc) for kc in range(2) for w, x in ((guh, XH), (guh, XL), (gul, XH))]
                        for m, (w, x, kc) in enumerate(mms):
                            mm = pe.matmul(dst[i][:], w[:, i, kc, o:o + P], x[:, kc, s], start=m == 0, stop=m == 5)
                        mm.then_inc(done, 1)

                def down(n):
                    i, p, ch = n % 2, n % STEPS, n // STEPS
                    pe.wait_ge(dl_ready, n + 1)
                    pe.wait_ge(il_ready, n + 1)
                    if p == 0 and ch:
                        pe.wait_ge(acc_out, 2 * ch)
                    for hc in range(2):
                        for m, (w, x) in enumerate(((dh, ih), (dh, il), (dl, ih))):
                            mm = pe.matmul(p_y[hc][:], w[:, i, P * hc:P * hc + P], x[:, i, :],
                                           start=p == 0 and m == 0, stop=p == STEPS - 1 and m == 2)
                    mm.then_inc(down_done, 1)

                def turn(ch):
                    pe.wait_ge(acc_out, 2 * (ch + 1))
                    n = (ch + 1) * STEPS
                    first = w_uses(n) + 1 if ch + 1 < NCH else w_uses(N - 1) + 1
                    pe.wait_ge(weighted_ready, min(n + 1, N))
                    for j in range(4):
                        t = 4 * ch + j
                        if j >= 2:
                            pe.wait_ge(summed, t - 1)
                        for hc in range(2):
                            mm = pe.transpose(p_w[(first + j) % 2][:, P * hc:P * hc + P], acc[:, hc, P * j:P * j + P], ident[:])
                        mm.then_inc(turned, 1)

                for n in range(N):
                    gates(n)
                    if n:
                        down(n - 1)
                    if n % STEPS == 0 and n:
                        turn(n // STEPS - 1)
                down(N - 1)
                turn(NCH - 1)


def build(nc, d, out, stop_after=99):
    T = 16
    H = 256
    with ExitStack() as ctx:
        k = Core(nc, ctx)
        X = k.sb("X", [P, T, H], F32)
        XH = k.sb("XH", [P, 2, T * P], FR)
        XL = k.sb("XL", [P, 2, T * P], FR)
        ident = k.sb("ident", [P, P], F32)
        half = k.sb("half", [P, 1], F32)
        half_set = k.sem("half_set")
        stored = k.sem("stored")
        with ExitStack() as c:
            qh, ql, kh, kl = (k.sb(n, [P, 2, T * P], FR, c) for n in ("qh", "ql", "kh", "kl"))
            V = k.sb("V", [P, T, H], F32, c)
            stage_l0_project(k, d, XH, XL, X, ident, qh, ql, kh, kl, V)
            with nc.Block() as block:
                @block.vector
                def _(dve):
                    nc.vector.memset(half[:], -0.5).then_inc(half_set, 1)
                    dve.wait_ge(half_set, 1)
            stage_l0_attention(k, XH, XL, X, ident, half, qh, ql, kh, kl, V)
        if stop_after > 2:
            from_stage_3(k, d, XH, XL, X, ident, half, out, stop_after)
        if stop_after < 6:
            with nc.Block() as block:
                @block.sync
                def _(sp):
                    sp.dma_start(out.rearrange("(t p) n -> p t n", p=P), X[:]).then_inc(stored, 16)
                    sp.wait_ge(stored, 16)


def from_stage_3(k, d, XH, XL, X, ident, half, out, stop_after):
    stage_ffn(k, d, XH, XL, X, ident, half)
    if stop_after > 3:
        with ExitStack() as c:
            cos, sin = (k.sb(n, [P, 8, 8], F32, c) for n in ("cos", "sin"))
            wh, wl = (k.sb(n, [P, 2, 768], FR, c) for n in ("l1_wh", "l1_wl"))
            woh, wol = (k.sb(n, [P, 2, 256], FR, c) for n in ("l1_woh", "l1_wol"))
            stage_l1_prepare(k, d, cos, sin, wh, wl, woh, wol)
            stage_l1_attention(k, XH, XL, X, ident, half, cos, sin, wh, wl, woh, wol)
    if stop_after > 5:
        with ExitStack() as c:
            WT = k.sb("WT", [P, XH.shape[2]], FR, c)
            WS = k.sb("WS", [2, XH.shape[2]], FR, c)
            stage_route(k, d, XH, XL, ident, WT, WS)
            stage_experts(k, d, XH, XL, X, ident, half, WT, WS, out)


def layouts(i):
    import numpy as np
    a = np.asarray
    x = a(i["L0_attn_input"]).reshape(-1, 256)
    gate_up = a(i["L1_ffn_gu_w"]).reshape(32, 2, 2, 64, 256)
    gate_up = gate_up.transpose(4, 0, 2, 1, 3).reshape(256, 32 * 256)
    no = np.zeros((256, 64), np.float32)
    shared = np.concatenate([a(i["L1_ffn_sh_gate_w"]).T, no, a(i["L1_ffn_sh_up_w"]).T, no], axis=1)
    down = a(i["L1_ffn_dp_w"]).transpose(0, 2, 1).reshape(64 * 64, 256)
    select = np.zeros((128, 32, 2, 64), np.float32)
    for e in range(64):
        select[e, e // 2, e % 2] = select[64 + e, e // 2, e % 2] = 1
    out = {
        "x": x,
        "xT": x.T,
        "wqkv": np.concatenate([a(i[f"L0_attn_W{n}"]).T for n in "qkv"], axis=1),
        "bqk": np.stack([a(i["L0_attn_bq"])[:128], a(i["L0_attn_bq"])[128:],
                         a(i["L0_attn_bk"])[:128], a(i["L0_attn_bk"])[128:]], axis=1),
        "bv": a(i["L0_attn_bv"]),
        "w_gate": a(i["L0_ffn_w_gate"]).view(np.int32),
        "w_up": a(i["L0_ffn_w_up"]).view(np.int32),
        "w_down": a(i["L0_ffn_w_down"]).view(np.int32),
        "s_gu": np.stack([a(i["L0_ffn_s_gate"]).reshape(8, 128).T, a(i["L0_ffn_s_up"]).reshape(8, 128).T], axis=1),
        "s_down": a(i["L0_ffn_s_down"]),
        "pos": np.arange(1024, dtype=np.float32).reshape(8, 128).T,
        "inv_freq": a(i["L1_attn_inv_freq"]),
        "l1_wqkv": np.concatenate([a(i[f"L1_attn_w{n}"]).T for n in "qkv"], axis=1),
        "l1_wo": a(i["L1_attn_wo"]).T,
        "router": np.concatenate([a(i["L1_ffn_gate_w"]).T, a(i["L1_ffn_sh_gate1_w"]).T], axis=1),
        "gu": np.concatenate([gate_up, shared], axis=1),
        "dn": np.concatenate([down, a(i["L1_ffn_sh_down_w"]).T, np.zeros((64, 256), np.float32)], axis=0),
        "sel": select.reshape(128, 32 * 128),
        "ident": np.eye(128, dtype=np.float32),
    }
    return {name: np.ascontiguousarray(v) for name, v in out.items()}


def kernel(**inputs):
    import numpy as np
    import concourse.bacc as bacc
    from concourse.bass_utils import run_bass_kernel_spmd

    nc = bacc.Bacc("TRN2", target_bir_lowering=False, num_devices=1)
    arrays, d = {}, {}
    for name, v in layouts(inputs).items():
        arrays[f"in_{name}"] = v
        d[name] = nc.dram_tensor(f"in_{name}", v.shape, mybir.dt.from_np(v.dtype), kind="ExternalInput").ap()
    out = nc.dram_tensor("out", (2048, 256), F32, kind="ExternalOutput").ap()
    build(nc, d, out)
    r = run_bass_kernel_spmd(nc, [arrays], core_ids=[0])
    return np.asarray(r.results[0]["out"]).reshape(2, 1024, 256)
```

```python
from contextlib import ExitStack

import concourse.bass as bass
from concourse import mybir

F32 = mybir.dt.float32
FR = mybir.dt.float32r
BF16 = mybir.dt.bfloat16
I8 = mybir.dt.int8
I32 = mybir.dt.int32
ALU = mybir.AluOpType
ACT = mybir.ActivationFunctionType
AX = mybir.AxisListType

P = 128
EPS = 1e-5


class Core:

    def __init__(self, nc, ctx):
        self.nc, self.ctx = nc, ctx

    def sb(self, name, shape, dt, ctx=None):
        return (ctx or self.ctx).enter_context(self.nc.sbuf_tensor("sb_" + name, shape, dt))

    def sem(self, name, ctx=None):
        return self.ctx.enter_context(self.nc.semaphore(name))


def chained(eng, sem):
    count = [0]

    def link(ins):
        count[0] += 1
        ins.then_inc(sem, 1)
        eng.wait_ge(sem, count[0])

    return link


def stage_l0_project(k, d, XH, XL, X, ident, qh, ql, kh, kl, V):
    nc = k.nc
    H, N = 256, X.shape[1] * P
    KC, NCH, TPC = H // P, N // 512, 4
    with ExitStack() as c:
        xf = k.sb("xf", [P, KC, N], F32, c)
        wf = k.sb("wf", [P, KC, 3 * H], F32, c)
        wh = k.sb("wh", [P, KC, 3 * H], FR, c)
        wl = k.sb("wl", [P, KC, 3 * H], FR, c)
        bqk = k.sb("bqk", [P, 4], F32, c)
        bvb = k.sb("bvb", [P, H], F32, c)
        ps = [c.enter_context(nc.psum_tensor(f"p1_{i}", [P, 512], F32)) for i in range(8)]
        x_in = [k.sem(f"x_in{i}", c) for i in range(NCH)]
        w_in = k.sem("w_in", c)
        misc_in = k.sem("misc_in", c)
        w_hi = k.sem("w_hi", c)
        w_split = k.sem("w_split", c)
        x_hi = k.sem("x_hi", c)
        x_split = k.sem("x_split", c)
        qk_done = k.sem("qk_done", c)
        v_done = k.sem("v_done", c)
        qk_hi = k.sem("qk_hi", c)
        qk_lo = k.sem("qk_lo", c)
        v_out = k.sem("v_out", c)

        with nc.Block() as block:
            @block.sync
            def _(sp):
                sp.dma_start(wf[:], d["wqkv"].rearrange("(c p) n -> p c n", p=P)).then_inc(w_in, 16)
                xt = d["xT"].rearrange("(c p) n -> p c n", p=P)
                for ch in range(NCH):
                    s = slice(512 * ch, 512 * ch + 512)
                    sp.dma_start(xf[:, :, s], xt[:, :, s]).then_inc(x_in[ch], 16)
                sp.dma_start(bqk[:], d["bqk"]).then_inc(misc_in, 16)
                sp.dma_start(bvb[:], d["bv"].partition_broadcast(P)).then_inc(misc_in, 16)
                sp.dma_start(ident[:], d["ident"]).then_inc(misc_in, 16)
                sp.dma_start(X[:], d["x"].rearrange("(t p) n -> p t n", p=P)).then_inc(misc_in, 16)
                sp.wait_ge(misc_in, 64)

            @block.scalar
            def _(act):
                act.wait_ge(w_in, 16)
                nc.scalar.copy(wh[:], wf[:]).then_inc(w_hi, 1)
                for ch in range(NCH):
                    s = slice(512 * ch, 512 * ch + 512)
                    act.wait_ge(x_in[ch], 16)
                    nc.scalar.copy(XH[:, :, s], xf[:, :, s]).then_inc(x_hi, 1)
                act.wait_ge(misc_in, 64)
                for n in range(4 * NCH):
                    ch, which, o = n // 4, (n // 2) % 2, n % 2
                    act.wait_ge(qk_done, n + 1)
                    dst = (qh, kh)[which]
                    nc.scalar.activation(dst[:, o, 512 * ch:512 * ch + 512], ps[n % 4][:], ACT.Identity,
                                         bias=bqk[:, 2 * which + o:2 * which + o + 1]).then_inc(qk_hi, 1)

            @block.vector
            def _(dve):
                dve.wait_ge(w_hi, 1)
                nc.vector.tensor_tensor(wl[:], wf[:], wh[:].bitcast(F32), ALU.subtract).then_inc(w_split, 1)
                for ch in range(NCH):
                    s = slice(512 * ch, 512 * ch + 512)
                    dve.wait_ge(x_hi, ch + 1)
                    nc.vector.tensor_tensor(XL[:, :, s], xf[:, :, s], XH[:, :, s].bitcast(F32),
                                            ALU.subtract).then_inc(x_split, 1)
                dve.wait_ge(misc_in, 64)
                for ch in range(NCH):
                    for j in range(4):
                        n, which, o = 4 * ch + j, j // 2, j % 2
                        hi, lo = ((qh, ql), (kh, kl))[which]
                        s = slice(512 * ch, 512 * ch + 512)
                        dve.wait_ge(qk_hi, n + 1)
                        nc.vector.scalar_tensor_tensor(
                            out=lo[:, o, s], in0=ps[n % 4][:], scalar=bqk[:, 2 * which + o:2 * which + o + 1],
                            in1=hi[:, o, s].bitcast(F32), op0=ALU.add, op1=ALU.subtract).then_inc(qk_lo, 1)
                    for j in range(TPC):
                        t = TPC * ch + j
                        dve.wait_ge(v_done, t + 1)
                        nc.vector.tensor_tensor(V[:, t, :], ps[4 + t % 4][:, 0:H], bvb[:], ALU.add).then_inc(v_out, 1)

            @block.tensor
            def _(pe):
                pe.wait_ge(w_split, 1)
                for ch in range(NCH):
                    pe.wait_ge(x_split, ch + 1)
                    s = slice(512 * ch, 512 * ch + 512)
                    for j in range(4):
                        n, which, o = 4 * ch + j, j // 2, j % 2
                        col = slice(H * which + P * o, H * which + P * o + P)
                        if n >= 4:
                            pe.wait_ge(qk_lo, n - 3)
                        mms = [(w[:, kc, col], x[:, kc, s]) for kc in range(KC)
                               for w, x in ((wh, XH), (wh, XL), (wl, XH))]
                        for i, (l, r) in enumerate(mms):
                            mm = pe.matmul(ps[n % 4][:], l, r, start=i == 0, stop=i == len(mms) - 1)
                        mm.then_inc(qk_done, 1)
                    for j in range(TPC):
                        t = TPC * ch + j
                        if t >= 4:
                            pe.wait_ge(v_out, t - 3)
                        ts = slice(P * t, P * t + P)
                        mms = [(x[:, kc, ts], w[:, kc, 2 * H:3 * H]) for kc in range(KC)
                               for x, w in ((XH, wh), (XL, wh), (XH, wl))]
                        for i, (l, r) in enumerate(mms):
                            mm = pe.matmul(ps[4 + t % 4][:, 0:H], l, r, start=i == 0, stop=i == len(mms) - 1)
                        mm.then_inc(v_done, 1)


class Norm:

    def __init__(self, k, ctx, half, tag):
        self.nc, self.half = k.nc, half
        self.stats = k.sb(tag + "_ln_stats", [P, 6], F32, ctx)
        self.mv = k.sb(tag + "_ln_mv", [P, 2, 2], F32, ctx)
        self.ve = k.sb(tag + "_ln_ve", [P, 1], F32, ctx)
        self.rstd = k.sb(tag + "_ln_rstd", [P, 2, 1], F32, ctx)
        self.var_ready = k.sem(tag + "_ln_var_ready", ctx)
        self.eps_added = k.sem(tag + "_ln_eps_added", ctx)
        self.rstd_ready = k.sem(tag + "_ln_rstd_ready", ctx)

    def statistics(self, n, y, link):
        link(self.nc.vector.bn_stats(self.stats[:], y))
        self.nc.vector.bn_aggr(self.mv[:, n % 2, :], self.stats[:]).then_inc(self.var_ready, 1)

    def power(self, pool, n):
        pool.wait_ge(self.var_ready, n + 1)
        if n >= 1:
            pool.wait_ge(self.rstd_ready, n)
        self.nc.gpsimd.tensor_scalar(self.ve[:], self.mv[:, n % 2, 1:2], EPS, None, ALU.add).then_inc(self.eps_added, 1)
        pool.wait_ge(self.eps_added, n + 1)
        self.nc.gpsimd.tensor_tensor(self.rstd[:, n % 2, :], self.ve[:], self.half[:], ALU.pow).then_inc(self.rstd_ready, 1)

    def scale(self, dve, n, out, y):
        dve.wait_ge(self.rstd_ready, n + 1)
        return self.nc.vector.tensor_scalar(out, y, self.mv[:, n % 2, 0:1], self.rstd[:, n % 2, :],
                                            ALU.subtract, ALU.mult)


def stage_l0_attention(k, XH, XL, X, ident, half, qh, ql, kh, kl, V):
    nc = k.nc
    H, T = 256, X.shape[1]
    S = 1024
    KT = S // P
    with ExitStack() as c:
        prob = k.sb("prob", [P, 2, S], F32, c)
        probT = k.sb("probT", [P, 2, KT, P], F32, c)
        neg_max = k.sb("neg_max", [P, 2, 1], F32, c)
        row_sum = k.sb("row_sum", [P, 2, 1], F32, c)
        inv_sum = k.sb("inv_sum", [P, 1], F32, c)
        y = k.sb("y2", [P, H], F32, c)
        p_s = [c.enter_context(nc.psum_tensor(f"p2_s{i}", [P, S], F32)) for i in range(2)]
        p_t = [c.enter_context(nc.psum_tensor(f"p2_t{i}", [P, 4, P], F32)) for i in range(2)]
        p_o = [c.enter_context(nc.psum_tensor(f"p2_o{i}", [P, 512], F32)) for i in range(2)]
        norm = Norm(k, c, half, "s2")
        scores_ready = k.sem("scores_ready", c)
        max_ready = k.sem("max_ready", c)
        prob_ready = k.sem("prob_ready", c)
        turned = k.sem("turned", c)
        turned_out = [k.sem(f"turned_out{i}", c) for i in range(2)]
        out_ready = k.sem("out_ready", c)
        x_new = k.sem("x_new", c)
        xT_ready = k.sem("xT_ready", c)
        xh_out = k.sem("xh_out", c)
        xl_out = k.sem("xl_out", c)
        v_chain = k.sem("v_chain", c)

        with nc.Block() as block:
            @block.tensor
            def _(pe):
                for t in range(T + 2):
                    if t < T:
                        if t >= 2:
                            pe.wait_ge(prob_ready, t - 1)
                        b, ts = t * P // S, slice(P * t, P * t + P)
                        for half_ in range(2):
                            ks = slice(b * S + 512 * half_, b * S + 512 * half_ + 512)
                            mms = [(q[:, kc, ts], kk[:, kc, ks]) for kc in range(2)
                                   for q, kk in ((qh, kh), (qh, kl), (ql, kh))]
                            for i, (l, r) in enumerate(mms):
                                mm = pe.matmul(p_s[t % 2][:, 512 * half_:512 * half_ + 512], l, r,
                                               start=i == 0, stop=i == len(mms) - 1)
                        mm.then_inc(scores_ready, 1)
                    u = t - 1
                    if 0 <= u < T:
                        pe.wait_ge(prob_ready, u + 1)
                        for h in range(2):
                            if u >= 1:
                                pe.wait_ge(turned_out[h], u)
                            for j in range(4):
                                kt = 4 * h + j
                                mm = pe.transpose(p_t[h][:, j, :], prob[:, u % 2, P * kt:P * kt + P], ident[:])
                            mm.then_inc(turned, 1)
                    w = t - 2
                    if 0 <= w < T:
                        pe.wait_ge(x_new, w + 1)
                        for kc in range(2):
                            mm = pe.transpose(p_o[w % 2][:, H + P * kc:H + P * kc + P], X[:, w, P * kc:P * kc + P], ident[:])
                        mm.then_inc(xT_ready, 1)
                    if 0 <= u < T:
                        pe.wait_ge(turned_out[0], u + 1)
                        pe.wait_ge(turned_out[1], u + 1)
                        if u >= 2:
                            pe.wait_ge(xl_out, u - 1)
                        b = u * P // S
                        for kt in range(KT):
                            mm = pe.matmul(p_o[u % 2][:, 0:H], probT[:, u % 2, kt, :], V[:, b * KT + kt, :],
                                           start=kt == 0, stop=kt == KT - 1)
                        mm.then_inc(out_ready, 1)

            @block.scalar
            def _(act):
                for t in range(T + 2):
                    if t < T:
                        act.wait_ge(max_ready, t + 1)
                        if t >= 2:
                            act.wait_ge(turned, 2 * (t - 1))
                        nc.scalar.activation(prob[:, t % 2, :], p_s[t % 2][:], ACT.Exp, bias=neg_max[:, t % 2, :],
                                             accum_out=row_sum[:, t % 2, :]).then_inc(prob_ready, 1)
                    u = t - 1
                    if 0 <= u < T:
                        act.wait_ge(turned, 2 * u + 1)
                        if u >= 2:
                            act.wait_ge(out_ready, u - 1)
                        nc.scalar.copy(probT[:, u % 2, 0:4, :], p_t[0][:]).then_inc(turned_out[0], 1)
                    w = t - 2
                    if 0 <= w < T:
                        act.wait_ge(xT_ready, w + 1)
                        nc.scalar.copy(XH[:, :, P * w:P * w + P],
                                       p_o[w % 2][:, H:2 * H].rearrange("p (c n) -> p c n", c=2)).then_inc(xh_out, 1)

            @block.vector
            def _(dve):
                link = chained(dve, v_chain)
                for t in range(T + 2):
                    if t < T:
                        dve.wait_ge(scores_ready, t + 1)
                        nc.vector.tensor_reduce(neg_max[:, t % 2, :], p_s[t % 2][:], AX.X, ALU.max,
                                                negate=True).then_inc(max_ready, 1)
                    u = t - 1
                    if 0 <= u < T:
                        dve.wait_ge(turned, 2 * u + 2)
                        if u >= 2:
                            dve.wait_ge(out_ready, u - 1)
                        nc.vector.tensor_copy(probT[:, u % 2, 4:8, :], p_t[1][:]).then_inc(turned_out[1], 1)
                    w = t - 2
                    if 0 <= w < T:
                        dve.wait_ge(xh_out, w + 1)
                        nc.vector.tensor_tensor(XL[:, :, P * w:P * w + P],
                                                p_o[w % 2][:, H:2 * H].rearrange("p (c n) -> p c n", c=2),
                                                XH[:, :, P * w:P * w + P].bitcast(F32), ALU.subtract).then_inc(xl_out, 1)
                    if 0 <= u < T:
                        dve.wait_ge(prob_ready, u + 1)
                        link(nc.vector.reciprocal(inv_sum[:], row_sum[:, u % 2, :]))
                        dve.wait_ge(out_ready, u + 1)
                        link(nc.vector.scalar_tensor_tensor(out=y[:], in0=p_o[u % 2][:, 0:H], scalar=inv_sum[:],
                                                            in1=X[:, u, :], op0=ALU.mult, op1=ALU.add))
                        norm.statistics(u, y[:], link)
                        norm.scale(dve, u, X[:, u, :], y[:]).then_inc(x_new, 1)
                        dve.wait_ge(x_new, u + 1)

            @block.gpsimd
            def _(pool):
                for u in range(T):
                    norm.power(pool, u)


def stage_ffn(k, d, XH, XL, X, ident, half):
    nc = k.nc
    H, IT, T = 256, 8, X.shape[1]
    I = IT * P
    NCH = T // 4
    with ExitStack() as c:
        wg8 = k.sb("wg8", [P, 2, I // 4], I32, c)
        wu8 = k.sb("wu8", [P, 2, I // 4], I32, c)
        wd8 = k.sb("wd8", [P, IT, H // 4], I32, c)
        wg = k.sb("wg", [P, 2, I], FR, c)
        wu = k.sb("wu", [P, 2, I], FR, c)
        wd = k.sb("wd", [P, IT, H], FR, c)
        s_gu = k.sb("s_gu", [P, 2, IT], F32, c)
        s_down = k.sb("s_down", [P, H], F32, c)
        gated = k.sb("gated", [P, 2, 512], F32, c)
        fuse = k.sb("fuse", [P, 2, 512], F32, c)
        fh = k.sb("fh", [P, 2, IT, 512], FR, c)
        fl = k.sb("fl", [P, 2, IT, 512], FR, c)
        y = k.sb("y3", [P, 2, H], F32, c)
        p_g = [c.enter_context(nc.psum_tensor(f"p3_g{i}", [P, 512], F32)) for i in range(2)]
        p_u = [c.enter_context(nc.psum_tensor(f"p3_u{i}", [P, 512], F32)) for i in range(2)]
        p_d = [c.enter_context(nc.psum_tensor(f"p3_d{i}", [P, 512], F32)) for i in range(2)]
        p_x = [c.enter_context(nc.psum_tensor(f"p3_x{i}", [P, 4, P], F32)) for i in range(2)]
        norm = Norm(k, c, half, "s3")
        wg_in, wu_in, wd_in, s_in = (k.sem(n, c) for n in ("wg_in", "wu_in", "wd_in", "s_in"))
        wg_cast, wu_cast, wd_cast = (k.sem(n, c) for n in ("wg_cast", "wu_cast", "wd_cast"))
        gate_ready, up_ready = k.sem("gate_ready", c), k.sem("up_ready", c)
        gated_ready, fuse_ready = k.sem("gated_ready", c), k.sem("fuse_ready", c)
        fh_ready, fl_ready = k.sem("fh_ready", c), k.sem("fl_ready", c)
        down_ready, scaled = k.sem("down_ready", c), k.sem("scaled", c)
        x_new, xT_ready, xh_out, xl_out = (k.sem(n, c) for n in ("x_new3", "xT_ready3", "xh_out3", "xl_out3"))
        v_chain = k.sem("v_chain3", c)

        def turned_after(m):
            return down_after(m - 2)

        def down_after(m):
            ch, i = divmod(m, IT)
            return [4 * (ch - 1) + (i - 1) // 2] if m >= 0 and ch >= 1 and i % 2 == 1 and ch < NCH else []

        with nc.Block() as block:
            @block.sync
            def _(sp):
                sp.dma_start(wg8[:], d["w_gate"].rearrange("(c p) n -> p c n", p=P)).then_inc(wg_in, 16)
                sp.dma_start(wu8[:], d["w_up"].rearrange("(c p) n -> p c n", p=P)).then_inc(wu_in, 16)
                sp.dma_start(s_gu[:], d["s_gu"]).then_inc(s_in, 16)
                sp.dma_start(s_down[:], d["s_down"].partition_broadcast(P)).then_inc(s_in, 16)
                sp.dma_start(wd8[:], d["w_down"].rearrange("(c p) n -> p c n", p=P)).then_inc(wd_in, 16)
                sp.wait_ge(wd_in, 16)

            @block.scalar
            def _(act):
                act.wait_ge(wg_in, 16)
                nc.scalar.copy(wg[:], wg8[:].bitcast(I8)).then_inc(wg_cast, 1)
                act.wait_ge(s_in, 32)
                for n in range(NCH * IT + 1):
                    if n == 1:
                        act.wait_ge(wd_in, 16)
                        nc.scalar.copy(wd[:], wd8[:].bitcast(I8)).then_inc(wd_cast, 1)
                    if n < NCH * IT:
                        i = n % IT
                        act.wait_ge(gate_ready, n + 1)
                        if n >= 2:
                            act.wait_ge(fuse_ready, n - 1)
                        nc.scalar.activation(gated[:, n % 2, :], p_g[n % 2][:], ACT.Silu,
                                             scale=s_gu[:, 0, i:i + 1]).then_inc(gated_ready, 1)
                    m = n - 1
                    if m >= 0:
                        ch, i = m // IT, m % IT
                        act.wait_ge(fuse_ready, m + 1)
                        if ch >= 2:
                            act.wait_ge(down_ready, 4 * (ch - 1))
                        nc.scalar.copy(fh[:, ch % 2, i, :], fuse[:, m % 2, :]).then_inc(fh_ready, 1)
                        for w in turned_after(m - 1):
                            act.wait_ge(xT_ready, w + 1)
                            nc.scalar.copy(XH[:, :, P * w:P * w + P], p_x[w % 2][:, 0:2, :]).then_inc(xh_out, 1)
                for w in range(T - 6, T):
                    act.wait_ge(xT_ready, w + 1)
                    nc.scalar.copy(XH[:, :, P * w:P * w + P], p_x[w % 2][:, 0:2, :]).then_inc(xh_out, 1)

            @block.vector
            def _(dve):
                link = chained(dve, v_chain)
                dve.wait_ge(wu_in, 16)
                nc.vector.tensor_copy(wu[:], wu8[:].bitcast(I8)).then_inc(wu_cast, 1)
                dve.wait_ge(s_in, 32)

                def low_x(w):
                    dve.wait_ge(xh_out, w + 1)
                    nc.vector.tensor_tensor(XL[:, :, P * w:P * w + P], p_x[w % 2][:, 0:2, :],
                                            XH[:, :, P * w:P * w + P].bitcast(F32), ALU.subtract).then_inc(xl_out, 1)

                def finish(t):
                    dve.wait_ge(down_ready, t + 1)
                    nc.vector.tensor_tensor(y[:, t % 2, :], p_d[t % 2][:, 0:H], s_down[:], ALU.mult).then_inc(scaled, 1)
                    dve.wait_ge(scaled, t + 1)
                    link(nc.vector.tensor_tensor(y[:, t % 2, :], y[:, t % 2, :], X[:, t, :], ALU.add))
                    norm.statistics(t, y[:, t % 2, :], link)
                    norm.scale(dve, t, X[:, t, :], y[:, t % 2, :]).then_inc(x_new, 1)

                for m in range(NCH * IT):
                    ch, i = divmod(m, IT)
                    dve.wait_ge(gated_ready, m + 1)
                    dve.wait_ge(up_ready, m + 1)
                    if m >= 2:
                        dve.wait_ge(fh_ready, m - 1)
                        dve.wait_ge(fl_ready, m - 1)
                    nc.vector.scalar_tensor_tensor(out=fuse[:, m % 2, :], in0=p_u[m % 2][:], scalar=s_gu[:, 1, i:i + 1],
                                                   in1=gated[:, m % 2, :], op0=ALU.mult, op1=ALU.mult).then_inc(fuse_ready, 1)
                    for w in turned_after(m - 1):
                        low_x(w)
                    for t in down_after(m - 1):
                        finish(t)
                low_x(T - 6)
                finish(T - 5)
                finish(T - 4)
                low_x(T - 5)
                for t in range(T - 3, T):
                    finish(t)
                    low_x(t - 1)
                low_x(T - 1)

            @block.gpsimd
            def _(pool):
                for m in range(NCH * IT):
                    ch, i = divmod(m, IT)
                    for t in down_after(m - 1):
                        norm.power(pool, t)
                    pool.wait_ge(fh_ready, m + 1)
                    if ch >= 2:
                        pool.wait_ge(down_ready, 4 * (ch - 1))
                    nc.gpsimd.tensor_tensor(fl[:, ch % 2, i, :], fuse[:, m % 2, :], fh[:, ch % 2, i, :].bitcast(F32),
                                            ALU.subtract).then_inc(fl_ready, 1)
                for t in range(T - 5, T):
                    norm.power(pool, t)

            @block.tensor
            def _(pe):
                def down(t):
                    ch, tt = divmod(t, 4)
                    pe.wait_ge(fl_ready, IT * (ch + 1))
                    if t == 0:
                        pe.wait_ge(wd_cast, 1)
                    if t >= 2:
                        pe.wait_ge(scaled, t - 1)
                    n = 0
                    for i in range(IT):
                        for part in (fh, fl):
                            mm = pe.matmul(p_d[t % 2][:, 0:H], part[:, ch % 2, i, P * tt:P * tt + P], wd[:, i, :],
                                           start=n == 0, stop=n == 2 * IT - 1)
                            n += 1
                    mm.then_inc(down_ready, 1)

                def turn(w):
                    pe.wait_ge(x_new, w + 1)
                    if w >= 2:
                        pe.wait_ge(xl_out, w - 1)
                    for kc in range(2):
                        mm = pe.transpose(p_x[w % 2][:, kc, :], X[:, w, P * kc:P * kc + P], ident[:])
                    mm.then_inc(xT_ready, 1)

                pe.wait_ge(wg_cast, 1)
                for m in range(NCH * IT):
                    ch, i = divmod(m, IT)
                    s = slice(512 * ch, 512 * ch + 512)
                    for dst, w, done, freed, cast in ((p_g, wg, gate_ready, gated_ready, wg_cast),
                                                      (p_u, wu, up_ready, fuse_ready, wu_cast)):
                        if m == 0:
                            pe.wait_ge(cast, 1)
                        if m >= 2:
                            pe.wait_ge(freed, m - 1)
                        mms = [(w[:, kc, P * i:P * i + P], x[:, kc, s]) for kc in range(2) for x in (XH, XL)]
                        for j, (l, r) in enumerate(mms):
                            mm = pe.matmul(dst[m % 2][:], l, r, start=j == 0, stop=j == len(mms) - 1)
                        mm.then_inc(done, 1)
                    for w_ in turned_after(m):
                        turn(w_)
                    for t in down_after(m):
                        down(t)
                down(T - 4)
                turn(T - 5)
                for t in range(T - 3, T):
                    down(t)
                    turn(t - 1)
                turn(T - 1)


HEADS, HD = 16, 16
TWO_PI = 6.283185307179586
TURN_PARTS = (6.28125, 0.001934051513671875, 1.255422830581665e-06, 2.430840251310684e-10)
ROUND = 12582912.0
HI0, MID1, Q_HI2, Q_MID4, Q_LO5 = 0, 1, 2, 4, 5
MAX_ROW, STACK_ROWS = 96, 99


def stage_l1_prepare(k, d, cos, sin, wh, wl, woh, wol, rh, rl):
    nc = k.nc
    ST = cos.shape[1]
    parts = TURN_PARTS
    with ExitStack() as c:
        wf = k.sb("l1_wf", [P, 2, 768], F32, c)
        wof = k.sb("l1_wof", [P, 2, 256], F32, c)
        rf = k.sb("router_f", [P, 2, 65], F32, c)
        pos = k.sb("pos", [P, ST], F32, c)
        freq = k.sb("freq", [P, 8], F32, c)
        ang = k.sb("ang", [P, ST, 8], F32, c)
        turns = k.sb("turns", [P, ST, 8], F32, c)
        over = k.sb("over", [P, ST, 8], F32, c)
        shifted = k.sb("shifted", [P, ST, 8], F32, c)
        w_in, hi_ready, small_in = k.sem("l1w_in"), k.sem("l1w_hi"), k.sem("l1_small_in")
        lo_ready, v_chain, reduced = k.sem("l1w_lo"), k.sem("v_chain4"), k.sem("angles_reduced")
        with nc.Block() as block:
            @block.sync
            def _(sp):
                sp.dma_start(pos[:], d["pos"]).then_inc(small_in, 16)
                sp.dma_start(freq[:], d["inv_freq"].partition_broadcast(P)).then_inc(small_in, 16)
                sp.dma_start(wf[:], d["l1_wqkv"].rearrange("(c p) n -> p c n", p=P)).then_inc(w_in, 16)
                sp.dma_start(wof[:], d["l1_wo"].rearrange("(c p) n -> p c n", p=P)).then_inc(w_in, 16)
                sp.dma_start(rf[:], d["router"].rearrange("(c p) n -> p c n", p=P)).then_inc(w_in, 16)
                sp.wait_ge(w_in, 48)

            @block.scalar
            def _(act):
                act.wait_ge(w_in, 48)
                nc.scalar.copy(rh[:, :, 0:65], rf[:]).then_inc(hi_ready, 1)
                nc.scalar.copy(wh[:], wf[:]).then_inc(hi_ready, 1)
                nc.scalar.copy(woh[:], wof[:]).then_inc(hi_ready, 1)
                act.wait_ge(reduced, 2)
                nc.scalar.activation(sin[:], ang[:], ACT.Sin)
                nc.scalar.activation(cos[:], shifted[:], ACT.Sin)

            @block.vector
            def _(dve):
                link = chained(dve, v_chain)
                dve.wait_ge(small_in, 32)
                link(nc.vector.tensor_tensor(ang[:], pos[:].unsqueeze(2).broadcast_to([P, ST, 8]),
                                             freq[:].unsqueeze(1).broadcast_to([P, ST, 8]), ALU.mult))
                link(nc.vector.tensor_scalar(turns[:], ang[:], 1.0 / TWO_PI, None, ALU.mult))
                link(nc.vector.tensor_scalar(turns[:], turns[:], ROUND, None, ALU.add))
                link(nc.vector.tensor_scalar(turns[:], turns[:], -ROUND, None, ALU.add))
                for part in parts:
                    if part:
                        link(nc.vector.scalar_tensor_tensor(out=ang[:], in0=turns[:], scalar=-part, in1=ang[:],
                                                            op0=ALU.mult, op1=ALU.add))
                link(nc.vector.tensor_scalar(shifted[:], ang[:], TWO_PI / 4, None, ALU.add))
                link(nc.vector.tensor_scalar(over[:], shifted[:], TWO_PI / 2, -TWO_PI, ALU.is_gt, ALU.mult))
                link(nc.vector.tensor_tensor(shifted[:], shifted[:], over[:], ALU.add))
                for x in (ang, shifted):
                    nc.vector.tensor_scalar(x[:], x[:], 3.1415925, -3.1415925, ALU.min, ALU.max).then_inc(reduced, 1)
                nc.vector.memset(rh[:, :, 65:66].bitcast(F32), 0.0)
                nc.vector.memset(rl[:, :, 65:66].bitcast(F32), 0.0)
                dve.wait_ge(hi_ready, 3)
                nc.vector.tensor_tensor(rl[:, :, 0:65], rf[:], rh[:, :, 0:65].bitcast(F32), ALU.subtract).then_inc(lo_ready, 1)
                nc.vector.tensor_tensor(wl[:], wf[:], wh[:].bitcast(F32), ALU.subtract).then_inc(lo_ready, 1)
                nc.vector.tensor_tensor(wol[:], wof[:], woh[:].bitcast(F32), ALU.subtract).then_inc(lo_ready, 1)


EXPERTS, TOP = 64, 8
PAIRS = EXPERTS // 2
LOWEST = -3.0e38
TILE_SLOTS = 6
TILE_LEN, ROUTE_LEN = 26, 7


def slots_of(T):
    starts = [TILE_SLOTS * t for t in range(T)]
    return starts, [starts[4 * c + 3] + TILE_LEN + ROUTE_LEN for c in range(T // 4)]


class Heads:

    DVE_HEADS = 4

    def __init__(self, k, c, d, XH, XL, X, ident, half, cos, sin, wh, wl, woh, wol, rh, rl, WT, WS, banks):
        nc = k.nc
        self.nc, self.X, self.XH, self.XL, self.ident = nc, X, XH, XL, ident
        self.cos, self.sin, self.wh, self.wl, self.woh, self.wol, self.rh, self.rl = cos, sin, wh, wl, woh, wol, rh, rl
        self.WT, self.WS = WT, WS
        self.T, self.ST = X.shape[1], cos.shape[1]
        self.starts, _ = slots_of(self.T)
        self.slots = {s + r: [] for s in self.starts for r in range(TILE_LEN + ROUTE_LEN + 1)}
        self.norm = Norm(k, c, half, "s5")
        b = lambda n, shape, dt=F32: k.sb(n, shape, dt, c)
        self.rt = b("rope_t", [P, 4, 2 * HEADS, 8])
        self.rope = b("rope", [P, 2 * HEADS, HD])
        self.v = b("v5", [P, 2, HEADS, HD])
        self.prod = b("prod", [P, HEADS, HEADS, HD])
        self.score = b("score", [P, HEADS, HEADS])
        self.nmax = b("nmax", [P, HEADS])
        self.shifted = b("shifted5", [P, HEADS, HEADS])
        self.prob = b("prob5", [P, HEADS, HEADS])
        self.total = b("total5", [P, HEADS])
        self.inv = b("inv5", [P, HEADS])
        self.pv = b("pv", [P, HEADS, HEADS, HD])
        self.a = b("a5", [P, HEADS, HD])
        self.ah = b("ah", [P, 2, P], FR)
        self.al = b("al", [P, 2, P], FR)
        self.y = b("y5", [P, 256])
        self.logit = b("logit", [P, 4, EXPERTS + 1])
        self.left = b("left", [P, 4, EXPERTS])
        self.best = b("best", [P, 4, TOP])
        self.chosen = b("chosen", [P, 4, EXPERTS])
        self.weight = b("weight", [P, 4, EXPERTS])
        self.expw = b("expw", [P, 4, EXPERTS])
        self.wtotal = b("wtotal", [P, 4])
        self.winv = b("winv", [P, 4])
        self.sig = b("sig", [P, 4])
        self.wn = b("wn", [P, 4, 2 * EXPERTS], FR)
        self.sn = b("sn", [P, 4, 2], FR)
        self.bank = dict(zip(("qk", "o", "v", "aT", "wT", "xT", "logit", "sT"),
                             (banks[i] for i in (0, 0, 1, 1, 2, 2, 2, 0)), strict=True))
        self.bank_no = {"qk": 0, "o": 0, "v": 1, "aT": 1, "wT": 2, "xT": 2, "logit": 2, "sT": 0}
        self.qk_ready = k.sem("qk_ready_h")
        self.v_ready = k.sem("v_ready_h")
        self.v_out = k.sem("v_out_h")
        self.rotated = k.sem("rotated_h")
        self.roped = k.sem("roped_h")
        self.prod_pool = k.sem("prod_pool_h")
        self.prod_dve = k.sem("prod_dve_h")
        self.summed_score = k.sem("summed_score_h")
        self.lowered = k.sem("lowered_h")
        self.prob_ready = k.sem("prob_ready_h")
        self.pv_pool = k.sem("pv_pool_h")
        self.pv_dve = k.sem("pv_dve_h")
        self.pv_added = k.sem("pv_added_h")
        self.a_ready = k.sem("a_ready_h")
        self.aT_ready = k.sem("aT_ready_h")
        self.ah_ready = k.sem("ah_ready_h")
        self.al_ready = k.sem("al_ready_h")
        self.o_ready = k.sem("o_ready_h")
        self.residual = k.sem("residual_h")
        self.x_new = k.sem("x_new_h")
        self.xT_ready = k.sem("xT_ready_h")
        self.xh_out = k.sem("xh_out_h")
        self.xl_out = k.sem("xl_out_h")
        self.l_ready = k.sem("l_ready_h")
        self.l_out = k.sem("l_out_h")
        self.best_ready = k.sem("best_ready_h")
        self.replaced = k.sem("replaced_h")
        self.w_lowered = k.sem("w_lowered_h")
        self.exp_ready = k.sem("exp_ready_h")
        self.w_split = k.sem("w_split_h")
        self.w_turned = k.sem("w_turned_h")
        self.s_turned = k.sem("s_turned_h")
        self.w_out = k.sem("w_out_h")
        self.s_out = k.sem("s_out_h")
        self.v_chain = k.sem("v_chain_h")
        self.order = self._bank_order()

    def _bank_order(self):
        uses = {0: [], 1: [], 2: []}
        for t, s in enumerate(self.starts):
            for kind, r, place in (("qk", 0, 0), ("v", 0, 1), ("aT", 14, 2), ("o", 17, 3), ("xT", 20, 4), ("logit", 23, 5)):
                uses[self.bank_no[kind]].append((s + r, place, kind, t))
            if t % 4 == 3:
                for kind, r in (("wT", 5), ("sT", 6)):
                    uses[self.bank_no[kind]].append((s + TILE_LEN + r, 6, kind, t // 4))
        before = {}
        for lst in uses.values():
            lst.sort()
            for i, (_, _, kind, t) in enumerate(lst):
                before[kind, t] = lst[i - 1][2:] if i else None
        return before

    def wait_bank(self, pe, kind, t):
        prev = self.order[kind, t]
        if prev is None:
            return
        what, u = prev
        sem, per = {"qk": (self.rotated, 4), "v": (self.v_out, 1), "aT": (self.al_ready, 1), "o": (self.residual, 1),
                    "xT": (self.xl_out, 1), "logit": (self.l_out, 1), "wT": (self.w_out, 1), "sT": (self.s_out, 1)}[what]
        pe.wait_ge(sem, per * (u + 1))

    def at(self, slot):
        tiles = [(t, slot - s) for t, s in enumerate(self.starts) if 0 <= slot - s < TILE_LEN]
        chunks = [(t // 4, slot - s - TILE_LEN) for t, s in enumerate(self.starts)
                  if t % 4 == 3 and 0 <= slot - s - TILE_LEN < ROUTE_LEN]
        return tiles, chunks

    def pe(self, pe, slot):
        tiles, chunks = self.at(slot)
        steps = {0: self._project, 14: self._turn_a, 17: self._output, 20: self._turn_x, 23: self._logits}
        for r in (0, 14, 17, 20, 23):
            for t, rr in tiles:
                if rr == r:
                    steps[r](pe, t)
        for ch, r in chunks:
            if r == 5:
                pe.wait_ge(self.w_split, 4 * (ch + 1))
                self.wait_bank(pe, "wT", ch)
                for j in range(4):
                    mm = pe.transpose(self.bank["wT"][:, P * j:P * j + P], self.wn[:, j, :].bitcast(F32), self.ident[:])
                mm.then_inc(self.w_turned, 1)
            if r == 6:
                pe.wait_ge(self.w_split, 4 * (ch + 1))
                self.wait_bank(pe, "sT", ch)
                for j in range(4):
                    mm = pe.transpose(self.bank["sT"][0:2, P * j:P * j + P], self.sn[:, j, :].bitcast(F32), self.ident[:])
                mm.then_inc(self.s_turned, 1)

    def _project(self, pe, t):
        ts = slice(P * t, P * t + P)
        mms = [(x, w, kc) for kc in range(2) for x, w in ((self.XH, self.wh), (self.XL, self.wh), (self.XH, self.wl))]
        for kind, cols, width, done in (("qk", slice(0, 512), 512, self.qk_ready), ("v", slice(512, 768), 256, self.v_ready)):
            self.wait_bank(pe, kind, t)
            for n, (x, w, kc) in enumerate(mms):
                mm = pe.matmul(self.bank[kind][:, 0:width], x[:, kc, ts], w[:, kc, cols], start=n == 0, stop=n == 5)
            mm.then_inc(done, 1)

    def _turn_a(self, pe, t):
        pe.wait_ge(self.a_ready, t + 1)
        self.wait_bank(pe, "aT", t)
        for kc in range(2):
            mm = pe.transpose(self.bank["aT"][:, P * kc:P * kc + P],
                              self.a[:, 8 * kc:8 * kc + 8, :].rearrange("p h n -> p (h n)"), self.ident[:])
        mm.then_inc(self.aT_ready, 1)

    def _output(self, pe, t):
        pe.wait_ge(self.al_ready, t + 1)
        self.wait_bank(pe, "o", t)
        mms = [(x, w, kc) for kc in range(2) for x, w in ((self.ah, self.woh), (self.al, self.woh), (self.ah, self.wol))]
        for n, (x, w, kc) in enumerate(mms):
            mm = pe.matmul(self.bank["o"][:, 0:256], x[:, kc, :], w[:, kc, :], start=n == 0, stop=n == 5)
        mm.then_inc(self.o_ready, 1)

    def _turn_x(self, pe, t):
        pe.wait_ge(self.x_new, t + 1)
        self.wait_bank(pe, "xT", t)
        for kc in range(2):
            mm = pe.transpose(self.bank["xT"][:, P * kc:P * kc + P], self.X[:, t, P * kc:P * kc + P], self.ident[:])
        mm.then_inc(self.xT_ready, 1)

    def _logits(self, pe, t):
        pe.wait_ge(self.xl_out, t + 1)
        self.wait_bank(pe, "logit", t)
        mms = [(x, w, kc) for kc in range(2) for x, w in ((self.XH, self.rh), (self.XL, self.rh), (self.XH, self.rl))]
        for n, (x, w, kc) in enumerate(mms):
            mm = pe.matmul(self.bank["logit"][:, 0:EXPERTS + 2], x[:, kc, P * t:P * t + P], w[:, kc, :],
                           start=n == 0, stop=n == 5)
        mm.then_inc(self.l_ready, 1)

    def act(self, act, slot):
        nc = self.nc
        tiles, chunks = self.at(slot)
        for t, r in tiles:
            if r == 1:
                act.wait_ge(self.v_ready, t + 1)
                if t >= 2:
                    act.wait_ge(self.pv_pool, 3 * (t - 1))
                    act.wait_ge(self.pv_dve, t - 1)
                nc.scalar.copy(self.v[:, t % 2], self.bank["v"][:, 0:256].rearrange("p (h n) -> p h n", h=HEADS)).then_inc(self.v_out, 1)
            if r == 7:
                act.wait_ge(self.lowered, t + 1)
                if t >= 1:
                    act.wait_ge(self.pv_pool, 3 * t)
                    act.wait_ge(self.a_ready, t)
                nc.scalar.activation(self.prob[:], self.shifted[:], ACT.Exp, scale=HD ** -0.5).then_inc(self.prob_ready, 1)
            if r == 15:
                act.wait_ge(self.aT_ready, t + 1)
                if t >= 1:
                    act.wait_ge(self.o_ready, t)
                nc.scalar.copy(self.ah[:], self.bank["aT"][:, 0:256].rearrange("p (c n) -> p c n", c=2)).then_inc(self.ah_ready, 1)
            if r == 21:
                act.wait_ge(self.xT_ready, t + 1)
                nc.scalar.copy(self.XH[:, :, P * t:P * t + P],
                               self.bank["xT"][:, 0:256].rearrange("p (c n) -> p c n", c=2)).then_inc(self.xh_out, 1)
            if r == 24:
                act.wait_ge(self.l_ready, t + 1)
                if t >= 4 and t % 4 == 0:
                    act.wait_ge(self.w_split, t)
                nc.scalar.copy(self.logit[:, t % 4, :], self.bank["logit"][:, 0:EXPERTS + 1]).then_inc(self.l_out, 1)
        for ch, r in chunks:
            if r == 1:
                act.wait_ge(self.w_lowered, ch + 1)
                act.wait_ge(self.l_out, 4 * (ch + 1))
                nc.scalar.activation(self.expw[:], self.weight[:], ACT.Exp).then_inc(self.exp_ready, 1)
                nc.scalar.activation(self.sig[:], self.logit[:, :, EXPERTS], ACT.Exp, scale=-1.0).then_inc(self.exp_ready, 1)
            cols = slice(512 * ch, 512 * ch + 512)
            if r == 5:
                act.wait_ge(self.w_turned, ch + 1)
                nc.scalar.copy(self.WT[:, cols], self.bank["wT"][:]).then_inc(self.w_out, 1)
            if r == 6:
                act.wait_ge(self.s_turned, ch + 1)
                nc.scalar.copy(self.WS[:, cols], self.bank["sT"][0:2, :]).then_inc(self.s_out, 1)

    def _score_product(self, eng, lo, hi):
        shape = [P, hi - lo, HEADS, HD]
        return eng.tensor_tensor(self.prod[:, lo:hi], self.rope[:, lo:hi, :].unsqueeze(2).broadcast_to(shape),
                                 self.rope[:, HEADS:2 * HEADS, :].unsqueeze(1).broadcast_to(shape), ALU.mult)

    def _value_product(self, eng, t, lo, hi):
        shape = [P, hi - lo, HEADS, HD]
        return eng.tensor_tensor(self.pv[:, lo:hi], self.v[:, t % 2, lo:hi, :].unsqueeze(2).broadcast_to(shape),
                                 self.prob[:, :, lo:hi].rearrange("p h t -> p t h").unsqueeze(3).broadcast_to(shape), ALU.mult)

    def pool(self, pool, slot):
        tiles, _ = self.at(slot)
        for t, r in tiles:
            if r in (3, 4, 5):
                i = r - 3
                if i == 0:
                    pool.wait_ge(self.roped, 2 * (t + 1))
                if t >= 1:
                    pool.wait_ge(self.summed_score, 4 * (t - 1) + 2 + i)
                self._score_product(self.nc.gpsimd, 4 * i, 4 * i + 4).then_inc(self.prod_pool, 1)
            if r in (8, 9, 10):
                i = r - 8
                if i == 0:
                    pool.wait_ge(self.prob_ready, t + 1)
                    pool.wait_ge(self.v_out, t + 1)
                if t >= 1:
                    pool.wait_ge(self.pv_added, 3 * (t - 1) + i + 1)
                self._value_product(self.nc.gpsimd, t, 4 * i, 4 * i + 4).then_inc(self.pv_pool, 1)
            if r == 18:
                self.norm.power(pool, t)

    def start_vector(self, dve):
        self.link = chained(dve, self.v_chain)

    def dve(self, dve, slot):
        nc, link = self.nc, self.link
        tiles, chunks = self.at(slot)
        for t, r in tiles:
            if r == 1:
                dve.wait_ge(self.qk_ready, t + 1)
                if t >= 1:
                    dve.wait_ge(self.roped, 2 * t)
                qk = self.bank["qk"][:].rearrange("p (h n two) -> p h n two", n=8, two=2)
                cb = self.cos[:, t % self.ST, :].unsqueeze(1).broadcast_to([P, 2 * HEADS, 8])
                sb = self.sin[:, t % self.ST, :].unsqueeze(1).broadcast_to([P, 2 * HEADS, 8])
                for m, (x, f) in enumerate(((0, cb), (1, sb), (0, sb), (1, cb))):
                    nc.vector.tensor_tensor(self.rt[:, m], qk[:, :, :, x], f, ALU.mult).then_inc(self.rotated, 1)
            if r == 2:
                dve.wait_ge(self.rotated, 4 * (t + 1))
                if t >= 1:
                    dve.wait_ge(self.prod_pool, 3 * t)
                    dve.wait_ge(self.prod_dve, t)
                nc.vector.tensor_tensor(self.rope[:, :, 0:8], self.rt[:, 0], self.rt[:, 1], ALU.subtract).then_inc(self.roped, 1)
                nc.vector.tensor_tensor(self.rope[:, :, 8:16], self.rt[:, 2], self.rt[:, 3], ALU.add).then_inc(self.roped, 1)
                dve.wait_ge(self.roped, 2 * (t + 1))
                if t >= 1:
                    dve.wait_ge(self.summed_score, 4 * (t - 1) + 1)
                self._score_product(nc.vector, 12, 16).then_inc(self.prod_dve, 1)
            if r in (3, 4, 5, 6):
                i = r - 4
                if r == 3:
                    dve.wait_ge(self.prod_dve, t + 1)
                    if t >= 1:
                        dve.wait_ge(self.lowered, t)
                else:
                    dve.wait_ge(self.prod_pool, 3 * t + i + 1)
                h = slice(12, 16) if r == 3 else slice(4 * i, 4 * i + 4)
                nc.vector.tensor_reduce(self.score[:, h], self.prod[:, h], AX.X, ALU.add).then_inc(self.summed_score, 1)
            if r == 7:
                dve.wait_ge(self.summed_score, 4 * (t + 1))
                link(nc.vector.tensor_reduce(self.nmax[:], self.score[:], AX.X, ALU.max, negate=True))
                if t >= 1:
                    dve.wait_ge(self.prob_ready, t)
                nc.vector.tensor_tensor(self.shifted[:], self.score[:], self.nmax[:].unsqueeze(2).broadcast_to([P, HEADS, HEADS]),
                                        ALU.add).then_inc(self.lowered, 1)
            if r == 8:
                dve.wait_ge(self.prob_ready, t + 1)
                dve.wait_ge(self.v_out, t + 1)
                self._value_product(nc.vector, t, 12, 16).then_inc(self.pv_dve, 1)
                link(nc.vector.tensor_reduce(self.total[:], self.prob[:], AX.X, ALU.add))
                link(nc.vector.reciprocal(self.inv[:], self.total[:]))
            if r in (10, 11, 12):
                i = r - 10
                dve.wait_ge(self.pv_pool, 3 * t + i + 1)
                dve.wait_ge(self.pv_dve, t + 1)
                if i:
                    dve.wait_ge(self.pv_added, 3 * t + i)
                nc.vector.tensor_tensor(self.pv[:, 12:16], self.pv[:, 12:16], self.pv[:, 4 * i:4 * i + 4], ALU.add).then_inc(self.pv_added, 1)
            if r == 13:
                dve.wait_ge(self.pv_added, 3 * (t + 1))
                link(nc.vector.tensor_tensor(self.pv[:, 12:14], self.pv[:, 12:14], self.pv[:, 14:16], ALU.add))
                link(nc.vector.tensor_tensor(self.pv[:, 12], self.pv[:, 12], self.pv[:, 13], ALU.add))
                if t >= 1:
                    dve.wait_ge(self.aT_ready, t)
                nc.vector.tensor_tensor(self.a[:], self.pv[:, 12], self.inv[:].unsqueeze(2).broadcast_to([P, HEADS, HD]),
                                        ALU.mult).then_inc(self.a_ready, 1)
            if r == 16:
                dve.wait_ge(self.ah_ready, t + 1)
                if t >= 1:
                    dve.wait_ge(self.o_ready, t)
                nc.vector.tensor_tensor(self.al[:], self.bank["aT"][:, 0:256].rearrange("p (c n) -> p c n", c=2),
                                        self.ah[:].bitcast(F32), ALU.subtract).then_inc(self.al_ready, 1)
            if r == 18:
                dve.wait_ge(self.o_ready, t + 1)
                if t >= 1:
                    dve.wait_ge(self.x_new, t)
                nc.vector.tensor_tensor(self.y[:], self.bank["o"][:, 0:256], self.X[:, t, :], ALU.add).then_inc(self.residual, 1)
                dve.wait_ge(self.residual, t + 1)
                self.norm.statistics(t, self.y[:], link)
            if r == 19:
                self.norm.scale(dve, t, self.X[:, t, :], self.y[:]).then_inc(self.x_new, 1)
            if r == 22:
                dve.wait_ge(self.xh_out, t + 1)
                nc.vector.tensor_tensor(self.XL[:, :, P * t:P * t + P], self.bank["xT"][:, 0:256].rearrange("p (c n) -> p c n", c=2),
                                        self.XH[:, :, P * t:P * t + P].bitcast(F32), ALU.subtract).then_inc(self.xl_out, 1)
            if r == 25:
                j = t % 4
                dve.wait_ge(self.l_out, t + 1)
                nc.vector.max(self.best[:, j, :], self.logit[:, j, 0:EXPERTS]).then_inc(self.best_ready, 1)
                dve.wait_ge(self.best_ready, t + 1)
                nc.vector.match_replace(self.left[:, j, :], self.best[:, j, :], self.logit[:, j, 0:EXPERTS], LOWEST).then_inc(self.replaced, 1)
        wide = lambda x: x.unsqueeze(2).broadcast_to([P, 4, EXPERTS])
        for ch, r in chunks:
            if r == 0:
                dve.wait_ge(self.replaced, 4 * (ch + 1))
                nc.vector.tensor_tensor(self.weight[:], self.logit[:, :, 0:EXPERTS], wide(self.best[:, :, 0]),
                                        ALU.subtract).then_inc(self.w_lowered, 1)
                link(nc.vector.tensor_tensor(self.chosen[:], self.left[:], self.logit[:, :, 0:EXPERTS], ALU.not_equal))
            if r == 2:
                dve.wait_ge(self.exp_ready, 2 * (ch + 1))
                if ch:
                    dve.wait_ge(self.w_turned, ch)
                    dve.wait_ge(self.s_turned, ch)
                link(nc.vector.tensor_tensor(self.weight[:], self.expw[:], self.chosen[:], ALU.mult))
                link(nc.vector.tensor_reduce(self.wtotal[:], self.weight[:], AX.X, ALU.add))
                link(nc.vector.reciprocal(self.winv[:], self.wtotal[:]))
                link(nc.vector.tensor_tensor(self.weight[:], self.weight[:], wide(self.winv[:]), ALU.mult))
                link(nc.vector.tensor_scalar(self.sig[:], self.sig[:], 1.0, None, ALU.add))
                link(nc.vector.reciprocal(self.sig[:], self.sig[:]))
                nc.vector.tensor_copy(self.wn[:, :, 0:EXPERTS], self.weight[:]).then_inc(self.w_split, 1)
                nc.vector.tensor_copy(self.sn[:, :, 0], self.sig[:]).then_inc(self.w_split, 1)
                dve.wait_ge(self.w_split, 4 * ch + 2)
                nc.vector.tensor_tensor(self.wn[:, :, EXPERTS:2 * EXPERTS], self.weight[:],
                                        self.wn[:, :, 0:EXPERTS].bitcast(F32), ALU.subtract).then_inc(self.w_split, 1)
                nc.vector.tensor_tensor(self.sn[:, :, 1], self.sig[:], self.sn[:, :, 0].bitcast(F32), ALU.subtract).then_inc(self.w_split, 1)
                dve.wait_ge(self.w_split, 4 * ch + 4)


def stage_heads_and_experts(k, d, XH, XL, X, ident, half, cos, sin, wh, wl, woh, wol, rh, rl, out):
    nc = k.nc
    H, T = 256, X.shape[1]
    NCH = T // 4
    STEPS = PAIRS + 1
    N = NCH * STEPS
    RING = 4
    COLS = 2 * 256 + 256 + P
    with ExitStack() as c:
        WT = k.sb("WT", [P, T * P], FR, c)
        WS = k.sb("WS", [2, T * P], FR, c)
        w = k.sb("w7", [P, RING, COLS], F32, c)
        ones = k.sb("ones7", [2, P], FR, c)
        guh = k.sb("guh", [P, 2, 512], FR, c)
        gul = k.sb("gul", [P, 2, 512], FR, c)
        dh = k.sb("dh", [P, 2, 256], FR, c)
        dl = k.sb("dl", [P, 2, 256], FR, c)
        sel = k.sb("sel", [P, 2, P], FR, c)
        gated = k.sb("gated7", [P, 2, 512], F32, c)
        weighted = k.sb("weighted", [P, 512], F32, c)
        inter = k.sb("inter", [P, 2, 512], F32, c)
        ih = k.sb("ih", [P, 2, 512], FR, c)
        il = k.sb("il", [P, 2, 512], FR, c)
        acc = k.sb("acc", [P, 2, 512], F32, c)
        y = k.sb("y7", [P, 4, H], F32, c)
        ps = [c.enter_context(nc.psum_tensor(f"p7_{i}", [P, 512], F32)) for i in range(8)]
        p_g, p_u, p_w, p_y = ps[0], ps[1], ps[2], ps[3:5]
        heads = Heads(k, c, d, XH, XL, X, ident, half, cos, sin, wh, wl, woh, wol, rh, rl, WT, WS, ps[5:8])
        starts, routed = slots_of(T)
        LEAD = routed[0]
        assert all(r <= LEAD + STEPS * ch for ch, r in enumerate(routed))
        norm = Norm(k, c, half, "s7")
        sem = lambda n: k.sem(n + "7")
        w_in = [sem(f"w_in{i}") for i in range(RING)]
        ones_set, sel_ready = sem("ones_set"), sem("sel_ready")
        guh_ready, dh_ready, gul_ready, dl_ready = sem("guh_ready"), sem("dh_ready"), sem("gul_ready"), sem("dl_ready")
        w_ready, g_ready, u_ready, down_done = sem("w_ready"), sem("g_ready"), sem("u_ready"), sem("down_done")
        gated_ready, weighted_ready, inter_ready = sem("gated_ready"), sem("weighted_ready"), sem("inter_ready")
        ih_ready, il_ready, acc_out, summed = sem("ih_ready"), sem("il_ready"), sem("acc_out"), sem("summed")
        turned, x_out, stored = sem("turned"), sem("x_out"), sem("stored")

        def finished(n):
            ch, p = divmod(n, STEPS)
            return 4 * (ch - 1) + p - 1 if ch and 1 <= p <= 4 else None

        with nc.Block() as block:
            @block.sync
            def _(sp):
                for n in range(N):
                    if n >= RING:
                        m = n - RING + 1
                        sp.wait_ge(sel_ready, m)
                        sp.wait_ge(gul_ready, m)
                        sp.wait_ge(dl_ready, m)
                    sp.dma_start(w[:, n % RING, :], d["experts"][n % STEPS]).then_inc(w_in[n % RING], 16)
                sp.wait_ge(stored, 16 * T)

            @block.scalar
            def _(act):
                def split_down(n):
                    if n < N:
                        act.wait_ge(w_in[n % RING], 16 * (n // RING + 1))
                        if n >= 2:
                            act.wait_ge(down_done, n - 1)
                        nc.scalar.copy(dh[:, n % 2], w[:, n % RING, 512:768]).then_inc(dh_ready, 1)

                def split_gates(n):
                    if n < N:
                        act.wait_ge(w_in[n % RING], 16 * (n // RING + 1))
                        if n >= 2:
                            act.wait_ge(u_ready, n - 1)
                        nc.scalar.copy(sel[:, n % 2, :], w[:, n % RING, 768:COLS]).then_inc(sel_ready, 1)
                        nc.scalar.copy(guh[:, n % 2], w[:, n % RING, 0:512]).then_inc(guh_ready, 1)

                def evacuate():
                    for i in range(2):
                        nc.scalar.copy(acc[:, i, :], p_y[i][:]).then_inc(acc_out, 1)

                for slot in range(LEAD):
                    heads.act(act, slot)
                split_gates(0)
                split_gates(1)
                split_down(0)
                for n in range(N):
                    act.wait_ge(g_ready, n + 1)
                    if n >= 2:
                        act.wait_ge(weighted_ready, n - 1)
                    nc.scalar.activation(gated[:, n % 2, :], p_g[:], ACT.Silu).then_inc(gated_ready, 1)
                    split_down(n + 1)
                    act.wait_ge(inter_ready, n + 1)
                    if n >= 2:
                        act.wait_ge(down_done, n - 1)
                    nc.scalar.copy(ih[:, n % 2, :], inter[:, n % 2, :]).then_inc(ih_ready, 1)
                    if n % STEPS == 0 and n:
                        act.wait_ge(down_done, n)
                        if n > STEPS:
                            act.wait_ge(turned, 2 * (n // STEPS - 1))
                        evacuate()
                    split_gates(n + 2)
                    heads.act(act, LEAD + n)
                    t = finished(n)
                    if t is not None:
                        act.wait_ge(x_out, t + 1)
                        act.dma_start(out[P * t:P * t + P, :], y[:, t % 4, :]).then_inc(stored, 16)
                act.wait_ge(down_done, N)
                act.wait_ge(turned, 2 * (NCH - 1))
                evacuate()
                for t in range(T - 4, T):
                    act.wait_ge(x_out, t + 1)
                    act.dma_start(out[P * t:P * t + P, :], y[:, t % 4, :]).then_inc(stored, 16)

            @block.gpsimd
            def _(pool):
                def split_down(n):
                    if n < N:
                        pool.wait_ge(dh_ready, n + 1)
                        if n >= 2:
                            pool.wait_ge(down_done, n - 1)
                        nc.gpsimd.tensor_tensor(dl[:, n % 2], w[:, n % RING, 512:768], dh[:, n % 2].bitcast(F32),
                                                ALU.subtract).then_inc(dl_ready, 1)

                def split_gates(n):
                    if n < N:
                        pool.wait_ge(guh_ready, n + 1)
                        if n >= 2:
                            pool.wait_ge(u_ready, n - 1)
                        nc.gpsimd.tensor_tensor(gul[:, n % 2], w[:, n % RING, 0:512], guh[:, n % 2].bitcast(F32),
                                                ALU.subtract).then_inc(gul_ready, 1)

                for slot in range(LEAD):
                    heads.pool(pool, slot)
                split_gates(0)
                split_gates(1)
                split_down(0)
                for n in range(N):
                    split_down(n + 1)
                    t = finished(n)
                    if t is not None:
                        norm.power(pool, t)
                    split_gates(n + 2)
                    heads.pool(pool, LEAD + n)
                for t in range(T - 4, T):
                    norm.power(pool, t)

            @block.vector
            def _(dve):
                heads.start_vector(dve)
                link = heads.link
                link(nc.vector.memset(ones[:].bitcast(F32), 1.0))
                nc.vector.tensor_copy(ones[:], ones[:].bitcast(F32)).then_inc(ones_set, 1)

                def step(n):
                    i = n % 2
                    dve.wait_ge(gated_ready, n + 1)
                    dve.wait_ge(w_ready, n + 1)
                    if n >= 1:
                        dve.wait_ge(inter_ready, n)
                    nc.vector.tensor_tensor(weighted[:], gated[:, i, :], p_w[:], ALU.mult).then_inc(weighted_ready, 1)
                    dve.wait_ge(weighted_ready, n + 1)
                    dve.wait_ge(u_ready, n + 1)
                    if n >= 2:
                        dve.wait_ge(ih_ready, n - 1)
                        dve.wait_ge(il_ready, n - 1)
                    nc.vector.tensor_tensor(inter[:, i, :], weighted[:], p_u[:], ALU.mult).then_inc(inter_ready, 1)

                def low(n):
                    i = n % 2
                    dve.wait_ge(ih_ready, n + 1)
                    if n >= 2:
                        dve.wait_ge(down_done, n - 1)
                    nc.vector.tensor_tensor(il[:, i, :], inter[:, i, :], ih[:, i, :].bitcast(F32), ALU.subtract).then_inc(il_ready, 1)

                def residual(ch):
                    for r, bank in enumerate((p_w, p_g)):
                        t = 4 * ch + 2 * r
                        dve.wait_ge(turned, 2 * ch + r + 1)
                        if ch:
                            dve.wait_ge(stored, 16 * 4 * ch)
                        nc.vector.tensor_tensor(y[:, 2 * r:2 * r + 2, :], bank[:].rearrange("p (t n) -> p t n", t=2), X[:, t:t + 2, :],
                                                ALU.add).then_inc(summed, 1)

                def finish(t):
                    dve.wait_ge(summed, 2 * (t // 4) + (t % 4) // 2 + 1)
                    norm.statistics(t, y[:, t % 4, :], link)
                    norm.scale(dve, t, y[:, t % 4, :], y[:, t % 4, :]).then_inc(x_out, 1)

                for slot in range(LEAD):
                    heads.dve(dve, slot)
                for n in range(N):
                    step(n)
                    low(n)
                    if n % STEPS == 0 and n:
                        residual(n // STEPS - 1)
                    t = finished(n)
                    if t is not None:
                        finish(t)
                    heads.dve(dve, LEAD + n)
                residual(NCH - 1)
                for t in range(T - 4, T):
                    finish(t)

            @block.tensor
            def _(pe):
                def gates(n):
                    ch, p = divmod(n, STEPS)
                    i, s = n % 2, slice(512 * ch, 512 * ch + 512)
                    if p == 0:
                        pe.wait_ge(heads.w_out, ch + 1)
                        pe.wait_ge(heads.s_out, ch + 1)
                    if ch and p == 1:
                        pe.wait_ge(summed, 2 * ch)
                    if n >= 1:
                        pe.wait_ge(weighted_ready, n)
                    pe.wait_ge(sel_ready, n + 1)
                    if p < PAIRS:
                        pe.matmul(p_w[:], sel[:, i, :], WT[:, s], start=True, stop=True).then_inc(w_ready, 1)
                    else:
                        pe.wait_ge(ones_set, 1)
                        pe.matmul(p_w[:], ones[:], WS[:, s], start=True, stop=True).then_inc(w_ready, 1)
                    pe.wait_ge(gul_ready, n + 1)
                    for dst, done, freed, o in ((p_g, g_ready, gated_ready, 0), (p_u, u_ready, inter_ready, P)):
                        if n >= 1:
                            pe.wait_ge(freed, n)
                        mms = [(wt, x, kc) for kc in range(2) for wt, x in ((guh, XH), (guh, XL), (gul, XH))]
                        for m, (wt, x, kc) in enumerate(mms):
                            mm = pe.matmul(dst[:], wt[:, i, 256 * kc + o:256 * kc + o + P], x[:, kc, s], start=m == 0, stop=m == 5)
                        mm.then_inc(done, 1)

                def down(n):
                    i, p, ch = n % 2, n % STEPS, n // STEPS
                    pe.wait_ge(dl_ready, n + 1)
                    pe.wait_ge(il_ready, n + 1)
                    if p == 0 and ch:
                        pe.wait_ge(acc_out, 2 * ch)
                    for hc in range(2):
                        for m, (wt, x) in enumerate(((dh, ih), (dh, il), (dl, ih))):
                            mm = pe.matmul(p_y[hc][:], wt[:, i, P * hc:P * hc + P], x[:, i, :],
                                           start=p == 0 and m == 0, stop=p == STEPS - 1 and m == 2)
                    mm.then_inc(down_done, 1)

                def turn(ch):
                    n = min(N, (ch + 1) * STEPS + 1)
                    pe.wait_ge(acc_out, 2 * (ch + 1))
                    for r, (bank, used) in enumerate(((p_w, weighted_ready), (p_g, gated_ready))):
                        pe.wait_ge(used, n)
                        for j in range(2):
                            for hc in range(2):
                                mm = pe.transpose(bank[:, 256 * j + P * hc:256 * j + P * hc + P],
                                                  acc[:, hc, P * (2 * r + j):P * (2 * r + j) + P], ident[:])
                        mm.then_inc(turned, 1)

                for slot in range(LEAD):
                    heads.pe(pe, slot)
                for n in range(N):
                    gates(n)
                    if n:
                        down(n - 1)
                    if n % STEPS == 0 and n:
                        turn(n // STEPS - 1)
                    heads.pe(pe, LEAD + n)
                down(N - 1)
                turn(NCH - 1)


def build(nc, d, out, stop_after=99):
    T = 16
    H = 256
    with ExitStack() as ctx:
        k = Core(nc, ctx)
        X = k.sb("X", [P, T, H], F32)
        XH = k.sb("XH", [P, 2, T * P], FR)
        XL = k.sb("XL", [P, 2, T * P], FR)
        ident = k.sb("ident", [P, P], F32)
        half = k.sb("half", [P, 1], F32)
        half_set = k.sem("half_set")
        stored = k.sem("stored")
        with ExitStack() as c:
            qh, ql, kh, kl = (k.sb(n, [P, 2, T * P], FR, c) for n in ("qh", "ql", "kh", "kl"))
            V = k.sb("V", [P, T, H], F32, c)
            stage_l0_project(k, d, XH, XL, X, ident, qh, ql, kh, kl, V)
            with nc.Block() as block:
                @block.vector
                def _(dve):
                    nc.vector.memset(half[:], -0.5).then_inc(half_set, 1)
                    dve.wait_ge(half_set, 1)
            stage_l0_attention(k, XH, XL, X, ident, half, qh, ql, kh, kl, V)
        if stop_after > 2:
            from_stage_3(k, d, XH, XL, X, ident, half, out, stop_after)
        if stop_after < 6:
            with nc.Block() as block:
                @block.sync
                def _(sp):
                    sp.dma_start(out.rearrange("(t p) n -> p t n", p=P), X[:]).then_inc(stored, 16)
                    sp.wait_ge(stored, 16)


def from_stage_3(k, d, XH, XL, X, ident, half, out, stop_after):
    stage_ffn(k, d, XH, XL, X, ident, half)
    if stop_after > 3:
        with ExitStack() as c:
            cos, sin = (k.sb(n, [P, 8, 8], F32, c) for n in ("cos", "sin"))
            wh, wl = (k.sb(n, [P, 2, 768], FR, c) for n in ("l1_wh", "l1_wl"))
            woh, wol = (k.sb(n, [P, 2, 256], FR, c) for n in ("l1_woh", "l1_wol"))
            rh, rl = (k.sb(n, [P, 2, EXPERTS + 2], FR, c) for n in ("router_h", "router_l"))
            stage_l1_prepare(k, d, cos, sin, wh, wl, woh, wol, rh, rl)
            stage_heads_and_experts(k, d, XH, XL, X, ident, half, cos, sin, wh, wl, woh, wol, rh, rl, out)


def layouts(i):
    import numpy as np
    a = np.asarray
    x = a(i["L0_attn_input"]).reshape(-1, 256)
    gu = a(i["L1_ffn_gu_w"]).reshape(32, 2, 2, 64, 2, 128)
    gate_up = np.zeros((2, 33, 128, 2, 2, 64), np.float32)
    gate_up[:, :32] = gu.transpose(4, 0, 5, 2, 1, 3)
    for j, name in enumerate(("gate", "up")):
        gate_up[:, 32, :, j, 0, :] = a(i[f"L1_ffn_sh_{name}_w"]).T.reshape(2, 128, 64)
    gate_up = gate_up.reshape(2, 33, 128, 256)
    down = np.zeros((33, 128, 256), np.float32)
    down[:32] = a(i["L1_ffn_dp_w"]).transpose(0, 2, 1).reshape(32, 128, 256)
    down[32, :64] = a(i["L1_ffn_sh_down_w"]).T
    select = np.zeros((33, 128, 2, 64), np.float32)
    for e in range(64):
        select[e // 2, e, e % 2] = select[e // 2, 64 + e, e % 2] = 1
    select = select.reshape(33, 128, 128)
    out = {
        "x": x,
        "xT": x.T,
        "wqkv": np.concatenate([a(i[f"L0_attn_W{n}"]).T for n in "qkv"], axis=1),
        "bqk": np.stack([a(i["L0_attn_bq"])[:128], a(i["L0_attn_bq"])[128:],
                         a(i["L0_attn_bk"])[:128], a(i["L0_attn_bk"])[128:]], axis=1),
        "bv": a(i["L0_attn_bv"]),
        "w_gate": a(i["L0_ffn_w_gate"]).view(np.int32),
        "w_up": a(i["L0_ffn_w_up"]).view(np.int32),
        "w_down": a(i["L0_ffn_w_down"]).view(np.int32),
        "s_gu": np.stack([a(i["L0_ffn_s_gate"]).reshape(8, 128).T, a(i["L0_ffn_s_up"]).reshape(8, 128).T], axis=1),
        "s_down": a(i["L0_ffn_s_down"]),
        "pos": np.arange(1024, dtype=np.float32).reshape(8, 128).T,
        "inv_freq": a(i["L1_attn_inv_freq"]),
        "l1_wqkv": np.concatenate([a(i[f"L1_attn_w{n}"]).T for n in "qkv"], axis=1),
        "l1_wo": a(i["L1_attn_wo"]).T,
        "router": np.concatenate([a(i["L1_ffn_gate_w"]).T, a(i["L1_ffn_sh_gate1_w"]).T], axis=1),
        "experts": np.concatenate([gate_up[0], gate_up[1], down, select], axis=2),
        "ident": np.eye(128, dtype=np.float32),
    }
    return {name: np.ascontiguousarray(v) for name, v in out.items()}


def kernel(**inputs):
    import numpy as np
    import concourse.bacc as bacc
    from concourse.bass_utils import run_bass_kernel_spmd

    nc = bacc.Bacc("TRN2", target_bir_lowering=False, num_devices=1)
    arrays, d = {}, {}
    for name, v in layouts(inputs).items():
        arrays[f"in_{name}"] = v
        d[name] = nc.dram_tensor(f"in_{name}", v.shape, mybir.dt.from_np(v.dtype), kind="ExternalInput").ap()
    out = nc.dram_tensor("out", (2048, 256), F32, kind="ExternalOutput").ap()
    build(nc, d, out)
    r = run_bass_kernel_spmd(nc, [arrays], core_ids=[0])
    return np.asarray(r.results[0]["out"]).reshape(2, 1024, 256)
```

```python
from contextlib import ExitStack

from concourse import mybir

F32 = mybir.dt.float32
FR = mybir.dt.float32r
I8 = mybir.dt.int8
I32 = mybir.dt.int32
ALU = mybir.AluOpType
ACT = mybir.ActivationFunctionType
AX = mybir.AxisListType

P = 128
EPS = 1e-5


class Core:

    def __init__(self, nc, ctx):
        self.nc, self.ctx = nc, ctx

    def sb(self, name, shape, dt, ctx=None):
        return (ctx or self.ctx).enter_context(self.nc.sbuf_tensor("sb_" + name, shape, dt))

    def sem(self, name, ctx=None):
        return self.ctx.enter_context(self.nc.semaphore(name))


def chained(eng, sem):
    count = [0]

    def link(ins):
        count[0] += 1
        ins.then_inc(sem, 1)
        eng.wait_ge(sem, count[0])

    return link


HEADS, HD = 16, 16
TWO_PI = 6.283185307179586
TURN_PARTS = (6.28125, 0.001934051513671875, 1.255422830581665e-06, 2.430840251310684e-10)
ROUND = 12582912.0


class Prepare:

    PIECES = 10

    def __init__(self, k, c, d, w):
        self.nc, self.d = k.nc, d
        self.cos, self.sin, self.wh, self.wl, self.woh, self.wol, self.rh, self.rl, self.wg, self.wu, self.wd, *scales = w
        self.ST = self.cos.shape[1]
        self.pos = k.sb("pos", [P, self.ST], F32, c)
        self.freq = k.sb("freq", [P, 8], F32, c)
        self.ang = k.sb("ang", [P, self.ST, 8], F32, c)
        self.turns = k.sb("turns", [P, self.ST, 8], F32, c)
        self.over = k.sb("over", [P, self.ST, 8], F32, c)
        self.shifted = k.sb("shifted", [P, self.ST, 8], F32, c)
        self.s_gu, self.s_down = scales
        self.small_in = k.sem("small_in")
        self.w_in = k.sem("l1_w_in")
        self.i8_in = k.sem("i8_in")
        self.hi_ready = k.sem("l1_w_hi")
        self.lo_ready = k.sem("l1_w_lo")
        self.cast = k.sem("i8_cast")
        self.reduced = k.sem("angles_reduced")
        self.padded = k.sem("router_padded")

    def allocate_weights(self, k, c):
        self.wf = k.sb("l1_wf", [P, 2, 768], F32, c)
        self.wof = k.sb("l1_wof", [P, 2, 256], F32, c)
        self.rf = k.sb("router_f", [P, 2, 65], F32, c)
        self.wg8 = k.sb("wg8", [P, 2, 256], I32, c)
        self.wu8 = k.sb("wu8", [P, 2, 256], I32, c)
        self.wd8 = k.sb("wd8", [P, 8, 64], I32, c)

    def load_positions(self, sp):
        d = self.d
        sp.dma_start(self.pos[:], d["pos"]).then_inc(self.small_in, 16)
        sp.dma_start(self.freq[:], d["inv_freq"].partition_broadcast(P)).then_inc(self.small_in, 16)

    def load_weights(self, sp):
        d = self.d
        for x, name in ((self.wf, "l1_wqkv"), (self.wof, "l1_wo"), (self.rf, "router")):
            sp.dma_start(x[:], d[name].rearrange("(c p) n -> p c n", p=P)).then_inc(self.w_in, 16)
        for x, name in ((self.wg8, "w_gate"), (self.wu8, "w_up"), (self.wd8, "w_down")):
            sp.dma_start(x[:], d[name].rearrange("(c p) n -> p c n", p=P)).then_inc(self.i8_in, 16)
        for x, name in ((self.s_gu, "s_gu"), (self.s_down, "s_down")):
            sp.dma_start(x[:], d[name]).then_inc(self.i8_in, 16)

    def angles(self, dve, link):
        nc, P_ST = self.nc, [P, self.ST, 8]
        ang, turns, over, shifted = self.ang, self.turns, self.over, self.shifted
        dve.wait_ge(self.small_in, 32)
        link(nc.vector.tensor_tensor(ang[:], self.pos[:].unsqueeze(2).broadcast_to(P_ST),
                                     self.freq[:].unsqueeze(1).broadcast_to(P_ST), ALU.mult))
        link(nc.vector.tensor_scalar(turns[:], ang[:], 1.0 / TWO_PI, None, ALU.mult))
        link(nc.vector.tensor_scalar(turns[:], turns[:], ROUND, None, ALU.add))
        link(nc.vector.tensor_scalar(turns[:], turns[:], -ROUND, None, ALU.add))
        for part in TURN_PARTS:
            link(nc.vector.scalar_tensor_tensor(out=ang[:], in0=turns[:], scalar=-part, in1=ang[:],
                                                op0=ALU.mult, op1=ALU.add))
        link(nc.vector.tensor_scalar(shifted[:], ang[:], TWO_PI / 4, None, ALU.add))
        link(nc.vector.tensor_scalar(over[:], shifted[:], TWO_PI / 2, -TWO_PI, ALU.is_gt, ALU.mult))
        link(nc.vector.tensor_tensor(shifted[:], shifted[:], over[:], ALU.add))
        for x in (ang, shifted):
            nc.vector.tensor_scalar(x[:], x[:], 3.1415925, -3.1415925, ALU.min, ALU.max).then_inc(self.reduced, 1)

    def sines(self, act):
        act.wait_ge(self.reduced, 2)
        self.nc.scalar.activation(self.sin[:], self.ang[:], ACT.Sin)
        self.nc.scalar.activation(self.cos[:], self.shifted[:], ACT.Sin)

    def act(self, act, i):
        nc = self.nc
        if i == 0:
            act.wait_ge(self.w_in, 48)
            nc.scalar.copy(self.rh[:, :, 0:65], self.rf[:]).then_inc(self.hi_ready, 1)
        elif i == 1:
            nc.scalar.copy(self.woh[:], self.wof[:]).then_inc(self.hi_ready, 1)
        elif i < 4:
            nc.scalar.copy(self.wh[:, i - 2], self.wf[:, i - 2]).then_inc(self.hi_ready, 1)
        elif i < self.PIECES:
            if i == 4:
                act.wait_ge(self.i8_in, 80)
            x, x8 = ((self.wg, self.wg8), (self.wu, self.wu8), (self.wd, self.wd8))[(i - 4) // 2]
            n = x.shape[1] // 2
            s = slice(n * (i % 2), n * (i % 2) + n)
            nc.scalar.copy(x[:, s], x8[:, s].bitcast(I8)).then_inc(self.cast, 1)

    def dve(self, dve, i):
        nc = self.nc
        if i >= 4:
            return
        if i == 0:
            nc.vector.memset(self.rh[:, :, 65:66].bitcast(F32), 0.0).then_inc(self.padded, 1)
            nc.vector.memset(self.rl[:, :, 65:66].bitcast(F32), 0.0).then_inc(self.padded, 1)
        dve.wait_ge(self.hi_ready, i + 1)
        if i == 0:
            lo, f, hi = self.rl[:, :, 0:65], self.rf[:], self.rh[:, :, 0:65]
        elif i == 1:
            lo, f, hi = self.wol[:], self.wof[:], self.woh[:]
        else:
            lo, f, hi = self.wl[:, i - 2], self.wf[:, i - 2], self.wh[:, i - 2]
        nc.vector.tensor_tensor(lo, f, hi.bitcast(F32), ALU.subtract).then_inc(self.lo_ready, 1)


def stage_project(k, d, prepare, XH, XL, X, ident, half, half_set, qh, ql, kh, kl, V):
    nc = k.nc
    H, N = 256, X.shape[1] * P
    KC, NCH, TPC = H // P, N // 512, 4
    W_PARTS = slice(0, H), slice(H, 3 * H)
    with ExitStack() as c:
        xf = k.sb("xf", [P, KC, N], F32, c)
        wf = k.sb("wf", [P, KC, 3 * H], F32, c)
        wh = k.sb("wh", [P, KC, 3 * H], FR, c)
        wl = k.sb("wl", [P, KC, 3 * H], FR, c)
        bqk = k.sb("bqk", [P, 4], F32, c)
        bvb = k.sb("bvb", [P, H], F32, c)
        ps = [c.enter_context(nc.psum_tensor(f"projection{i}", [P, 512], F32)) for i in range(8)]
        x_in = [k.sem(f"x_in{i}", c) for i in range(NCH)]
        w_in = [k.sem(f"w_in{i}", c) for i in range(2)]
        v_chain = k.sem("v_chain1")
        misc_in = k.sem("misc_in", c)
        w_hi = k.sem("w_hi", c)
        w_split = k.sem("w_split", c)
        x_hi = k.sem("x_hi", c)
        x_split = k.sem("x_split", c)
        qk_done = k.sem("qk_done", c)
        v_done = k.sem("v_done", c)
        qk_hi = k.sem("qk_hi", c)
        qk_lo = k.sem("qk_lo", c)
        v_out = k.sem("v_out", c)

        with nc.Block() as block:
            @block.sync
            def _(sp):
                w, xt = (d[name].rearrange("(c p) n -> p c n", p=P) for name in ("wqkv", "xT"))
                for ch in range(NCH):
                    if ch < 2:
                        sp.dma_start(wf[:, :, W_PARTS[ch]], w[:, :, W_PARTS[ch]]).then_inc(w_in[ch], 16)
                    s = slice(512 * ch, 512 * ch + 512)
                    sp.dma_start(xf[:, :, s], xt[:, :, s]).then_inc(x_in[ch], 16)
                prepare.load_positions(sp)
                sp.dma_start(bqk[:], d["bqk"]).then_inc(misc_in, 16)
                sp.dma_start(bvb[:], d["bv"].partition_broadcast(P)).then_inc(misc_in, 16)
                sp.dma_start(ident[:], d["ident"]).then_inc(misc_in, 16)
                sp.dma_start(X[:], d["x"].rearrange("(t p) n -> p t n", p=P)).then_inc(misc_in, 16)
                sp.wait_ge(misc_in, 64)

            @block.scalar
            def _(act):
                for ch in range(NCH):
                    if ch < 2:
                        act.wait_ge(w_in[ch], 16)
                        nc.scalar.copy(wh[:, :, W_PARTS[ch]], wf[:, :, W_PARTS[ch]]).then_inc(w_hi, 1)
                    s = slice(512 * ch, 512 * ch + 512)
                    act.wait_ge(x_in[ch], 16)
                    nc.scalar.copy(XH[:, :, s], xf[:, :, s]).then_inc(x_hi, 1)
                prepare.sines(act)
                act.wait_ge(misc_in, 64)
                for n in range(4 * NCH):
                    ch, which, o = n // 4, (n // 2) % 2, n % 2
                    act.wait_ge(qk_done, n + 1)
                    dst = (qh, kh)[which]
                    nc.scalar.activation(dst[:, o, 512 * ch:512 * ch + 512], ps[n % 4][:], ACT.Identity,
                                         bias=bqk[:, 2 * which + o:2 * which + o + 1]).then_inc(qk_hi, 1)

            @block.vector
            def _(dve):
                nc.vector.memset(half[:], -0.5).then_inc(half_set, 1)
                for ch in range(NCH):
                    if ch < 2:
                        dve.wait_ge(w_hi, ch + 1)
                        nc.vector.tensor_tensor(wl[:, :, W_PARTS[ch]], wf[:, :, W_PARTS[ch]], wh[:, :, W_PARTS[ch]].bitcast(F32),
                                                ALU.subtract).then_inc(w_split, 1)
                    s = slice(512 * ch, 512 * ch + 512)
                    dve.wait_ge(x_hi, ch + 1)
                    nc.vector.tensor_tensor(XL[:, :, s], xf[:, :, s], XH[:, :, s].bitcast(F32),
                                            ALU.subtract).then_inc(x_split, 1)
                prepare.angles(dve, chained(dve, v_chain))
                dve.wait_ge(misc_in, 64)
                for ch in range(NCH):
                    for j in range(4):
                        n, which, o = 4 * ch + j, j // 2, j % 2
                        hi, lo = ((qh, ql), (kh, kl))[which]
                        s = slice(512 * ch, 512 * ch + 512)
                        dve.wait_ge(qk_hi, n + 1)
                        nc.vector.scalar_tensor_tensor(
                            out=lo[:, o, s], in0=ps[n % 4][:], scalar=bqk[:, 2 * which + o:2 * which + o + 1],
                            in1=hi[:, o, s].bitcast(F32), op0=ALU.add, op1=ALU.subtract).then_inc(qk_lo, 1)
                    for j in range(TPC):
                        t = TPC * ch + j
                        dve.wait_ge(v_done, t + 1)
                        nc.vector.tensor_tensor(V[:, t, :], ps[4 + t % 4][:, 0:H], bvb[:], ALU.add).then_inc(v_out, 1)

            @block.tensor
            def _(pe):
                for ch in range(NCH):
                    pe.wait_ge(x_split, ch + 1)
                    s = slice(512 * ch, 512 * ch + 512)
                    for j in range(4):
                        n, which, o = 4 * ch + j, j // 2, j % 2
                        if ch == 0 and j in (0, 2):
                            pe.wait_ge(w_split, which + 1)
                        col = slice(H * which + P * o, H * which + P * o + P)
                        if n >= 4:
                            pe.wait_ge(qk_lo, n - 3)
                        mms = [(w[:, kc, col], x[:, kc, s]) for kc in range(KC)
                               for w, x in ((wh, XH), (wh, XL), (wl, XH))]
                        for i, (l, r) in enumerate(mms):
                            mm = pe.matmul(ps[n % 4][:], l, r, start=i == 0, stop=i == len(mms) - 1)
                        mm.then_inc(qk_done, 1)
                    for j in range(TPC):
                        t = TPC * ch + j
                        if t >= 4:
                            pe.wait_ge(v_out, t - 3)
                        ts = slice(P * t, P * t + P)
                        mms = [(x[:, kc, ts], w[:, kc, 2 * H:3 * H]) for kc in range(KC)
                               for x, w in ((XH, wh), (XL, wh), (XH, wl))]
                        for i, (l, r) in enumerate(mms):
                            mm = pe.matmul(ps[4 + t % 4][:, 0:H], l, r, start=i == 0, stop=i == len(mms) - 1)
                        mm.then_inc(v_done, 1)


class Norm:

    def __init__(self, k, ctx, half, tag):
        self.nc, self.half = k.nc, half
        self.stats = k.sb(tag + "_ln_stats", [P, 4, 6], F32, ctx)
        self.mv = k.sb(tag + "_ln_mv", [P, 4, 2], F32, ctx)
        self.ve = k.sb(tag + "_ln_ve", [P, 1], F32, ctx)
        self.rstd = k.sb(tag + "_ln_rstd", [P, 4, 1], F32, ctx)
        self.var_ready = k.sem(tag + "_ln_var_ready", ctx)
        self.eps_added = k.sem(tag + "_ln_eps_added", ctx)
        self.rstd_ready = k.sem(tag + "_ln_rstd_ready", ctx)

    def statistics(self, n, y, link):
        link(self.nc.vector.bn_stats(self.stats[:, n % 4, :], y))
        self.nc.vector.bn_aggr(self.mv[:, n % 4, :], self.stats[:, n % 4, :]).then_inc(self.var_ready, 1)

    def power(self, pool, n):
        pool.wait_ge(self.var_ready, n + 1)
        if n >= 1:
            pool.wait_ge(self.rstd_ready, n)
        self.nc.gpsimd.tensor_scalar(self.ve[:], self.mv[:, n % 4, 1:2], EPS, None, ALU.add).then_inc(self.eps_added, 1)
        pool.wait_ge(self.eps_added, n + 1)
        self.nc.gpsimd.tensor_tensor(self.rstd[:, n % 4, :], self.ve[:], self.half[:], ALU.pow).then_inc(self.rstd_ready, 1)

    def scale(self, dve, n, out, y):
        dve.wait_ge(self.rstd_ready, n + 1)
        return self.nc.vector.tensor_scalar(out, y, self.mv[:, n % 4, 0:1], self.rstd[:, n % 4, :],
                                            ALU.subtract, ALU.mult)


class Attention:

    PREPARE_AT = 4
    S = 1024
    H = 256

    def __init__(self, k, c, prepare, XH, XL, X, ident, half, qh, ql, kh, kl, V):
        nc = self.nc = k.nc
        self.XH, self.XL, self.X, self.ident = XH, XL, X, ident
        self.qh, self.ql, self.kh, self.kl, self.V = qh, ql, kh, kl, V
        self.T = X.shape[1]
        self.STEPS = self.T + 3
        S, H = self.S, self.H
        self.prob = k.sb("prob", [P, 2, S], F32, c)
        self.probT = k.sb("probT", [P, 2, S // P, P], F32, c)
        self.neg_max = k.sb("neg_max", [P, 2, 1], F32, c)
        self.row_sum = k.sb("row_sum", [P, 4, 1], F32, c)
        self.inv_sum = k.sb("inv_sum", [P, 1], F32, c)
        self.y = k.sb("y_attention", [P, H], F32, c)
        self.p_s = [c.enter_context(nc.psum_tensor(f"attention_s{i}", [P, S], F32)) for i in range(2)]
        self.p_t = [c.enter_context(nc.psum_tensor(f"attention_t{i}", [P, 4, P], F32)) for i in range(2)]
        self.p_o = [c.enter_context(nc.psum_tensor(f"attention_o{i}", [P, 512], F32)) for i in range(2)]
        self.norm = Norm(k, c, half, "attention")
        self.prepare = prepare
        prepare.allocate_weights(k, c)
        self.scores_ready = k.sem("scores_ready")
        self.max_ready = k.sem("max_ready")
        self.prob_ready = k.sem("prob_ready")
        self.turned = k.sem("turned")
        self.turned_out = [k.sem(f"turned_out{i}") for i in range(2)]
        self.out_ready = k.sem("out_ready")
        self.inverted = k.sem("inverted")
        self.x_new = k.sem("x_new")
        self.xT_ready = k.sem("xT_ready")
        self.xh_out = k.sem("xh_out")
        self.xl_out = k.sem("xl_out")

    def pe(self, pe, t):
        S, H, KT = self.S, self.H, self.S // P
        if t >= self.STEPS:
            return
        if t < self.T:
            if t >= 2:
                pe.wait_ge(self.prob_ready, t - 1)
            b, ts = t * P // S, slice(P * t, P * t + P)
            for half_ in range(2):
                ks = slice(b * S + 512 * half_, b * S + 512 * half_ + 512)
                mms = [(q[:, kc, ts], kk[:, kc, ks]) for kc in range(2)
                       for q, kk in ((self.qh, self.kh), (self.qh, self.kl), (self.ql, self.kh))]
                for i, (l, r) in enumerate(mms):
                    mm = pe.matmul(self.p_s[t % 2][:, 512 * half_:512 * half_ + 512], l, r,
                                   start=i == 0, stop=i == len(mms) - 1)
            mm.then_inc(self.scores_ready, 1)
        w = t - 3
        if w >= 0:
            pe.wait_ge(self.x_new, w + 1)
            for kc in range(2):
                mm = pe.transpose(self.p_o[w % 2][:, H + P * kc:H + P * kc + P], self.X[:, w, P * kc:P * kc + P], self.ident[:])
            mm.then_inc(self.xT_ready, 1)
        u = t - 1
        if 0 <= u < self.T:
            pe.wait_ge(self.prob_ready, u + 1)
            for h in range(2):
                if u >= 1:
                    pe.wait_ge(self.turned_out[h], u)
                for j in range(4):
                    kt = 4 * h + j
                    mm = pe.transpose(self.p_t[h][:, j, :], self.prob[:, u % 2, P * kt:P * kt + P], self.ident[:])
                mm.then_inc(self.turned, 1)
        v = t - 2
        if 0 <= v < self.T:
            pe.wait_ge(self.turned_out[0], v + 1)
            pe.wait_ge(self.turned_out[1], v + 1)
            if v >= 2:
                pe.wait_ge(self.xl_out, v - 1)
            b = v * P // S
            for kt in range(KT):
                mm = pe.matmul(self.p_o[v % 2][:, 0:H], self.probT[:, v % 2, kt, :], self.V[:, b * KT + kt, :],
                               start=kt == 0, stop=kt == KT - 1)
            mm.then_inc(self.out_ready, 1)

    def act(self, act, t):
        nc, H = self.nc, self.H
        if t >= self.STEPS:
            return
        if t < self.T:
            act.wait_ge(self.max_ready, t + 1)
            if t >= 2:
                act.wait_ge(self.turned, 2 * (t - 1))
            if t >= 4:
                act.wait_ge(self.inverted, t - 3)
            nc.scalar.activation(self.prob[:, t % 2, :], self.p_s[t % 2][:], ACT.Exp, bias=self.neg_max[:, t % 2, :],
                                 accum_out=self.row_sum[:, t % 4, :]).then_inc(self.prob_ready, 1)
        w = t - 3
        if w >= 0:
            act.wait_ge(self.xT_ready, w + 1)
            nc.scalar.copy(self.XH[:, :, P * w:P * w + P],
                           self.p_o[w % 2][:, H:2 * H].rearrange("p (c n) -> p c n", c=2)).then_inc(self.xh_out, 1)
        u = t - 1
        if 0 <= u < self.T:
            act.wait_ge(self.turned, 2 * u + 1)
            if u >= 2:
                act.wait_ge(self.out_ready, u - 1)
            nc.scalar.copy(self.probT[:, u % 2, 0:4, :], self.p_t[0][:]).then_inc(self.turned_out[0], 1)
        if self.PREPARE_AT <= t:
            self.prepare.act(act, t - self.PREPARE_AT)

    def dve(self, dve, t, link):
        nc, H = self.nc, self.H
        if t >= self.STEPS:
            return
        w = t - 3
        if w >= 0:
            dve.wait_ge(self.prob_ready, w + 1)
            nc.vector.reciprocal(self.inv_sum[:], self.row_sum[:, w % 4, :]).then_inc(self.inverted, 1)
            dve.wait_ge(self.inverted, w + 1)
            dve.wait_ge(self.out_ready, w + 1)
            link(nc.vector.scalar_tensor_tensor(out=self.y[:], in0=self.p_o[w % 2][:, 0:H], scalar=self.inv_sum[:],
                                                in1=self.X[:, w, :], op0=ALU.mult, op1=ALU.add))
            self.norm.statistics(w, self.y[:], link)
            self.norm.scale(dve, w, self.X[:, w, :], self.y[:]).then_inc(self.x_new, 1)
            dve.wait_ge(self.x_new, w + 1)
        if t < self.T:
            dve.wait_ge(self.scores_ready, t + 1)
            nc.vector.tensor_reduce(self.neg_max[:, t % 2, :], self.p_s[t % 2][:], AX.X, ALU.max,
                                    negate=True).then_inc(self.max_ready, 1)
        if w >= 0:
            dve.wait_ge(self.xh_out, w + 1)
            nc.vector.tensor_tensor(self.XL[:, :, P * w:P * w + P],
                                    self.p_o[w % 2][:, H:2 * H].rearrange("p (c n) -> p c n", c=2),
                                    self.XH[:, :, P * w:P * w + P].bitcast(F32), ALU.subtract).then_inc(self.xl_out, 1)
        u = t - 1
        if 0 <= u < self.T:
            dve.wait_ge(self.turned, 2 * u + 2)
            if u >= 2:
                dve.wait_ge(self.out_ready, u - 1)
            nc.vector.tensor_copy(self.probT[:, u % 2, 4:8, :], self.p_t[1][:]).then_inc(self.turned_out[1], 1)
        if self.PREPARE_AT <= t:
            self.prepare.dve(dve, t - self.PREPARE_AT)

    def pool(self, pool, t):
        if 0 <= t - 3 < self.T:
            self.norm.power(pool, t - 3)


class FeedForward:

    IT = 8
    TAIL = 5
    SPLIT = 14

    def __init__(self, k, c, d, XH, XL, X, ident, half, wg, wu, wd, s_gu, s_down, gated, inter, ih, il, acc, y, banks):
        self.nc, self.X, self.XH, self.XL, self.ident = k.nc, X, XH, XL, ident
        self.wg, self.wu, self.wd, self.s_gu, self.s_down = wg, wu, wd, s_gu, s_down
        self.gated, self.inter, self.ih, self.il, self.acc, self.y = gated, inter, ih, il, acc, y
        self.p_g, self.p_u, self.p_y, self.p_t = banks
        self.NCH = X.shape[1] // 4
        self.M = self.NCH * self.IT
        self.END = self.M + self.TAIL
        self.norm = Norm(k, c, half, "ffn")

        def for_ffn(name):
            return k.sem(name + "_ffn")

        self.g_ready = for_ffn("g_ready")
        self.u_ready = for_ffn("u_ready")
        self.gated_ready = for_ffn("gated_ready")
        self.inter_ready = for_ffn("inter_ready")
        self.ih_ready = for_ffn("ih_ready")
        self.il_ready = for_ffn("il_ready")
        self.down_done = for_ffn("down_done")
        self.acc_out = for_ffn("acc_out")
        self.turned = for_ffn("turned")
        self.summed = for_ffn("summed")
        self.x_new = for_ffn("x_new")
        self.xT_ready = for_ffn("xT_ready")
        self.xh_out = for_ffn("xh_out")
        self.xl_out = for_ffn("xl_out")

    def ended(self, slot):
        ch, r = divmod(slot, self.IT)
        return (ch - 1, r) if 1 <= ch <= self.NCH and r < self.TAIL else (None, None)

    def pair(self, ch, r):
        return slice(P * (4 * ch + 2 * r), P * (4 * ch + 2 * r + 2))

    def pe_gates(self, pe, m):
        if m >= self.M:
            return
        ch, i = divmod(m, self.IT)
        for dst, w, done, freed in ((self.p_g, self.wg, self.g_ready, self.gated_ready),
                                    (self.p_u, self.wu, self.u_ready, self.inter_ready)):
            if m >= 1:
                pe.wait_ge(freed, m)
            mms = [(w[:, kc, P * i:P * i + P], x[:, kc, 512 * ch:512 * ch + 512]) for kc in range(2) for x in (self.XH, self.XL)]
            for j, (l, r) in enumerate(mms):
                mm = pe.matmul(dst[:], l, r, start=j == 0, stop=j == len(mms) - 1)
            mm.then_inc(done, 1)

    def pe_down(self, pe, m):
        if not 0 <= m < self.M:
            return
        ch, i = divmod(m, self.IT)
        if m < self.SPLIT:
            pe.wait_ge(self.il_ready, m + 1)
            parts = (self.ih, self.il)
        else:
            pe.wait_ge(self.inter_ready, m + 1)
            parts = (self.inter,)
        if i == 0 and ch:
            pe.wait_ge(self.acc_out, 2 * ch)
        for hc in range(2):
            for j, x in enumerate(parts):
                w = self.wd[:, i, P * hc:P * hc + P]
                mm = pe.matmul(self.p_y[hc][:], w if m < self.SPLIT else w.bitcast(F32), x[:, m % 2, :],
                               start=i == 0 and j == 0, stop=i == self.IT - 1 and j == len(parts) - 1)
        mm.then_inc(self.down_done, 1)

    def pe_end(self, pe, slot):
        ch, k = self.ended(slot)
        if k in (1, 2):
            r = k - 1
            pe.wait_ge(self.acc_out, 2 * (ch + 1))
            if r:
                pe.wait_ge(self.summed, 2 * ch + 1)
            elif ch:
                pe.wait_ge(self.xl_out, 2 * ch)
            for j in range(2):
                for hc in range(2):
                    mm = pe.transpose(self.p_t[:, 256 * j + P * hc:256 * j + P * hc + P],
                                      self.acc[:, hc, P * (2 * r + j):P * (2 * r + j) + P], self.ident[:])
            mm.then_inc(self.turned, 1)
        if k in (3, 4):
            r = k - 3
            pe.wait_ge(self.summed, 2 * (ch + 1))
            pe.wait_ge(self.x_new, 4 * ch + 2 * r + 2)
            if r:
                pe.wait_ge(self.xl_out, 2 * ch + 1)
            for hc in range(2):
                for j in range(2):
                    mm = pe.transpose(self.p_t[:, 256 * hc + P * j:256 * hc + P * j + P],
                                      self.X[:, 4 * ch + 2 * r + j, P * hc:P * hc + P], self.ident[:])
            mm.then_inc(self.xT_ready, 1)

    def act(self, act, slot):
        nc, m = self.nc, slot
        if m < self.M:
            act.wait_ge(self.g_ready, m + 1)
            if m >= 2:
                act.wait_ge(self.inter_ready, m - 1)
            nc.scalar.activation(self.gated[:, m % 2, :], self.p_g[:], ACT.Silu,
                                 scale=self.s_gu[:, 0, m % self.IT:m % self.IT + 1]).then_inc(self.gated_ready, 1)
        if m < self.SPLIT:
            act.wait_ge(self.inter_ready, m + 1)
            if m >= 2:
                act.wait_ge(self.down_done, m - 1)
            nc.scalar.copy(self.ih[:, m % 2, :], self.inter[:, m % 2, :]).then_inc(self.ih_ready, 1)
        ch, k = self.ended(slot)
        if k == 0:
            act.wait_ge(self.down_done, self.IT * (ch + 1))
            if ch:
                act.wait_ge(self.turned, 2 * ch)
            for hc in range(2):
                nc.scalar.mul(self.acc[:, hc, :], self.p_y[hc][:], self.s_down[:, hc:hc + 1]).then_inc(self.acc_out, 1)
        if k in (3, 4):
            r = k - 3
            act.wait_ge(self.xT_ready, 2 * ch + r + 1)
            nc.scalar.copy(self.XH[:, :, self.pair(ch, r)],
                           self.p_t[:].rearrange("p (c n) -> p c n", c=2)).then_inc(self.xh_out, 1)

    def pool(self, pool, slot):
        m = slot
        if m < self.SPLIT:
            pool.wait_ge(self.ih_ready, m + 1)
            if m >= 2:
                pool.wait_ge(self.down_done, m - 1)
            self.nc.gpsimd.tensor_tensor(self.il[:, m % 2, :], self.inter[:, m % 2, :], self.ih[:, m % 2, :].bitcast(F32),
                                         ALU.subtract).then_inc(self.il_ready, 1)
        ch, k = self.ended(slot)
        if k in (1, 2):
            for j in range(2):
                self.norm.power(pool, 4 * ch + 2 * (k - 1) + j)

    def dve_fuse(self, dve, m):
        if m >= self.M:
            return
        dve.wait_ge(self.gated_ready, m + 1)
        dve.wait_ge(self.u_ready, m + 1)
        if 2 <= m < self.SPLIT + 2:
            dve.wait_ge(self.ih_ready, m - 1)
            dve.wait_ge(self.il_ready, m - 1)
        elif m >= 2:
            dve.wait_ge(self.down_done, m - 1)
        self.nc.vector.scalar_tensor_tensor(out=self.inter[:, m % 2, :], in0=self.p_u[:],
                                            scalar=self.s_gu[:, 1, m % self.IT:m % self.IT + 1], in1=self.gated[:, m % 2, :],
                                            op0=ALU.mult, op1=ALU.mult).then_inc(self.inter_ready, 1)

    def dve_end(self, dve, slot, link):
        nc = self.nc
        ch, k = self.ended(slot)
        if k in (2, 3):
            for j in range(2):
                t = 2 * (k - 2) + j
                self.norm.scale(dve, 4 * ch + t, self.X[:, 4 * ch + t, :], self.y[:, t, :]).then_inc(self.x_new, 1)
        if k in (1, 2):
            r = k - 1
            t = 4 * ch + 2 * r
            dve.wait_ge(self.turned, 2 * ch + r + 1)
            if ch:
                dve.wait_ge(self.x_new, 4 * ch)
            nc.vector.tensor_tensor(self.y[:, 2 * r:2 * r + 2, :], self.p_t[:].rearrange("p (t n) -> p t n", t=2),
                                    self.X[:, t:t + 2, :], ALU.add).then_inc(self.summed, 1)
            dve.wait_ge(self.summed, 2 * ch + r + 1)
            for j in range(2):
                self.norm.statistics(t + j, self.y[:, 2 * r + j, :], link)
        if k in (3, 4):
            r = k - 3
            dve.wait_ge(self.xh_out, 2 * ch + r + 1)
            nc.vector.tensor_tensor(self.XL[:, :, self.pair(ch, r)], self.p_t[:].rearrange("p (c n) -> p c n", c=2),
                                    self.XH[:, :, self.pair(ch, r)].bitcast(F32), ALU.subtract).then_inc(self.xl_out, 1)


EXPERTS, TOP = 64, 8
PAIRS = EXPERTS // 2
LOWEST = -3.0e38
LEAD_PLAN = {
    "project": 0, "v_out": 1, "rotate": 1, "rope": 2, "score_dve": 4, "score0": 3, "score1": 4, "score2": 4,
    "sum0": 4, "sum1": 6, "sum2": 7, "lower": 7, "exp": 8, "value_dve": 9, "value0": 9, "value1": 10,
    "merge": 11, "add0": 12, "add1": 12, "attend": 12, "turn_a": 14, "a_high": 15, "a_low": 16, "output": 17,
    "residual": 18, "power": 19, "scale": 21, "turn_x": 21, "x_high": 22, "x_low": 22, "logits": 23,
    "logits_out": 24, "best": 27,
}
PLAN = {
    "project": 0, "v_out": 1, "rotate": 1, "rope": 2, "score_dve": 3, "score0": 3, "score1": 4, "score2": 5,
    "sum0": 5, "sum1": 5, "sum2": 6, "lower": 7, "exp": 8, "value_dve": 10, "value0": 9, "value1": 10,
    "merge": 14, "add0": 11, "add1": 16, "attend": 17, "turn_a": 18, "a_high": 19, "a_low": 20, "output": 21,
    "residual": 21, "power": 23, "scale": 24, "turn_x": 26, "x_high": 27, "x_low": 28, "logits": 29,
    "logits_out": 30, "best": 31,
}
LEAD_BANKS = {"qk": 0, "v": 1, "aT": 0, "o": 2, "xT": 1, "logit": 2}
BANKS = {"qk": 0, "v": 1, "aT": 0, "o": 0, "xT": 1, "logit": 1, "wT": 2, "sT": 2}
STARTS = (0, 4, 8, 12, 16, 24, 32, 40, 48, 56, 64, 72, 80, 88, 96, 104)
ROUTE_LEN = 6


def plan(t):
    return LEAD_PLAN if t < 4 else PLAN


def slots_of(T):
    starts = list(STARTS[:T])
    return starts, [starts[t] + max(plan(t).values()) + 1 + ROUTE_LEN for t in range(3, T, 4)]


class Heads:

    VALUE_HEADS = 6

    def __init__(self, k, c, d, XH, XL, X, ident, half, cos, sin, wh, wl, woh, wol, rh, rl, WT, WS, banks, x_split, spread, sums_read):
        nc = k.nc
        self.sums_read = sums_read
        self.spread = spread
        self.x_split = x_split
        self.nc, self.X, self.XH, self.XL, self.ident = nc, X, XH, XL, ident
        self.cos, self.sin, self.wh, self.wl, self.woh, self.wol, self.rh, self.rl = cos, sin, wh, wl, woh, wol, rh, rl
        self.WT, self.WS = WT, WS
        self.T, self.ST = X.shape[1], cos.shape[1]
        self.starts, self.routed = slots_of(self.T)
        self.norm = Norm(k, c, half, "heads")

        def b(name, shape, dt=F32):
            return k.sb(name, shape, dt, c)

        self.rt = b("rope_t", [P, 4, 2 * HEADS, 8])
        self.rope = b("rope", [P, 2 * HEADS, HD])
        self.v = b("v_heads", [P, 3, HEADS, HD])
        self.prod = b("prod", [P, HEADS, HEADS, HD])
        self.score = b("score", [P, HEADS, HEADS])
        self.nmax = b("nmax", [P, HEADS])
        self.shifted = b("shifted_heads", [P, HEADS, HEADS])
        self.prob = b("prob_heads", [P, HEADS, HEADS])
        self.total = b("total_heads", [P, HEADS])
        self.inv = b("inv_heads", [P, HEADS])
        self.pv = b("pv", [P, HEADS, HEADS, HD])
        self.a = b("a_heads", [P, 2, HEADS, HD])
        self.ah = b("ah", [P, 2, P], FR)
        self.al = b("al", [P, 2, P], FR)
        self.y = b("y_heads", [P, 256])
        self.one_silu = b("one_silu", [P, 1])
        self.logit = b("logit", [P, 4, EXPERTS + 1])
        self.left = b("left", [P, 4, EXPERTS])
        self.best = b("best", [P, 4, TOP])
        self.weight = b("weight", [P, 4, EXPERTS])
        self.wtotal = b("wtotal", [P, 4])
        self.winv = b("winv", [P, 4])
        self.sig = b("sig", [P, 4])
        self.wn = b("wn", [P, 4, 2 * EXPERTS], FR)
        self.sn = b("sn", [P, 4, 2], FR)
        self.banks = banks
        self.qk_ready = k.sem("qk_ready_h")
        self.v_ready = k.sem("v_ready_h")
        self.v_out = k.sem("v_out_h")
        self.rotated = k.sem("rotated_h")
        self.roped = k.sem("roped_h")
        self.prod_pool = k.sem("prod_pool_h")
        self.prod_dve = k.sem("prod_dve_h")
        self.summed_score = k.sem("summed_score_h")
        self.lowered = k.sem("lowered_h")
        self.prob_ready = k.sem("prob_ready_h")
        self.pv_pool = k.sem("pv_pool_h")
        self.pv_dve = k.sem("pv_dve_h")
        self.totaled = k.sem("totaled_h")
        self.silu_loaded = k.sem("silu_loaded_h")
        self.pv_merged = k.sem("pv_merged_h")
        self.pv_added = k.sem("pv_added_h")
        self.a_ready = k.sem("a_ready_h")
        self.aT_ready = k.sem("aT_ready_h")
        self.ah_ready = k.sem("ah_ready_h")
        self.al_ready = k.sem("al_ready_h")
        self.o_ready = k.sem("o_ready_h")
        self.residual = k.sem("residual_h")
        self.x_new = k.sem("x_new_h")
        self.xT_ready = k.sem("xT_ready_h")
        self.xh_out = k.sem("xh_out_h")
        self.xl_out = k.sem("xl_out_h")
        self.l_ready = k.sem("l_ready_h")
        self.l_out = k.sem("l_out_h")
        self.best_ready = k.sem("best_ready_h")
        self.replaced = k.sem("replaced_h")
        self.w_lowered = k.sem("w_lowered_h")
        self.exp_ready = k.sem("exp_ready_h")
        self.w_split = k.sem("w_split_h")
        self.w_turned = k.sem("w_turned_h")
        self.s_turned = k.sem("s_turned_h")
        self.w_out = k.sem("w_out_h")
        self.s_out = k.sem("s_out_h")
        self.v_chain = k.sem("v_chain_h")
        self.silus = 0
        self.order = self._bank_order()

    def bank(self, kind, t):
        return self.banks[self.bank_no(kind, t)]

    def bank_no(self, kind, t):
        return LEAD_BANKS[kind] if t < 4 and kind in LEAD_BANKS else BANKS[kind]

    def _bank_order(self):
        uses = {0: [], 1: [], 2: []}
        for t, s in enumerate(self.starts):
            for place, (kind, step) in enumerate((("qk", "project"), ("v", "project"), ("aT", "turn_a"), ("o", "output"),
                                                  ("xT", "turn_x"), ("logit", "logits"))):
                uses[self.bank_no(kind, t)].append((s + plan(t)[step], place, kind, t))
            if t % 4 == 3:
                for kind, r in (("wT", 3), ("sT", 5)):
                    uses[BANKS[kind]].append((self.routed[t // 4] - ROUTE_LEN + r, 6, kind, t // 4))
        before = {}
        for lst in uses.values():
            lst.sort()
            for i, (_, _, kind, t) in enumerate(lst):
                before[kind, t] = lst[i - 1][2:] if i else None
        return before

    def wait_bank(self, pe, kind, t):
        prev = self.order[kind, t]
        if prev is None:
            return
        what, u = prev
        sem, per = {"qk": (self.rotated, 4), "v": (self.v_out, 1), "aT": (self.al_ready, 1), "o": (self.residual, 1),
                    "xT": (self.xl_out, 1), "logit": (self.l_out, 1), "wT": (self.w_out, 1), "sT": (self.s_out, 1)}[what]
        pe.wait_ge(sem, per * (u + 1))

    def at(self, slot):
        tiles = [(t, [step for step, r in plan(t).items() if slot - s == r]) for t, s in enumerate(self.starts)
                 if 0 <= slot - s <= max(plan(t).values())]
        chunks = [(ch, slot - (end - ROUTE_LEN)) for ch, end in enumerate(self.routed) if end - ROUTE_LEN <= slot < end]
        return tiles, chunks

    def pe(self, pe, slot):
        tiles, chunks = self.at(slot)
        for step, make in (("project", self._project), ("turn_a", self._turn_a), ("output", self._output),
                           ("turn_x", self._turn_x), ("logits", self._logits)):
            for t, steps in tiles:
                if step in steps:
                    make(pe, t)
        for ch, r in chunks:
            if r == 3:
                pe.wait_ge(self.w_split, 4 * (ch + 1))
                self.wait_bank(pe, "wT", ch)
                if ch >= 2:
                    pe.wait_ge(self.sums_read, 2 * (ch - 1))
                for j in range(4):
                    mm = pe.transpose(self.bank("wT", ch)[:, P * j:P * j + P], self.wn[:, j, :].bitcast(F32), self.ident[:])
                mm.then_inc(self.w_turned, 1)
            if r == 5:
                pe.wait_ge(self.w_split, 4 * (ch + 1))
                self.wait_bank(pe, "sT", ch)
                for j in range(4):
                    mm = pe.transpose(self.bank("sT", ch)[0:2, P * j:P * j + P], self.sn[:, j, :].bitcast(F32), self.ident[:])
                mm.then_inc(self.s_turned, 1)

    def _project(self, pe, t):
        ts = slice(P * t, P * t + P)
        pe.wait_ge(self.x_split, t // 2 + 1)
        mms = [(x, w, kc) for kc in range(2) for x, w in ((self.XH, self.wh), (self.XL, self.wh), (self.XH, self.wl))]
        for kind, cols, width, done in (("qk", slice(0, 512), 512, self.qk_ready), ("v", slice(512, 768), 256, self.v_ready)):
            self.wait_bank(pe, kind, t)
            for n, (x, w, kc) in enumerate(mms):
                mm = pe.matmul(self.bank(kind, t)[:, 0:width], x[:, kc, ts], w[:, kc, cols], start=n == 0, stop=n == 5)
            mm.then_inc(done, 1)

    def _turn_a(self, pe, t):
        pe.wait_ge(self.a_ready, t + 1)
        self.wait_bank(pe, "aT", t)
        for kc in range(2):
            mm = pe.transpose(self.bank("aT", t)[:, P * kc:P * kc + P],
                              self.a[:, t % 2, 8 * kc:8 * kc + 8, :].rearrange("p h n -> p (h n)"), self.ident[:])
        mm.then_inc(self.aT_ready, 1)

    def _output(self, pe, t):
        pe.wait_ge(self.al_ready, t + 1)
        self.wait_bank(pe, "o", t)
        mms = [(x, w, kc) for kc in range(2) for x, w in ((self.ah, self.woh), (self.al, self.woh), (self.ah, self.wol))]
        for n, (x, w, kc) in enumerate(mms):
            mm = pe.matmul(self.bank("o", t)[:, 0:256], x[:, kc, :], w[:, kc, :], start=n == 0, stop=n == 5)
        mm.then_inc(self.o_ready, 1)

    def _turn_x(self, pe, t):
        pe.wait_ge(self.x_new, t + 1)
        self.wait_bank(pe, "xT", t)
        for kc in range(2):
            mm = pe.transpose(self.bank("xT", t)[:, P * kc:P * kc + P], self.X[:, t, P * kc:P * kc + P], self.ident[:])
        mm.then_inc(self.xT_ready, 1)

    def _logits(self, pe, t):
        pe.wait_ge(self.xl_out, t + 1)
        self.wait_bank(pe, "logit", t)
        mms = [(x, w, kc) for kc in range(2) for x, w in ((self.XH, self.rh), (self.XL, self.rh), (self.XH, self.rl))]
        for n, (x, w, kc) in enumerate(mms):
            mm = pe.matmul(self.bank("logit", t)[:, 0:EXPERTS + 2], x[:, kc, P * t:P * t + P], w[:, kc, :],
                           start=n == 0, stop=n == 5)
        mm.then_inc(self.l_ready, 1)

    def load_silu(self, act, slot):
        tiles, chunks = self.at(slot)
        if any("exp" in steps for _, steps in tiles) or any(r == 0 for _, r in chunks):
            if self.silus:
                act.wait_ge(self.silu_loaded, self.silus)
            self.nc.scalar.activation(self.one_silu[:], self.ident[:, 0:1], ACT.Silu).then_inc(self.silu_loaded, 1)
            self.silus += 1

    def act(self, act, slot):
        nc = self.nc
        tiles, chunks = self.at(slot)
        for t, steps in tiles:
            if "v_out" in steps:
                act.wait_ge(self.v_ready, t + 1)
                if t >= 3:
                    act.wait_ge(self.pv_pool, 2 * (t - 2))
                    act.wait_ge(self.pv_dve, t - 2)
                nc.scalar.copy(self.v[:, t % 3], self.bank("v", t)[:, 0:256].rearrange("p (h n) -> p h n", h=HEADS)).then_inc(self.v_out, 1)
            if "exp" in steps:
                act.wait_ge(self.lowered, t + 1)
                if t >= 1:
                    act.wait_ge(self.pv_pool, 2 * t)
                    act.wait_ge(self.pv_dve, t)
                    act.wait_ge(self.totaled, t)
                nc.scalar.activation(self.prob[:], self.shifted[:], ACT.Exp, scale=HD ** -0.5).then_inc(self.prob_ready, 1)
            if "a_high" in steps:
                act.wait_ge(self.aT_ready, t + 1)
                if t >= 1:
                    act.wait_ge(self.o_ready, t)
                nc.scalar.copy(self.ah[:], self.bank("aT", t)[:, 0:256].rearrange("p (c n) -> p c n", c=2)).then_inc(self.ah_ready, 1)
            if "x_high" in steps:
                act.wait_ge(self.xT_ready, t + 1)
                nc.scalar.copy(self.XH[:, :, P * t:P * t + P],
                               self.bank("xT", t)[:, 0:256].rearrange("p (c n) -> p c n", c=2)).then_inc(self.xh_out, 1)
            if "logits_out" in steps:
                act.wait_ge(self.l_ready, t + 1)
                if t >= 4 and t % 4 == 0:
                    act.wait_ge(self.w_split, t)
                nc.scalar.copy(self.logit[:, t % 4, :], self.bank("logit", t)[:, 0:EXPERTS + 1]).then_inc(self.l_out, 1)
        for ch, r in chunks:
            if r == 0:
                act.wait_ge(self.w_lowered, ch + 1)
                act.wait_ge(self.l_out, 4 * (ch + 1))
                nc.scalar.activation(self.weight[:], self.weight[:], ACT.Exp).then_inc(self.exp_ready, 1)
                nc.scalar.activation(self.sig[:], self.logit[:, :, EXPERTS], ACT.Exp, scale=-1.0).then_inc(self.exp_ready, 1)
            cols = slice(512 * (ch % 2), 512 * (ch % 2) + 512)
            if r in (4, 5) and ch >= 2:
                act.wait_ge(self.spread, (PAIRS + 1) * (ch - 1))
            if r == 4:
                act.wait_ge(self.w_turned, ch + 1)
                nc.scalar.copy(self.WT[:, cols], self.bank("wT", ch)[:]).then_inc(self.w_out, 1)
            if r == 5:
                act.wait_ge(self.s_turned, ch + 1)
                nc.scalar.copy(self.WS[:, cols], self.bank("sT", ch)[0:2, :]).then_inc(self.s_out, 1)

    def _score_product(self, eng, lo, hi):
        shape = [P, hi - lo, HEADS, HD]
        return eng.tensor_tensor(self.prod[:, lo:hi], self.rope[:, lo:hi, :].unsqueeze(2).broadcast_to(shape),
                                 self.rope[:, HEADS:2 * HEADS, :].unsqueeze(1).broadcast_to(shape), ALU.mult)

    def _value_product(self, eng, t, lo, hi):
        shape = [P, hi - lo, HEADS, HD]
        return eng.tensor_tensor(self.pv[:, lo:hi], self.v[:, t % 3, lo:hi, :].unsqueeze(2).broadcast_to(shape),
                                 self.prob[:, :, lo:hi].rearrange("p h t -> p t h").unsqueeze(3).broadcast_to(shape), ALU.mult)

    def pool(self, pool, slot):
        tiles, _ = self.at(slot)
        for t, steps in tiles:
            for i in range(3):
                if f"score{i}" in steps:
                    if i == 0:
                        pool.wait_ge(self.roped, 2 * (t + 1))
                    if t >= 1:
                        pool.wait_ge(self.summed_score, 4 * (t - 1) + 1 + i)
                    self._score_product(self.nc.gpsimd, 4 * i, 4 * i + 4).then_inc(self.prod_pool, 1)
            for i in range(2):
                if f"value{i}" in steps:
                    if i == 0:
                        pool.wait_ge(self.prob_ready, t + 1)
                        pool.wait_ge(self.v_out, t + 1)
                        if t >= 1:
                            pool.wait_ge(self.pv_added, 2 * t)
                    heads = self.VALUE_HEADS
                    self._value_product(self.nc.gpsimd, t, heads * i, heads * (i + 1)).then_inc(self.pv_pool, 1)
            if "merge" in steps:
                pool.wait_ge(self.pv_pool, 2 * (t + 1))
                self.nc.gpsimd.tensor_tensor(self.pv[:, 4:8], self.pv[:, 0:4], self.pv[:, 4:8], ALU.add).then_inc(self.pv_merged, 1)
            if "power" in steps:
                self.norm.power(pool, t)

    @staticmethod
    def wide(x):
        return x.unsqueeze(2).broadcast_to([P, 4, EXPERTS])

    def start_vector(self, dve):
        self.link = chained(dve, self.v_chain)

    EARLY = {"rotate", "rope", "score_dve", "sum0", "sum1", "sum2", "lower"}

    def dve(self, dve, slot, part=None):
        nc, link = self.nc, self.link
        tiles, chunks = self.at(slot)
        if part is not None:
            tiles = [(t, [step for step in steps if (step in self.EARLY) == (part == 0)]) for t, steps in tiles]
            chunks = chunks if part == 1 else []
        for t, steps in tiles:
            if "rotate" in steps:
                dve.wait_ge(self.qk_ready, t + 1)
                if t >= 1:
                    dve.wait_ge(self.roped, 2 * t)
                qk = self.bank("qk", t)[:].rearrange("p (h n two) -> p h n two", n=8, two=2)
                cb = self.cos[:, t % self.ST, :].unsqueeze(1).broadcast_to([P, 2 * HEADS, 8])
                sb = self.sin[:, t % self.ST, :].unsqueeze(1).broadcast_to([P, 2 * HEADS, 8])
                for m, (x, f) in enumerate(((0, cb), (1, sb), (0, sb), (1, cb))):
                    nc.vector.tensor_tensor(self.rt[:, m], qk[:, :, :, x], f, ALU.mult).then_inc(self.rotated, 1)
            if "rope" in steps:
                dve.wait_ge(self.rotated, 4 * (t + 1))
                if t >= 1:
                    dve.wait_ge(self.prod_pool, 3 * t)
                    dve.wait_ge(self.prod_dve, t)
                nc.vector.tensor_tensor(self.rope[:, :, 0:8], self.rt[:, 0], self.rt[:, 1], ALU.subtract).then_inc(self.roped, 1)
                nc.vector.tensor_tensor(self.rope[:, :, 8:16], self.rt[:, 2], self.rt[:, 3], ALU.add).then_inc(self.roped, 1)
            if "score_dve" in steps:
                dve.wait_ge(self.roped, 2 * (t + 1))
                if t >= 1:
                    dve.wait_ge(self.summed_score, 4 * t)
                self._score_product(nc.vector, 12, 16).then_inc(self.prod_dve, 1)
            for i in range(3):
                if f"sum{i}" in steps:
                    dve.wait_ge(self.prod_pool, 3 * t + i + 1)
                    if i == 0 and t >= 1:
                        dve.wait_ge(self.lowered, t)
                    h = slice(4 * i, 4 * i + 4)
                    nc.vector.tensor_reduce(self.score[:, h], self.prod[:, h], AX.X, ALU.add).then_inc(self.summed_score, 1)
            if "lower" in steps:
                dve.wait_ge(self.prod_dve, t + 1)
                nc.vector.tensor_reduce(self.score[:, 12:16], self.prod[:, 12:16], AX.X, ALU.add).then_inc(self.summed_score, 1)
                dve.wait_ge(self.summed_score, 4 * (t + 1))
                link(nc.vector.tensor_reduce(self.nmax[:], self.score[:], AX.X, ALU.max, negate=True))
                if t >= 1:
                    dve.wait_ge(self.prob_ready, t)
                nc.vector.tensor_tensor(self.shifted[:], self.score[:], self.nmax[:].unsqueeze(2).broadcast_to([P, HEADS, HEADS]),
                                        ALU.add).then_inc(self.lowered, 1)
            if "value_dve" in steps:
                dve.wait_ge(self.prob_ready, t + 1)
                dve.wait_ge(self.v_out, t + 1)
                if t >= 1:
                    dve.wait_ge(self.a_ready, t)
                self._value_product(nc.vector, t, 12, 16).then_inc(self.pv_dve, 1)
                nc.vector.tensor_reduce(self.total[:], self.prob[:], AX.X, ALU.add).then_inc(self.totaled, 1)
                dve.wait_ge(self.totaled, t + 1)
                link(nc.vector.reciprocal(self.inv[:], self.total[:]))
            for i, heads in enumerate((slice(8, 12), slice(4, 8))):
                if f"add{i}" in steps:
                    if i == 0:
                        dve.wait_ge(self.pv_pool, 2 * (t + 1))
                        dve.wait_ge(self.pv_dve, t + 1)
                    else:
                        dve.wait_ge(self.pv_merged, t + 1)
                        dve.wait_ge(self.pv_added, 2 * t + 1)
                    nc.vector.tensor_tensor(self.pv[:, 12:16], self.pv[:, 12:16], self.pv[:, heads], ALU.add).then_inc(self.pv_added, 1)
            if "attend" in steps:
                dve.wait_ge(self.pv_added, 2 * (t + 1))
                link(nc.vector.tensor_tensor(self.pv[:, 12:14], self.pv[:, 12:14], self.pv[:, 14:16], ALU.add))
                link(nc.vector.tensor_tensor(self.pv[:, 12], self.pv[:, 12], self.pv[:, 13], ALU.add))
                if t >= 2:
                    dve.wait_ge(self.aT_ready, t - 1)
                nc.vector.tensor_tensor(self.a[:, t % 2], self.pv[:, 12], self.inv[:].unsqueeze(2).broadcast_to([P, HEADS, HD]),
                                        ALU.mult).then_inc(self.a_ready, 1)
            if "a_low" in steps:
                dve.wait_ge(self.ah_ready, t + 1)
                if t >= 1:
                    dve.wait_ge(self.o_ready, t)
                nc.vector.tensor_tensor(self.al[:], self.bank("aT", t)[:, 0:256].rearrange("p (c n) -> p c n", c=2),
                                        self.ah[:].bitcast(F32), ALU.subtract).then_inc(self.al_ready, 1)
            if "residual" in steps:
                dve.wait_ge(self.o_ready, t + 1)
                if t >= 1:
                    dve.wait_ge(self.x_new, t)
                nc.vector.tensor_tensor(self.y[:], self.bank("o", t)[:, 0:256], self.X[:, t, :], ALU.add).then_inc(self.residual, 1)
                dve.wait_ge(self.residual, t + 1)
                self.norm.statistics(t, self.y[:], link)
            if "scale" in steps:
                self.norm.scale(dve, t, self.X[:, t, :], self.y[:]).then_inc(self.x_new, 1)
            if "x_low" in steps:
                dve.wait_ge(self.xh_out, t + 1)
                nc.vector.tensor_tensor(self.XL[:, :, P * t:P * t + P], self.bank("xT", t)[:, 0:256].rearrange("p (c n) -> p c n", c=2),
                                        self.XH[:, :, P * t:P * t + P].bitcast(F32), ALU.subtract).then_inc(self.xl_out, 1)
            if "best" in steps:
                j = t % 4
                dve.wait_ge(self.l_out, t + 1)
                nc.vector.max(self.best[:, j, :], self.logit[:, j, 0:EXPERTS]).then_inc(self.best_ready, 1)
                dve.wait_ge(self.best_ready, t + 1)
                nc.vector.match_replace(self.left[:, j, :], self.best[:, j, :], self.logit[:, j, 0:EXPERTS], LOWEST).then_inc(self.replaced, 1)
                if j == 3:
                    dve.wait_ge(self.replaced, t + 1)
                    nc.vector.tensor_tensor(self.weight[:], self.logit[:, :, 0:EXPERTS], self.wide(self.best[:, :, 0]),
                                            ALU.subtract).then_inc(self.w_lowered, 1)
                    link(nc.vector.tensor_tensor(self.left[:], self.left[:], self.logit[:, :, 0:EXPERTS], ALU.not_equal))
        for ch, r in chunks:
            if r == 1:
                dve.wait_ge(self.exp_ready, 2 * (ch + 1))
                if ch:
                    dve.wait_ge(self.w_turned, ch)
                    dve.wait_ge(self.s_turned, ch)
                link(nc.vector.tensor_tensor(self.weight[:], self.weight[:], self.left[:], ALU.mult))
                link(nc.vector.tensor_reduce(self.wtotal[:], self.weight[:], AX.X, ALU.add))
                link(nc.vector.reciprocal(self.winv[:], self.wtotal[:]))
                link(nc.vector.tensor_tensor(self.weight[:], self.weight[:], self.wide(self.winv[:]), ALU.mult))
            if r == 2:
                link(nc.vector.tensor_scalar(self.sig[:], self.sig[:], 1.0, None, ALU.add))
                link(nc.vector.reciprocal(self.sig[:], self.sig[:]))
                nc.vector.tensor_copy(self.wn[:, :, 0:EXPERTS], self.weight[:]).then_inc(self.w_split, 1)
                nc.vector.tensor_copy(self.sn[:, :, 0], self.sig[:]).then_inc(self.w_split, 1)
                dve.wait_ge(self.w_split, 4 * ch + 2)
                nc.vector.tensor_tensor(self.wn[:, :, EXPERTS:2 * EXPERTS], self.weight[:],
                                        self.wn[:, :, 0:EXPERTS].bitcast(F32), ALU.subtract).then_inc(self.w_split, 1)
                nc.vector.tensor_tensor(self.sn[:, :, 1], self.sig[:], self.sn[:, :, 0].bitcast(F32), ALU.subtract).then_inc(self.w_split, 1)
                dve.wait_ge(self.w_split, 4 * ch + 4)


def stage_attention_to_experts(k, d, attention, XH, XL, X, ident, half, cos, sin, wh, wl, woh, wol, rh, rl, wg, wu, wd, s_gu, s_down, out):
    nc = k.nc
    H, T = 256, X.shape[1]
    NCH = T // 4
    STEPS = PAIRS + 1
    N = NCH * STEPS
    RING = 3
    GATES = 3
    COLS = 2 * 256 + 256 + P
    with ExitStack() as c:
        gated = k.sb("gated_experts", [P, 2, 512], F32, c)
        inter = k.sb("inter", [P, 2, 512], F32, c)
        ih = k.sb("ih", [P, 2, 512], FR, c)
        il = k.sb("il", [P, 2, 512], FR, c)
        acc = k.sb("acc", [P, 2, 512], F32, c)
        y = k.sb("y_experts", [P, 4, H], F32, c)
        WT = k.sb("WT", [P, 2 * 512], FR, c)
        WS = k.sb("WS", [2, 2 * 512], FR, c)
        w = k.sb("w_experts", [P, RING, COLS], F32, c)
        ones = k.sb("ones_experts", [2, P], FR, c)
        guh = k.sb("guh", [P, GATES, 512], FR, c)
        gul = k.sb("gul", [P, GATES, 512], FR, c)
        dh = k.sb("dh", [P, 2, 256], FR, c)
        dl = k.sb("dl", [P, 2, 256], FR, c)
        sel = k.sb("sel", [P, GATES, P], FR, c)
        weighted = k.sb("weighted", [P, 512], F32, c)
        ps = [c.enter_context(nc.psum_tensor(f"bank{i}", [P, 512], F32)) for i in range(8)]
        p_g, p_u, p_y, p_w, p_t = ps[0], ps[1], ps[2:4], ps[4], ps[7]
        def sem(name):
            return k.sem(name + "_experts")

        w_ready, summed = sem("w_ready"), sem("summed")
        ffn = FeedForward(k, c, d, XH, XL, X, ident, half, wg, wu, wd, s_gu, s_down, gated, inter, ih, il, acc, y,
                          (p_g, p_u, p_y, p_w))
        heads = Heads(k, c, d, XH, XL, X, ident, half, cos, sin, wh, wl, woh, wol, rh, rl, WT, WS, ps[5:8], ffn.xl_out, w_ready, summed)
        starts, routed = slots_of(T)
        HEADS_AT = ffn.IT + ffn.TAIL - 1
        FIRST = HEADS_AT + routed[0]
        assert FIRST >= ffn.END and all(s >= ffn.IT * (t // 4) for t, s in enumerate(starts))
        assert all(r <= routed[0] + STEPS * ch for ch, r in enumerate(routed))
        SPLIT_AHEAD = 3
        T0 = attention.T
        norm = Norm(k, c, half, "experts")
        w_in = [sem(f"w_in{i}") for i in range(RING)]
        ones_set, sel_ready = sem("ones_set"), sem("sel_ready")
        guh_ready, dh_ready, gul_ready, dl_ready = sem("guh_ready"), sem("dh_ready"), sem("gul_ready"), sem("dl_ready")
        g_ready, u_ready, down_done = sem("g_ready"), sem("u_ready"), sem("down_done")
        gated_ready, weighted_ready, inter_ready = sem("gated_ready"), sem("weighted_ready"), sem("inter_ready")
        ih_ready, il_ready, acc_out = sem("ih_ready"), sem("il_ready"), sem("acc_out")
        turned, x_out, stored = sem("turned"), sem("x_out"), sem("stored")

        def ended(n):
            ch, p = divmod(n, STEPS)
            return ch - 1, (p if ch else None)

        with nc.Block() as block:
            def store(sp, ch, r):
                t = 4 * ch + 2 * r
                sp.wait_ge(x_out, t + 2)
                sp.dma_start(out[P * t:P * (t + 2), :].rearrange("(t p) n -> p t n", p=P), y[:, 2 * r:2 * r + 2, :]).then_inc(stored, 16)

            @block.sync
            def _(sp):
                attention.prepare.load_weights(sp)
                sp.wait_ge(attention.xl_out, T)
                for n in range(N):
                    if n >= RING:
                        m = n - RING + 1
                        sp.wait_ge(sel_ready, m)
                        sp.wait_ge(gul_ready, m)
                        sp.wait_ge(dl_ready, m)
                    sp.dma_start(w[:, n % RING, :], d["experts"][n % STEPS]).then_inc(w_in[n % RING], 16)
                    ch, p = ended(n - RING - 1)
                    if p in (4, 6):
                        store(sp, ch, (p - 4) // 2)
                for r in range(2):
                    store(sp, NCH - 1, r)
                sp.wait_ge(stored, 16 * T // 2)

            @block.scalar
            def _(act):
                def split_down(n):
                    if n < N:
                        act.wait_ge(w_in[n % RING], 16 * (n // RING + 1))
                        if n >= 2:
                            act.wait_ge(down_done, n - 1)
                        nc.scalar.copy(dh[:, n % 2], w[:, n % RING, 512:768]).then_inc(dh_ready, 1)

                def split_gates(n):
                    if n < N:
                        act.wait_ge(w_in[n % RING], 16 * (n // RING + 1))
                        if n >= GATES:
                            act.wait_ge(u_ready, n - GATES + 1)
                        nc.scalar.copy(sel[:, n % GATES, :], w[:, n % RING, 768:COLS]).then_inc(sel_ready, 1)
                        nc.scalar.copy(guh[:, n % GATES], w[:, n % RING, 0:512]).then_inc(guh_ready, 1)

                def evacuate():
                    for i in range(2):
                        nc.scalar.copy(acc[:, i, :], p_y[i][:]).then_inc(acc_out, 1)

                for slot in range(-T0, FIRST):
                    attention.act(act, slot + T0)
                    if slot < 0:
                        continue
                    ffn.act(act, slot)
                    heads.act(act, slot - HEADS_AT)
                    if slot < ffn.M or slot >= FIRST - SPLIT_AHEAD:
                        heads.load_silu(act, slot - HEADS_AT)
                    if slot == FIRST - SPLIT_AHEAD:
                        split_gates(0)
                        split_down(0)
                        split_gates(1)
                for n in range(N):
                    act.wait_ge(g_ready, n + 1)
                    if n >= 2:
                        act.wait_ge(weighted_ready, n - 1)
                    nc.scalar.activation(gated[:, n % 2, :], p_g[:], ACT.Silu).then_inc(gated_ready, 1)
                    split_down(n + 1)
                    split_gates(n + 2)
                    act.wait_ge(inter_ready, n + 1)
                    if n >= 2:
                        act.wait_ge(down_done, n - 1)
                    nc.scalar.copy(ih[:, n % 2, :], inter[:, n % 2, :]).then_inc(ih_ready, 1)
                    if n % STEPS == 0 and n:
                        act.wait_ge(down_done, n)
                        if n > STEPS:
                            act.wait_ge(turned, 2 * (n // STEPS - 1))
                        evacuate()
                    heads.act(act, FIRST + n - HEADS_AT)
                    heads.load_silu(act, FIRST + n - HEADS_AT)
                act.wait_ge(down_done, N)
                act.wait_ge(turned, 2 * (NCH - 1))
                nc.scalar.copy(acc[:, 0, :], p_y[0][:]).then_inc(acc_out, 1)

            @block.gpsimd
            def _(pool):
                def split_down(n):
                    if n < N:
                        pool.wait_ge(dh_ready, n + 1)
                        if n >= 2:
                            pool.wait_ge(down_done, n - 1)
                        nc.gpsimd.tensor_tensor(dl[:, n % 2], w[:, n % RING, 512:768], dh[:, n % 2].bitcast(F32),
                                                ALU.subtract).then_inc(dl_ready, 1)

                def split_gates(n):
                    if n < N:
                        pool.wait_ge(guh_ready, n + 1)
                        if n >= GATES:
                            pool.wait_ge(u_ready, n - GATES + 1)
                        nc.gpsimd.tensor_tensor(gul[:, n % GATES], w[:, n % RING, 0:512], guh[:, n % GATES].bitcast(F32),
                                                ALU.subtract).then_inc(gul_ready, 1)

                for slot in range(-T0, FIRST):
                    attention.pool(pool, slot + T0)
                    if slot < 0:
                        continue
                    ffn.pool(pool, slot)
                    heads.pool(pool, slot - HEADS_AT)
                    if slot == FIRST - SPLIT_AHEAD + 1:
                        split_gates(0)
                    if slot == FIRST - SPLIT_AHEAD + 2:
                        split_down(0)
                        split_gates(1)
                for n in range(N):
                    split_down(n + 1)
                    ch, p = ended(n)
                    if p in (2, 3, 4, 5):
                        norm.power(pool, 4 * ch + p - 2)
                    split_gates(n + 2)
                    heads.pool(pool, FIRST + n - HEADS_AT)
                for t in range(T - 4, T):
                    norm.power(pool, t)

            @block.vector
            def _(dve):
                heads.start_vector(dve)
                link = heads.link

                def step(n):
                    i = n % 2
                    dve.wait_ge(gated_ready, n + 1)
                    dve.wait_ge(w_ready, n + 1)
                    if n >= 1:
                        dve.wait_ge(inter_ready, n)
                    nc.vector.tensor_tensor(weighted[:], gated[:, i, :], p_w[:], ALU.mult).then_inc(weighted_ready, 1)
                    dve.wait_ge(weighted_ready, n + 1)
                    dve.wait_ge(u_ready, n + 1)
                    if n >= 2:
                        dve.wait_ge(ih_ready, n - 1)
                        dve.wait_ge(il_ready, n - 1)
                    nc.vector.tensor_tensor(inter[:, i, :], weighted[:], p_u[:], ALU.mult).then_inc(inter_ready, 1)

                def low(n):
                    i = n % 2
                    dve.wait_ge(ih_ready, n + 1)
                    if n >= 2:
                        dve.wait_ge(down_done, n - 1)
                    nc.vector.tensor_tensor(il[:, i, :], inter[:, i, :], ih[:, i, :].bitcast(F32), ALU.subtract).then_inc(il_ready, 1)

                def residual(ch, r, bank):
                    t = 4 * ch + 2 * r
                    dve.wait_ge(turned, 2 * ch + r + 1)
                    if ch:
                        dve.wait_ge(stored, 16 * (2 * ch - 1 + r))
                    nc.vector.tensor_tensor(y[:, 2 * r:2 * r + 2, :], bank[:].rearrange("p (t n) -> p t n", t=2), X[:, t:t + 2, :],
                                            ALU.add).then_inc(summed, 1)
                    dve.wait_ge(summed, 2 * ch + r + 1)

                def statistics(ch, j):
                    norm.statistics(4 * ch + j, y[:, j, :], link)

                def scale(ch, j):
                    norm.scale(dve, 4 * ch + j, y[:, j, :], y[:, j, :]).then_inc(x_out, 1)

                for slot in range(-T0, FIRST):
                    attention.dve(dve, slot + T0, link)
                    if slot < 0:
                        continue
                    if slot == ffn.END:
                        link(nc.vector.memset(ones[:].bitcast(F32), 1.0))
                        nc.vector.tensor_copy(ones[:], ones[:].bitcast(F32)).then_inc(ones_set, 1)
                    ffn.dve_fuse(dve, slot)
                    ffn.dve_end(dve, slot, link)
                    heads.dve(dve, slot - HEADS_AT)
                for n in range(N):
                    step(n)
                    heads.dve(dve, FIRST + n - HEADS_AT, 0)
                    low(n)
                    ch, p = ended(n)
                    if p in (2, 4):
                        residual(ch, (p - 2) // 2, p_t)
                    if p in (2, 3, 4, 5):
                        statistics(ch, p - 2)
                    if p in (3, 4, 5, 6):
                        scale(ch, p - 3)
                    heads.dve(dve, FIRST + n - HEADS_AT, 1)
                dve.wait_ge(down_done, N)
                dve.wait_ge(turned, 2 * (NCH - 1))
                nc.vector.tensor_copy(acc[:, 1, :], p_y[1][:]).then_inc(acc_out, 1)
                residual(NCH - 1, 0, p_t)
                statistics(NCH - 1, 0)
                statistics(NCH - 1, 1)
                residual(NCH - 1, 1, p_w)
                scale(NCH - 1, 0)
                scale(NCH - 1, 1)
                statistics(NCH - 1, 2)
                statistics(NCH - 1, 3)
                scale(NCH - 1, 2)
                scale(NCH - 1, 3)

            @block.tensor
            def _(pe):
                def gates(n):
                    ch, p = divmod(n, STEPS)
                    i, s, ws = n % GATES, slice(512 * ch, 512 * ch + 512), slice(512 * (ch % 2), 512 * (ch % 2) + 512)
                    if p == 0:
                        pe.wait_ge(heads.xl_out, 4 * (ch + 1))
                    pe.wait_ge(gul_ready, n + 1)

                    def product(dst, freed, o, done):
                        if n >= 1:
                            pe.wait_ge(freed, n)
                        mms = [(wt, x, kc) for kc in range(2) for wt, x in ((guh, XH), (guh, XL), (gul, XH))]
                        for m, (wt, x, kc) in enumerate(mms):
                            mm = pe.matmul(dst[:], wt[:, i, 256 * kc + o:256 * kc + o + P], x[:, kc, s], start=m == 0, stop=m == 5)
                        mm.then_inc(done, 1)

                    product(p_g, gated_ready, 0, g_ready)
                    if n >= 1:
                        pe.wait_ge(weighted_ready, n)
                    pe.wait_ge(sel_ready, n + 1)
                    if p == 0:
                        pe.wait_ge(heads.w_out, ch + 1)
                    if p < PAIRS:
                        pe.matmul(p_w[:], sel[:, i, :], WT[:, ws], start=True, stop=True).then_inc(w_ready, 1)
                    else:
                        pe.wait_ge(ones_set, 1)
                        pe.wait_ge(heads.s_out, ch + 1)
                        pe.matmul(p_w[:], ones[:], WS[:, ws], start=True, stop=True).then_inc(w_ready, 1)
                    product(p_u, inter_ready, P, u_ready)

                def down(n):
                    i, p, ch = n % 2, n % STEPS, n // STEPS
                    pe.wait_ge(dl_ready, n + 1)
                    pe.wait_ge(il_ready, n + 1)
                    if p == 0 and ch:
                        pe.wait_ge(acc_out, 2 * ch)
                    for hc in range(2):
                        for m, (wt, x) in enumerate(((dh, ih), (dh, il), (dl, ih))):
                            mm = pe.matmul(p_y[hc][:], wt[:, i, P * hc:P * hc + P], x[:, i, :],
                                           start=p == 0 and m == 0, stop=p == STEPS - 1 and m == 2)
                    mm.then_inc(down_done, 1)

                def turn(ch, r, bank):
                    pe.wait_ge(acc_out, 2 * (ch + 1))
                    if r and bank is p_t:
                        pe.wait_ge(summed, 2 * ch + 1)
                    for j in range(2):
                        for hc in range(2):
                            mm = pe.transpose(bank[:, 256 * j + P * hc:256 * j + P * hc + P],
                                              acc[:, hc, P * (2 * r + j):P * (2 * r + j) + P], ident[:])
                    mm.then_inc(turned, 1)

                for slot in range(-T0, FIRST):
                    if slot < 0:
                        attention.pe(pe, slot + T0)
                        continue
                    if slot % ffn.IT == 0 and slot < ffn.M:
                        pe.wait_ge(attention.xl_out, 4 * (slot // ffn.IT + 1))
                    if slot == 0:
                        pe.wait_ge(attention.prob_ready, T - 1)
                    if slot == 1:
                        pe.wait_ge(attention.prob_ready, T)
                    ffn.pe_gates(pe, slot)
                    attention.pe(pe, slot + T0)
                    ffn.pe_down(pe, slot - 1)
                    ffn.pe_end(pe, slot)
                    if slot == ffn.END:
                        pe.wait_ge(ffn.xl_out, 2 * ffn.NCH)
                    heads.pe(pe, slot - HEADS_AT)
                for n in range(N):
                    gates(n)
                    if n:
                        down(n - 1)
                    ch, p = ended(n)
                    if p in (1, 3):
                        turn(ch, (p - 1) // 2, p_t)
                    heads.pe(pe, FIRST + n - HEADS_AT)
                down(N - 1)
                turn(NCH - 1, 0, p_t)
                pe.wait_ge(weighted_ready, N)
                turn(NCH - 1, 1, p_w)


def build(nc, d, out):
    T = 16
    H = 256
    with ExitStack() as ctx:
        k = Core(nc, ctx)
        X = k.sb("X", [P, T, H], F32)
        XH = k.sb("XH", [P, 2, T * P], FR)
        XL = k.sb("XL", [P, 2, T * P], FR)
        ident = k.sb("ident", [P, P], F32)
        half = k.sb("half", [P, 1], F32)
        cos, sin = (k.sb(n, [P, 8, 8], F32) for n in ("cos", "sin"))
        wh, wl = (k.sb(n, [P, 2, 768], FR) for n in ("l1_wh", "l1_wl"))
        woh, wol = (k.sb(n, [P, 2, 256], FR) for n in ("l1_woh", "l1_wol"))
        rh, rl = (k.sb(n, [P, 2, EXPERTS + 2], FR) for n in ("router_h", "router_l"))
        wg, wu = (k.sb(n, [P, 2, 1024], FR) for n in ("wg", "wu"))
        wd = k.sb("wd", [P, 8, H], FR)
        s_gu = k.sb("s_gu", [P, 2, 8], F32)
        s_down = k.sb("s_down", [P, 2], F32)
        half_set = k.sem("half_set")
        with ExitStack() as c:
            qh, ql, kh, kl = (k.sb(n, [P, 2, T * P], FR, c) for n in ("qh", "ql", "kh", "kl"))
            V = k.sb("V", [P, T, H], F32, c)
            prepare = Prepare(k, c, d, (cos, sin, wh, wl, woh, wol, rh, rl, wg, wu, wd, s_gu, s_down))
            stage_project(k, d, prepare, XH, XL, X, ident, half, half_set, qh, ql, kh, kl, V)
            attention = Attention(k, c, prepare, XH, XL, X, ident, half, qh, ql, kh, kl, V)
        stage_attention_to_experts(k, d, attention, XH, XL, X, ident, half, cos, sin, wh, wl, woh, wol, rh, rl, wg, wu, wd, s_gu, s_down, out)


def layouts(i):
    import numpy as np
    a = np.asarray
    x = a(i["L0_attn_input"]).reshape(-1, 256)
    gu = a(i["L1_ffn_gu_w"]).reshape(32, 2, 2, 64, 2, 128)
    gate_up = np.zeros((2, 33, 128, 2, 2, 64), np.float32)
    gate_up[:, :32] = gu.transpose(4, 0, 5, 2, 1, 3)
    for j, name in enumerate(("gate", "up")):
        gate_up[:, 32, :, j, 0, :] = a(i[f"L1_ffn_sh_{name}_w"]).T.reshape(2, 128, 64)
    gate_up = gate_up.reshape(2, 33, 128, 256)
    down = np.zeros((33, 128, 256), np.float32)
    down[:32] = a(i["L1_ffn_dp_w"]).transpose(0, 2, 1).reshape(32, 128, 256)
    down[32, :64] = a(i["L1_ffn_sh_down_w"]).T
    select = np.zeros((33, 128, 2, 64), np.float32)
    for e in range(64):
        select[e // 2, e, e % 2] = select[e // 2, 64 + e, e % 2] = 1
    select = select.reshape(33, 128, 128)
    out = {
        "x": x,
        "xT": x.T,
        "wqkv": np.concatenate([a(i[f"L0_attn_W{n}"]).T for n in "qkv"], axis=1),
        "bqk": np.stack([a(i["L0_attn_bq"])[:128], a(i["L0_attn_bq"])[128:],
                         a(i["L0_attn_bk"])[:128], a(i["L0_attn_bk"])[128:]], axis=1),
        "bv": a(i["L0_attn_bv"]),
        "w_gate": a(i["L0_ffn_w_gate"]).view(np.int32),
        "w_up": a(i["L0_ffn_w_up"]).view(np.int32),
        "w_down": a(i["L0_ffn_w_down"]).view(np.int32),
        "s_gu": np.stack([a(i["L0_ffn_s_gate"]).reshape(8, 128).T, a(i["L0_ffn_s_up"]).reshape(8, 128).T], axis=1),
        "s_down": a(i["L0_ffn_s_down"]).reshape(2, 128).T,
        "pos": np.arange(1024, dtype=np.float32).reshape(8, 128).T,
        "inv_freq": a(i["L1_attn_inv_freq"]),
        "l1_wqkv": np.concatenate([a(i[f"L1_attn_w{n}"]).T for n in "qkv"], axis=1),
        "l1_wo": a(i["L1_attn_wo"]).T,
        "router": np.concatenate([a(i["L1_ffn_gate_w"]).T, a(i["L1_ffn_sh_gate1_w"]).T], axis=1),
        "experts": np.concatenate([gate_up[0], gate_up[1], down, select], axis=2),
        "ident": np.eye(128, dtype=np.float32),
    }
    return {name: np.ascontiguousarray(v) for name, v in out.items()}


def kernel(**inputs):
    import numpy as np
    import concourse.bacc as bacc
    from concourse.bass_utils import run_bass_kernel_spmd

    nc = bacc.Bacc("TRN2", target_bir_lowering=False, num_devices=1)
    arrays, d = {}, {}
    for name, v in layouts(inputs).items():
        arrays[f"in_{name}"] = v
        d[name] = nc.dram_tensor(f"in_{name}", v.shape, mybir.dt.from_np(v.dtype), kind="ExternalInput").ap()
    out = nc.dram_tensor("out", (2048, 256), F32, kind="ExternalOutput").ap()
    build(nc, d, out)
    r = run_bass_kernel_spmd(nc, [arrays], core_ids=[0])
    return np.asarray(r.results[0]["out"]).reshape(2, 1024, 256)
```
